# Optimizing a Trainium2 kernel written in Bass

```python
import numpy as np
import jax
import jax.numpy as jnp

def _softmax(x, axis=-1):
    return jax.nn.softmax(x, axis=axis)

def _gelu(x):
    return jax.nn.gelu(x, approximate=True)

def _silu(x):
    return jax.nn.silu(x)

def _sigmoid(x):
    return jax.nn.sigmoid(x)

def _layernorm(x, axis=-1, eps=1e-05):
    m = jnp.mean(x, axis=axis, keepdims=True)
    v = jnp.var(x, axis=axis, keepdims=True)
    return (x - m) / jnp.sqrt(v + eps)

def _scatter_add(tgt, idx, src, axis=0):
    return tgt.at[idx].add(src)

def _segment_sum(src, seg, n):
    return jax.ops.segment_sum(src, seg, n)
kernel_name = 'mk_gnn_preln_d2_gnn_r64_608392'

def setup_inputs(seed: int=0):
    np.random.seed(seed)
    _w = jnp.asarray

    def _rec_inputs():
        import jax
        import jax.numpy as jnp
        _gk = jax.random.key(seed)
        x = -0.0005121 + 1.001 * jax.random.normal(jax.random.fold_in(_gk, 1), (100000, 64), jnp.float32)
        src = jax.random.randint(jax.random.fold_in(_gk, 2), (25000,), 0, 100000, jnp.int32)
        dst = jnp.minimum((100000 * jax.random.uniform(jax.random.fold_in(_gk, 3), (25000,)) ** 2.0).astype(jnp.int32), 99999)
        _o = jnp.argsort(dst, stable=True)
        src = src[_o]
        dst = dst[_o]
        edge_attr_3 = 0.000438201 + 0.99985 * jax.random.normal(jax.random.fold_in(_gk, 12), (25000, 3), jnp.float32)
        edge_weight = jax.random.uniform(jax.random.fold_in(_gk, 14), (25000,), jnp.float32, 0.0, 0.999999)
        return (x, src, dst, edge_attr_3, edge_weight)
    x, src, dst, edge_attr_3, edge_weight = _rec_inputs()

    def _L0_gnn_setup():
        import jax, jax.numpy as jnp
        import numpy as np
        N_NODES = 50000
        N_EDGES = 500000
        FEAT = 64
        HEADS = 4
        key = jax.random.key(seed)
        ks = jax.random.split(key, 8)
        x = jax.random.normal(ks[0], (N_NODES, FEAT), jnp.float32)
        edge_index = jax.random.randint(ks[1], (2, N_EDGES), 0, N_NODES)
        edge_vec = jax.random.normal(ks[2], (N_EDGES, 3), jnp.float32)
        edge_len = jax.random.uniform(ks[3], (N_EDGES,), jnp.float32)
        w_proj = jax.random.normal(ks[4], (HEADS, FEAT, FEAT), jnp.float32) / np.float32(np.sqrt(FEAT))
        xav = np.float32(np.sqrt(6.0 / (HEADS + FEAT)))
        radial_score = jax.random.uniform(ks[5], (HEADS, FEAT), jnp.float32, -xav, xav)
        tangential_score = jax.random.uniform(ks[6], (HEADS, FEAT), jnp.float32, -xav, xav)
        radial_distance_scale = jnp.array(1.0, jnp.float32)
        w_out = jax.random.normal(ks[7], (FEAT, FEAT), jnp.float32) / np.float32(np.sqrt(FEAT))
        return {'x': x, 'edge_index': edge_index, 'edge_vec': edge_vec, 'edge_len': edge_len, 'w_proj': w_proj, 'radial_score': radial_score, 'tangential_score': tangential_score, 'radial_distance_scale': radial_distance_scale, 'w_out': w_out}
    _L0_gnn_all = _L0_gnn_setup()
    _L0_gnn_in = {k: v for k, v in _L0_gnn_all.items() if k in ('w_proj', 'radial_score', 'tangential_score', 'radial_distance_scale', 'w_out')}
    del _L0_gnn_all

    def _L1_gnn_setup():
        import jax, jax.numpy as jnp
        import numpy as np
        N_NODES = 100000
        N_EDGES = 18750
        HID = 64
        N_LAYERS = 3
        GAMMA = -0.45
        ZETA = 1.05
        key = jax.random.key(seed)
        ks = jax.random.split(key, 8)
        s = 0.05
        return {'features': jax.random.normal(ks[0], (N_NODES, HID), jnp.float32), 'nb_W': jax.random.normal(ks[1], (N_LAYERS, HID, HID), jnp.float32) * s, 'nb_b': jnp.zeros((N_LAYERS, HID), jnp.float32), 'self_W': jax.random.normal(ks[2], (N_LAYERS, HID, HID), jnp.float32) * s, 'self_b': jnp.zeros((N_LAYERS, HID), jnp.float32), 'att1_W': jax.random.normal(ks[3], (N_LAYERS, 2 * HID, HID), jnp.float32) * s, 'att1_b': jnp.zeros((N_LAYERS, HID), jnp.float32), 'att2_W': jax.random.normal(ks[4], (N_LAYERS, HID, 1), jnp.float32) * s, 'att2_b': jnp.zeros((N_LAYERS, 1), jnp.float32), 'row': jax.random.randint(ks[5], (N_EDGES,), 0, N_NODES, jnp.int32), 'col': jax.random.randint(ks[6], (N_EDGES,), 0, N_NODES, jnp.int32)}
    _L1_gnn_all = _L1_gnn_setup()
    _L1_gnn_in = {k: v for k, v in _L1_gnn_all.items() if k in ('nb_W', 'nb_b', 'self_W', 'self_b', 'att1_W', 'att1_b', 'att2_W', 'att2_b')}
    del _L1_gnn_all
    return {'x': x, 'src': src, 'dst': dst, 'edge_attr_3': edge_attr_3, 'edge_weight': edge_weight, 'L0_gnn_w_proj': _L0_gnn_in['w_proj'], 'L0_gnn_radial_score': _L0_gnn_in['radial_score'], 'L0_gnn_tangential_score': _L0_gnn_in['tangential_score'], 'L0_gnn_radial_distance_scale': _L0_gnn_in['radial_distance_scale'], 'L0_gnn_w_out': _L0_gnn_in['w_out'], 'L1_gnn_nb_W': _L1_gnn_in['nb_W'], 'L1_gnn_nb_b': _L1_gnn_in['nb_b'], 'L1_gnn_self_W': _L1_gnn_in['self_W'], 'L1_gnn_self_b': _L1_gnn_in['self_b'], 'L1_gnn_att1_W': _L1_gnn_in['att1_W'], 'L1_gnn_att1_b': _L1_gnn_in['att1_b'], 'L1_gnn_att2_W': _L1_gnn_in['att2_W'], 'L1_gnn_att2_b': _L1_gnn_in['att2_b']}

def reference(x, src, dst, edge_attr_3, edge_weight, L0_gnn_w_proj, L0_gnn_radial_score, L0_gnn_tangential_score, L0_gnn_radial_distance_scale, L0_gnn_w_out, L1_gnn_nb_W, L1_gnn_nb_b, L1_gnn_self_W, L1_gnn_self_b, L1_gnn_att1_W, L1_gnn_att1_b, L1_gnn_att2_W, L1_gnn_att2_b):
    import jax
    import jax.numpy as jnp

    def _L0_gnn_ref(x, edge_index, edge_vec, edge_len, w_proj, radial_score, tangential_score, radial_distance_scale, w_out):
        import jax, jax.numpy as jnp
        import numpy as np
        N_NODES = 50000
        N_EDGES = 500000
        FEAT = 64
        HEADS = 4
        sender, receiver = (edge_index[0], edge_index[1])
        num_nodes = x.shape[0]
        proj = jnp.einsum('nf,hfg->nhg', x, w_proj)
        delta = proj[sender] - proj[receiver]
        radial_logits = jnp.einsum('ehf,hf->eh', delta, radial_score) - radial_distance_scale * edge_len[:, None]
        tangential_logits = jnp.einsum('ehf,hf->eh', delta, tangential_score)

        def seg_softmax_msg(logits):
            m = jax.ops.segment_max(logits, receiver, num_segments=num_nodes)
            e = jnp.exp(logits - m[receiver])
            s = jax.ops.segment_sum(e, receiver, num_segments=num_nodes)
            alpha = e / s[receiver]
            return jax.ops.segment_sum(alpha[:, :, None] * delta, receiver, num_segments=num_nodes)
        out = seg_softmax_msg(radial_logits) + seg_softmax_msg(tangential_logits)
        out = out.mean(axis=1)
        out = jnp.nan_to_num(out)
        return x + out @ w_out

    def _L1_gnn_ref(features, nb_W, nb_b, self_W, self_b, att1_W, att1_b, att2_W, att2_b, row, col):
        import jax, jax.numpy as jnp
        import numpy as np
        N_NODES = 100000
        N_EDGES = 18750
        HID = 64
        N_LAYERS = 3
        GAMMA = -0.45
        ZETA = 1.05
        n = features.shape[0]
        x = features
        out = features
        for l in range(N_LAYERS):
            f1 = jax.nn.relu(x[row] @ nb_W[l] + nb_b[l])
            f2 = jax.nn.relu(x[col] @ self_W[l] + self_b[l])
            h = jax.nn.relu(jnp.concatenate([f1, f2], axis=1) @ att1_W[l] + att1_b[l])
            log_alpha = (h @ att2_W[l] + att2_b[l])[:, 0]
            mask = jnp.clip(jax.nn.sigmoid(log_alpha) * (ZETA - GAMMA) + GAMMA, 0.0, 1.0)
            rowsum = jax.ops.segment_sum(mask, row, num_segments=n) + 1e-06
            d_inv_sqrt = jnp.clip(rowsum ** (-0.5), 0.0, 10.0)
            vals = mask * d_inv_sqrt[row] * d_inv_sqrt[col]
            x = jax.ops.segment_sum(vals[:, None] * x[col], row, num_segments=n)
            out = out + x
        return out
    edge_index = jnp.stack([src, dst])
    h = jnp.maximum(_layernorm(x, axis=-1), 0.0)
    x = x + _L0_gnn_ref(h, edge_index, edge_attr_3, edge_weight, L0_gnn_w_proj, L0_gnn_radial_score, L0_gnn_tangential_score, L0_gnn_radial_distance_scale, L0_gnn_w_out)
    h = jnp.maximum(_layernorm(x, axis=-1), 0.0)
    x = x + _L1_gnn_ref(h, L1_gnn_nb_W, L1_gnn_nb_b, L1_gnn_self_W, L1_gnn_self_b, L1_gnn_att1_W, L1_gnn_att1_b, L1_gnn_att2_W, L1_gnn_att2_b, src, dst)
    return x

_drawn_inputs = setup_inputs


def setup_inputs(seed=0):
    import zlib

    import numpy as np

    out = dict(_drawn_inputs(seed))
    spreads = {'L1_gnn_nb_b': (0.0, 0.8),
     'L1_gnn_self_b': (0.0, 0.8),
     'L1_gnn_att1_b': (0.0, 0.8),
     'L1_gnn_att2_b': (0.0, 0.311)}
    factors = {'edge_weight': 8.0,
     'L0_gnn_radial_score': 3.219,
     'L0_gnn_tangential_score': 3.19,
     'L1_gnn_self_W': 2.755}
    for name, (base, spread) in spreads.items():
        noise = np.random.default_rng([zlib.crc32(name.encode()), seed]).standard_normal(out[name].shape)
        drawn = base * np.exp(spread * noise) if base else spread * noise
        out[name] = jnp.asarray(drawn.astype(out[name].dtype))
    for name, factor in factors.items():
        out[name] = (out[name] * factor).astype(out[name].dtype)
    return out
```

```python
from contextlib import ExitStack

import numpy as np
import concourse.bass as bass
from concourse import mybir

F32 = mybir.dt.float32
BF16 = mybir.dt.bfloat16
I32 = mybir.dt.int32
ALU = mybir.AluOpType
ACT = mybir.ActivationFunctionType
AX = mybir.AxisListType
ds = bass.ds

P = 128
N, F = 100000, 64
E = 25000
HEADS, LAYERS = 4, 3
H8 = 2 * HEADS
GAMMA, ZETA = -0.45, 1.05
LN_EPS = 1e-5

TE = 126
CARRY = TE
T = 200
HT = T // 2
SLOTS = T * TE
C = 4
NCH = T // C
SMALL = 20
NSM = T // SMALL
SORT = 32768
SW = SORT // P
HALF = N // 2
OFFSET = 1 << 23
FLIP = -2147483648 + 32767
NOWHERE = 2.0e6
FAR = 1.0e6
ZERO_ROW = SLOTS
LOW = -1.0e38
HUGE = 3.4028234663852886e38
HC = 8
KC = T // HC
SCAN = KC * TE

RW = 8
DCH = 96
TAILP = (N - P * RW * DCH) // (2 * RW)
assert P * RW * DCH + 2 * RW * TAILP == N


def build(nc, a, out, STOP, scratch_kind):
    ctx = ExitStack()
    with ctx:
        def sb(name, shape, dt=F32):
            return ctx.enter_context(nc.sbuf_tensor(name, shape, dt))

        def sem(name):
            return ctx.enter_context(nc.semaphore(name))

        def dram(name, shape, dt=F32):
            return nc.dram_tensor("out_dbg_" + name if scratch_kind == "ExternalOutput" else name,
                                  shape, dt, kind=scratch_kind).ap()

        def at(ap, offset, pattern):
            return bass.AP(tensor=ap.tensor, offset=offset, ap=pattern)

        key_d = dram("keys", (2, SORT))
        pay_d = dram("payload", (E, 2))
        dstf_d = dram("dst_float", (E, 1))
        NTROW = 128 + T * 128 + 128
        node_d = dram("tile_nodes", (2, NTROW))
        flag_d = dram("tile_flags", (2, 2, T))
        pos_d = dram("position_of", (N, 1))
        x1_d = dram("x_after_layer0", (N, F))
        xt_d = [dram(f"layer_rows{l}", (SLOTS + 8, F)) for l in range(2)]
        dt_d = [dram(f"degree_rows{l}", (SLOTS + 8, 1)) for l in range(LAYERS)]
        base_d = dram("base_rows", (SLOTS, F))

        big1 = sb("big1", [P, T, F])
        big2 = sb("big2", [P, T, F])
        regs = sb("regs", [P, T * F])
        den = sb("den", [P, 9 * RW * F + 192])
        S = regs[:, :].bitcast(BF16).rearrange("p (t e) -> p t e", e=P)
        b2 = big2[:, :, :].rearrange("p t f -> p (t f)")
        b1 = big1[:, :, :].rearrange("p t f -> p (t f)")
        dX = [den[:, (3 * k) * 512:(3 * k + 1) * 512].rearrange("p (r f) -> p r f", f=F) for k in range(3)]
        dC = [den[:, (3 * k + 1) * 512:(3 * k + 2) * 512].rearrange("p (r f) -> p r f", f=F) for k in range(3)]
        dQ = [den[:, (3 * k + 2) * 512:(3 * k + 3) * 512].rearrange("p (r f) -> p r f", f=F) for k in range(3)]
        dstat = sb("dstat", [P, 3, 3, RW])

        KA, KB = b1[:, 0:512], b1[:, 512:1024]
        NI = b1[:, 1024:1536].bitcast(I32)
        NF = b1[:, 1536:2048]
        EI = b1[:, 2048:2560].bitcast(I32)
        T1t, T2t = b1[:, 2560:3072], b1[:, 3072:3584]
        EW = b1[:, 3584:3840]
        PAYT = b1[:, 3840:4352].rearrange("p (j w) -> p j w", w=2)
        SG = b1[:, 4352:4368]
        PI = b1[:, 4368:4369].bitcast(I32)
        PB = b1[:, 4369:4376].bitcast(I32)
        TR = b1[0:HT, 4400:4400 + 508].bitcast(I32)
        D1 = b1[0:HT, 4920:4920 + 508].bitcast(I32)
        D2 = b1[0:HT, 5440:5440 + 508].bitcast(I32)
        D3 = b1[0:HT, 5960:5960 + 508]
        D4 = b1[0:HT, 6480:6480 + 508]
        ND = b1[0:HT, 7000:7000 + 508].rearrange("r (q j) -> r q j", j=127)
        NTt = b1[0:HT, 7520:7520 + 512].rearrange("r (q j) -> r q j", j=128)
        SIt = b1[0:HT, 8040:8040 + 512].rearrange("r (q j) -> r q j", j=128)
        Et = b1[0:HT, 8560:8560 + 512].rearrange("r (q j) -> r q j", j=128)
        NE = b1[0:HT, 9080:9080 + 504].rearrange("r (q j) -> r q j", j=126)
        NLt = b1[0:HT, 9600:9604]
        FUt = b1[0:HT, 9604:9608]
        PADT = b1[0:2, 9700:9828]
        INIT = b1[0:100, 10000:11000]

        node = [sb(f"node{o}", [P, T]) for o in range(2)]
        scat_i = [sb(f"scat_i{o}", [P, T + 8], I32) for o in range(2)]
        own_i = [sb(f"own_i{o}", [P, T + 8], I32) for o in range(2)]
        far_i = [sb(f"far_i{o}", [P, T + 8], I32) for o in range(2)]
        pos_i = sb("pos_i", [P, T + 8], I32)
        wneg = sb("wneg", [P, T])
        perm_i = [b2[:, o * 208:o * 208 + 208].bitcast(I32) for o in range(2)]
        payg = b2[:, 416:816].rearrange("p (t w) -> p t w", w=2)
        dstg = b2[:, 816:1016].rearrange("p (t w) -> p t w", w=1)
        posv = b2[:, 1016:1216].rearrange("p (t w) -> p t w", w=1)
        posg = b2[:, 1216:1416].rearrange("p (t w) -> p t w", w=1)
        posn = b2[:, 1416:1616].bitcast(I32)
        small_v = sb("small_v", [P, 2, SMALL, 2])
        small_i = sb("small_i", [P, 2, SMALL], I32)
        small_v1 = sb("small_v1", [P, 2, SMALL, 1])

        G = sb("G", [P, 2, C, 2, F])
        XC = sb("XC", [P, 2, C, 2, F])
        SQ = sb("SQ", [P, 2, C, 2, F])
        VS = sb("VS", [P, 2, C, F])
        TS = sb("TS", [P, 2, C, F])
        stat = sb("stat", [P, 2, 3, 2 * C])
        idx_s = sb("idx_s", [P, 2, 2, C], I32)
        SE = sb("SE", [P, T, 2])
        Zs = [t_[:, :, :, :, :].rearrange("p b c d f -> p (b c d f)").rearrange("p (c h f) -> p c h f", c=C, f=F) for t_ in (G, XC)]
        ZTs = [SQ[:, :, :, :, :].rearrange("p b c d f -> p (b c d f)"), den[:, 1024:2048]]
        LG = den[:, 3200:4800].rearrange("p (t h) -> p t h", h=H8)
        LGP = regs[:, 9480:9480 + T * H8]
        BT = den[:, 3200:4000].rearrange("p (t h) -> p t h", h=HEADS)
        NB = [den[:, k * 512:(k + 1) * 512].rearrange("p (t e) -> p t e", e=P) for k in range(2)]
        STg = [den[:, 2048 + k * 512:2560 + k * 512].rearrange("p (t e) -> p t e", e=P) for k in range(2)]
        IDS = den[0:64, 0:SCAN + 2]
        SQn = den[0:64, 0:SCAN]
        SAME = regs[0:64, 0:SCAN + 1]
        NEG = regs[0:64, 3160:3160 + SCAN + 1]
        SL = regs[0:64, 6320:6320 + SCAN]
        SP_ = regs[0:64, 9480:9480 + SCAN]
        ccol = sb("ccol", [P, 8])
        crow = den[0:1, 4000:4400]
        carr = den[0:1, 4400:4800]
        FLS = den[0:F, 4000:4400].rearrange("f (t k) -> f t k", k=2)
        AF, AB, BF_, BB = [den[0:F, k * 200:(k + 1) * 200] for k in range(4)]
        CF = den[0:F, 1024:1424].rearrange("f (k t) -> f k t", k=2)
        CT = den[0:HT, 1424:1680].rearrange("r (q f) -> r q f", f=F)
        FLB = [sb(f"FLB{o}", [F, 2, T]) for o in range(1)]
        TT = [[den[:, (3 * b + k) * 512:(3 * b + k + 1) * 512] for k in range(3)] for b in range(2)]
        LR = [den[:, 3072 + b * 768:3072 + (b + 1) * 768].rearrange("p (n c f) -> p n c f", n=3, f=F) for b in range(2)]
        MT, PF, PB_ = [den[0:HT, k * 256:k * 256 + 252].rearrange("r (h e) -> r h e", h=2) for k in range(3)]
        MSK = sb("MSK", [P, T])
        VAL0 = sb("VAL0", [P, T])
        VAL1 = sb("VAL1", [P, T])
        DCc = sb("DCc", [P, T])
        smr = sb("smr", [HT, 2, TE + 1])
        em = sb("em", [P, 1])
        tiny_c = sb("tiny_c", [P, 1])

        wp = SQ[:, 0, :, 0, :]
        wp4 = sb("wp4", [P, HEADS, F])
        wm = sb("wm", [P, 2, F])
        rsT = sb("rsT", [F, H8])
        A2 = sb("A2", [P, 2 * H8])
        wo = sb("wo", [P, P])
        wb = sb("wb", [P, LAYERS, P])
        at1 = sb("at1", [P, LAYERS, F])
        at2 = sb("at2", [F, LAYERS])
        bias1 = sb("bias1", [P, LAYERS])
        bias2 = sb("bias2", [F, LAYERS])
        bias3 = sb("bias3", [P, LAYERS])
        rscale = sb("rscale", [P, 1])
        wT = b1[0:F, 11100:11100 + 512]
        zrow = b1[0:8, 11700:11764]
        zrow_ten = b1[0:8, 11764:11765]

        ident = sb("ident", [P, P])
        eps_c = sb("eps_c", [P, 1])

        bank = [ctx.enter_context(nc.psum_tensor(f"bank{i}", [P, 512], F32)) for i in range(8)]

        s = {}

        def S_(name):
            if name not in s:
                s[name] = sem(name)
            return s[name]

        def pipelined(eng, stages):
            deep = max(lag for lag, _ in stages)
            peel = (deep + 3) // 2 * 2
            for c in range(peel):
                for lag, fn in stages:
                    if c - lag >= 0:
                        fn(c - lag, (c - lag) % 2, (c - lag) // 2)
            with eng.Fori(peel // 2, NCH // 2) as j:
                for b in range(2):
                    for lag, fn in stages:
                        fn(j * 2 + (b - lag), (b - lag) % 2, j + (b - lag) // 2)
            for c in range(NCH, NCH + deep):
                for lag, fn in stages:
                    if c - lag < NCH:
                        fn(c - lag, (c - lag) % 2, (c - lag) // 2)

        def early(c):
            return isinstance(c, int) and c < 2

        def tiles(c, shift=0):
            return slice(c * C + shift, c * C + shift + C) if isinstance(c, int) else ds(c * C + shift, C)

        def one(c, k):
            return slice(c * C + k, c * C + k + 1) if isinstance(c, int) else ds(c * C + k, 1)

        def bc(ap, n):
            return ap.unsqueeze(len(ap.shape)).broadcast_to([*ap.shape, n])

        BLOCK3 = at

        ctx.enter_context(nc.allow_non_contiguous_dma(reason="columns of flags, biases and ends of tiles"))
        block = ctx.enter_context(nc.Block())

        def rest(n):
            return STOP >= n

        def dense_view(ap, c):
            if isinstance(c, int) and c >= DCH:
                u = c - DCH
                return ap[P * RW * DCH:N, :].rearrange("(p u r) f -> u p r f", u=2, r=RW)[u]
            return ap[0:P * RW * DCH, :].rearrange("(p c r) f -> c p r f", c=DCH, r=RW)

        def dense_sp(sp, tag, src, dst):
            def load(c, k, j):
                if j is not None:
                    sp.wait_ge(S_(f"d{tag}_out{k}"), 16 * j)
                if isinstance(c, int) and c >= DCH:
                    sp.dma_start(dX[k][0:TAILP], dense_view(src, c)).then_inc(S_(f"d{tag}_in{k}"), 16)
                else:
                    sp.dma_start(dX[k], dense_view(src, c)[ds(c, 1)].rearrange("o p r f -> (o p) r f") if not isinstance(c, int) else dense_view(src, c)[c]).then_inc(S_(f"d{tag}_in{k}"), 16)

            def store(c, k):
                sp.wait_ge(S_(f"d{tag}_done"), c + 1)
                if isinstance(c, int) and c >= DCH:
                    sp.dma_start(dense_view(dst, c), dX[k][0:TAILP]).then_inc(S_(f"d{tag}_out{k}"), 16)
                else:
                    sp.dma_start(dense_view(dst, c)[ds(c, 1)].rearrange("o p r f -> (o p) r f") if not isinstance(c, int) else dense_view(dst, c)[c], dX[k]).then_inc(S_(f"d{tag}_out{k}"), 16)

            for c in range(3):
                load(c, c, None)
            with sp.Fori(0, DCH // 3 - 1) as j:
                for k in range(3):
                    store(j * 3 + k, k)
                    load(j * 3 + k + 3, k, j + 1)
            n = DCH // 3
            for k in range(3):
                store(DCH - 3 + k, k)
                if k < 2:
                    load(DCH + k, k, n)
            for k in range(2):
                store(DCH + k, k)
            for k in range(3):
                sp.wait_ge(S_(f"d{tag}_out{k}"), 16 * (n + (k < 2)))

        def dense_dve(v, tag):
            def first(c, k, n, j):
                v.wait_ge(S_(f"d{tag}_in{k}"), 16 * (j + 1))
                v.tensor_reduce(dstat[0:n, k, 0], dX[k][0:n], AX.X, ALU.add)
                v.drain()
                v.scalar_tensor_tensor(dC[k][0:n], dstat[0:n, k, 0].unsqueeze(2).broadcast_to([n, RW, F]), -1.0 / F,
                                       dX[k][0:n], ALU.mult, ALU.add).then_inc(S_(f"d{tag}_cen"), 1)

            def second(c, k, n):
                v.wait_ge(S_(f"d{tag}_sq"), c + 1)
                v.tensor_reduce(dstat[0:n, k, 1], dQ[k][0:n], AX.X, ALU.add).then_inc(S_(f"d{tag}_var"), 1)

            def third(c, k, n):
                v.wait_ge(S_(f"d{tag}_std"), c + 1)
                v.reciprocal(dstat[0:n, k, 2], dstat[0:n, k, 2])
                v.drain()
                v.scalar_tensor_tensor(dC[k][0:n], dC[k][0:n], 0.0,
                                       dstat[0:n, k, 2].unsqueeze(2).broadcast_to([n, RW, F]), ALU.max, ALU.mult)
                v.drain()
                v.tensor_tensor(dX[k][0:n], dX[k][0:n], dC[k][0:n], ALU.add).then_inc(S_(f"d{tag}_done"), 1)

            first(0, 0, P, 0)
            first(1, 1, P, 0)
            second(0, 0, P)
            with v.Fori(0, (DCH - 3) // 3) as j:
                for k in range(3):
                    c, slot = j * 3 + k + 2, (k + 2) % 3
                    third(c - 2, (slot + 1) % 3, P)
                    first(c, slot, P, j + (k + 2) // 3)
                    second(c - 1, (slot + 2) % 3, P)
            for c in range(DCH - 1, DCH + 4):
                if c - 2 < DCH + 2:
                    third(c - 2, (c - 2) % 3, P if c - 2 < DCH else TAILP)
                if c < DCH + 2:
                    first(c, c % 3, P if c < DCH else TAILP, c // 3)
                if c - 1 < DCH + 2:
                    second(c - 1, (c - 1) % 3, P if c - 1 < DCH else TAILP)

        def dense_act(s_, tag):
            def square(c, k, n):
                s_.wait_ge(S_(f"d{tag}_cen"), c + 1)
                s_.activation(dQ[k][0:n], dC[k][0:n], ACT.Square).then_inc(S_(f"d{tag}_sq"), 1)

            def root(c, k, n):
                s_.wait_ge(S_(f"d{tag}_var"), c + 1)
                s_.activation(dstat[0:n, k, 2], dstat[0:n, k, 1], ACT.Sqrt, bias=eps_c[0:n, :], scale=1.0 / F).then_inc(S_(f"d{tag}_std"), 1)

            square(0, 0, P)
            with s_.Fori(0, (DCH - 3) // 3 + 0) as j:
                for k in range(3):
                    square(j * 3 + k + 1, (k + 1) % 3, P)
                    root(j * 3 + k, k, P)
            for c in range(DCH - 3, DCH + 2):
                if c + 1 < DCH + 2:
                    square(c + 1, (c + 1) % 3, P if c + 1 < DCH else TAILP)
                root(c, c % 3, P if c < DCH else TAILP)

        def gather_pair(g, top, tag, table, free):
            def step(c, b, j):
                g.wait_ge(S_(f"{tag}_free{b}"), j + 1)
                g.sem_inc(S_("pool_turn"), 1)
                for k in range(C):
                    for d in range(2):
                        g.indirect_dma_start(G[:, b, k, d, :], None, table,
                                             bass.IndirectOffsetOnAxis(ap=idx_s[:, b, d, k:k + 1], axis=0),
                                             bounds_check=top, oob_is_err=False).then_inc(S_(f"{tag}_in{b}"), 16)
            pipelined(g, [(0, step)])

        def stage_indices(v, tag, idx, c, b):
            for d, ix in enumerate(idx[:-1]):
                v.tensor_copy(idx_s[:, b, d, :], ix[:, tiles(c)])
            v.tensor_copy(idx_s[:, b, len(idx) - 1, :], idx[-1][:, tiles(c)]).then_inc(S_(f"{tag}_free{b}"), 1)

        def norm_dve(v, tag, c, b, j):
            flat = lambda t_: t_[:, b].rearrange("p c d f -> p (c d) f")
            v.wait_ge(S_(f"{tag}_in{b}"), (j + 1) * (32 * C))
            v.tensor_reduce(stat[:, b, 0], flat(G), AX.X, ALU.add)
            v.drain()
            v.scalar_tensor_tensor(flat(XC), bc(stat[:, b, 0], F), -1.0 / F, flat(G), ALU.mult, ALU.add).then_inc(S_(f"{tag}_cen"), 1)
            v.wait_ge(S_(f"{tag}_sq"), c + 1)
            v.tensor_reduce(stat[:, b, 1], flat(SQ), AX.X, ALU.add).then_inc(S_(f"{tag}_var"), 1)
            v.wait_ge(S_(f"{tag}_std"), c + 1)
            v.reciprocal(stat[:, b, 2], stat[:, b, 2])
            v.drain()
            v.scalar_tensor_tensor(flat(XC), flat(XC), 0.0, bc(stat[:, b, 2], F), ALU.max, ALU.mult)
            v.drain()

        def norm_act(s_, tag, c, b, j):
            s_.wait_ge(S_(f"{tag}_cen"), c + 1)
            s_.activation(SQ[:, b], XC[:, b], ACT.Square).then_inc(S_(f"{tag}_sq"), 1)
            s_.wait_ge(S_(f"{tag}_var"), c + 1)
            s_.activation(stat[:, b, 2], stat[:, b, 1], ACT.Sqrt, bias=eps_c[:, :], scale=1.0 / F).then_inc(S_(f"{tag}_std"), 1)

        def pairs(ap):
            return ap.rearrange("p c f -> p (c f)")

        def build_S_sp(sp, tag, o):
            def step(c, b, j):
                if not early(c):
                    sp.wait_ge(S_(f"{tag}_made{b}"), j)
                off = 128 + c * 512
                src = node_d[o:o + 1, off:off + 512] if isinstance(c, int) else node_d[o:o + 1, ds(off, 512)]
                sp.dma_start(NB[b].rearrange("p t e -> p (t e)"), src.broadcast_to([P, 512])).then_inc(S_(f"{tag}_ids{b}"), 16)
            pipelined(sp, [(0, step)])

        def build_S_dve(v, tag, o):
            def step(c, b, j):
                v.wait_ge(S_(f"{tag}_ids{b}"), (j + 1) * 16)
                v.tensor_tensor(S[:, tiles(c), :], NB[b], bc(node[o][:, tiles(c)], P), ALU.is_equal).then_inc(S_(f"{tag}_made{b}"), 1)
            pipelined(v, [(0, step)])
            v.drain()
            v.tensor_copy(SE[:, :, :], S[:, :, TE:])
            v.drain().then_inc(S_(f"{tag}_S"), 1)

        def carry_dve(v, tag, i=0):
            nl, fu = FLB[0][:, 0, :], FLB[0][:, 1, :]
            m = T - 1
            v.wait_ge(S_(f"{tag}_fl_c"), NCH * (i + 1))
            v.tensor_tensor(AF, nl, fu, ALU.mult)
            v.tensor_tensor(AB[:, 0:m], nl[:, 0:m], fu[:, 1:T], ALU.mult)
            v.tensor_tensor(BF_[:, 0:m], nl[:, 0:m], FLS[:, 0:m, 1], ALU.mult)
            v.tensor_tensor(BB[:, 0:m], nl[:, 0:m], FLS[:, 1:T, 0], ALU.mult)
            v.memset(CF[:, :, :], 0.0)
            v.drain()
            v.tensor_tensor_scan(CF[:, 0, 1:T], AF[:, 0:m], BF_[:, 0:m], 0.0, ALU.mult, ALU.add)
            v.tensor_tensor_scan(CF[:, 1, 0:m][:, ::-1], AB[:, 0:m][:, ::-1], BB[:, 0:m][:, ::-1], 0.0, ALU.mult, ALU.add)
            v.drain().then_inc(S_(f"{tag}_carry"), 1)
            v.wait_ge(S_(f"{tag}_carry_t"), i + 1)
            v.tensor_copy(CT.rearrange("r q f -> r (q f)"), bank[0][0:HT, 0:256]).then_inc(S_(f"{tag}_carry"), 1)

        def carry_pe(pe, tag, i=0):
            pe.wait_ge(S_(f"{tag}_carry"), 2 * i + 1)
            for q in range(4):
                ins = pe.transpose(bank[0][0:HT, q * F:(q + 1) * F], CF[:, q // 2, (q % 2) * HT:(q % 2 + 1) * HT], ident[0:F, 0:F])
            ins.then_inc(S_(f"{tag}_carry_t"), 1)

        def carry_sp(sp, tag, big, i=0):
            sp.wait_ge(S_(f"{tag}_carry"), 2 * i + 2)
            for q in range(4):
                sp.dma_start(big[CARRY + q // 2:CARRY + q // 2 + 1, (q % 2) * HT:(q % 2 + 1) * HT, :].rearrange("o t f -> o (t f)"),
                             CT[:, q, :]).then_inc(S_(f"{tag}_carried"), 16)

        def L0_sp(sp):
            sp.wait_ge(S_("sm_lg"), 1)
            for h in range(H8):
                rows = slice(h * HC, (h + 1) * HC)
                sp.dma_start(IDS[rows, 1:SCAN + 1].rearrange("c (k e) -> c k e", k=KC),
                             at(node_d, 128, [[KC * 128, HC], [128, KC], [1, TE]])).then_inc(S_("scan_ids"), 16)
                sp.dma_start(IDS[rows, 0:1], at(node_d, TE - 1, [[KC * 128, HC], [1, 1]])).then_inc(S_("scan_ids"), 16)
                sp.dma_start(IDS[rows, SCAN + 1:SCAN + 2], at(node_d, 128 + KC * 128, [[KC * 128, HC], [1, 1]])).then_inc(S_("scan_ids"), 16)
            for n_ in range(2):
                sp.wait_ge(S_("ends_up"), n_ + 1)
                sp.dma_start(crow[0:1, 0:320], ccol[0:64, 0:5]).then_inc(S_("ends_row"), 16)
                sp.wait_ge(S_("carry_row"), n_ + 1)
                sp.dma_start(ccol[0:64, 5:7], carr[0:1, 0:128]).then_inc(S_("carry_col"), 16)
            sp.dma_start(FLB[0][:, :, :], at(flag_d, 0, [[0, F], [1, 2 * T]])).then_inc(S_("flags0"), 16)
            sp.wait_ge(S_("alpha_out"), 4)
            build_S_sp(sp, "s0", 0)
            carry_sp(sp, "m", big1)

        def L0_pool(g, top):
            gather_pair(g, top, "g", a["x"], None)

            def step(c, b, j):
                g.wait_ge(S_("n_rows"), c + 1)
                g.sem_inc(S_("pool_turn"), 1)
                for k in range(C):
                    g.indirect_dma_start(x1_d, bass.IndirectOffsetOnAxis(ap=idx_s[:, b, 0, k:k + 1], axis=0), G[:, b, k, 0, :], None,
                                         bounds_check=top, oob_is_err=False).then_inc(S_(f"n_out{b}"), 16)
            pipelined(g, [(0, step)])
            for b in range(2):
                g.wait_ge(S_(f"n_out{b}"), 16 * C * (NCH // 2))
            g.sem_inc(S_("x1_fixed"), 1)

        def segment_ends(v, data, op0, op1, first, mask):
            v.tensor_tensor_scan(SP_, mask[:, 0:SCAN], data, first, op0, op1)
            v.tensor_tensor_scan(SQn[:, ::-1], mask[:, 1:SCAN + 1][:, ::-1], data[:, ::-1], first, op0, op1)
            v.drain()
            v.tensor_copy(ccol[0:64, 0:1], SP_[:, SCAN - 1:SCAN])
            v.tensor_copy(ccol[0:64, 1:2], SQn[:, 0:1]).then_inc(S_("ends_up"), 1)

        def row_carry(v, n_, is_max):
            R = crow[0:1, 0:320].rearrange("o (q k) -> o q k", k=5)
            last, frst, lp, ln_, full = [R[:, :, k] for k in range(5)]
            m = 63
            A_, B_ = carr[0:1, 128:192], carr[0:1, 192:256]
            A2_, B2_ = carr[0:1, 256:320], carr[0:1, 320:384]
            O = carr[0:1, 0:128].rearrange("o (q k) -> o q k", k=2)
            first = LOW if is_max else 0.0
            v.wait_ge(S_("ends_row"), 16 * (n_ + 1))
            v.memset(O, first)
            v.tensor_tensor(A_[:, 0:m], lp[:, 1:64], full[:, 0:m], ALU.mult)
            v.tensor_tensor(A2_[:, 0:m], ln_[:, 0:m], full[:, 1:64], ALU.mult)
            if is_max:
                v.tensor_scalar(B_[:, 0:m], lp[:, 1:64], -1.0, -LOW, ALU.add, ALU.mult)
                v.tensor_scalar(B2_[:, 0:m], ln_[:, 0:m], -1.0, -LOW, ALU.add, ALU.mult)
                v.drain()
                v.tensor_scalar(A_[:, 0:m], A_[:, 0:m], -1.0, -LOW, ALU.add, ALU.mult)
                v.tensor_scalar(A2_[:, 0:m], A2_[:, 0:m], -1.0, -LOW, ALU.add, ALU.mult)
                v.tensor_tensor(B_[:, 0:m], B_[:, 0:m], last[:, 0:m], ALU.add)
                v.tensor_tensor(B2_[:, 0:m], B2_[:, 0:m], frst[:, 1:64], ALU.add)
                op0, op1 = ALU.add, ALU.max
            else:
                v.tensor_tensor(B_[:, 0:m], lp[:, 1:64], last[:, 0:m], ALU.mult)
                v.tensor_tensor(B2_[:, 0:m], ln_[:, 0:m], frst[:, 1:64], ALU.mult)
                op0, op1 = ALU.mult, ALU.add
            v.drain()
            v.tensor_tensor_scan(O[:, 1:64, 0], A_[:, 0:m], B_[:, 0:m], first, op0, op1)
            v.tensor_tensor_scan(O[:, 0:m, 1][:, ::-1], A2_[:, 0:m][:, ::-1], B2_[:, 0:m][:, ::-1], first, op0, op1)
            v.drain().then_inc(S_("carry_row"), 1)
            v.wait_ge(S_("carry_col"), 16 * (n_ + 1))

        def L0_dve(v):
            v.wait_ge(S_("small_done"), 1)
            v.wait_ge(S_("nodes_out"), 16 * 8)
            v.wait_ge(S_("weights_in"), 16 * 17)
            for k in range(3):
                v.wait_ge(S_(f"da_out{k}"), 16 * (DCH // 3 + (k < 2)))
            v.tensor_scalar(wneg[:, :], payg[:, :, 1], rscale[:, 0:1], -1.0, ALU.mult, ALU.mult)
            for o in range(2):
                v.memset(far_i[o][:, T:], 0)
            v.memset(pos_i[:, T:], 0)
            v.drain()
            idx = (own_i[0], far_i[0])
            for b in range(2):
                stage_indices(v, "g", idx, b, b)

            def step(c, b, j):
                norm_dve(v, "g", c, b, j)
                if not early(c):
                    v.wait_ge(S_("g_raw"), c - 1)
                v.tensor_tensor(VS[:, b], XC[:, b, :, 1, :], XC[:, b, :, 0, :], ALU.subtract).then_inc(S_("g_dl"), 1)
                v.tensor_tensor(big2[:, tiles(c), :], G[:, b, :, 0, :], XC[:, b, :, 0, :], ALU.add)
                v.drain()
                stage_indices(v, "g", idx, c + 2, b)
            pipelined(v, [(0, step)])

            v.wait_ge(S_("g_raw"), NCH)
            LGc, LPv = LG.rearrange("p (c k) h -> p h k c", c=HC), LGP.rearrange("p (k h c) -> p h k c", k=KC, h=H8)
            wv = wneg[:, :].rearrange("p (c k) -> p k c", c=HC)
            for h in range(H8):
                if h < HEADS:
                    v.tensor_tensor(LPv[:, h], LGc[:, h], wv, ALU.add)
                else:
                    v.tensor_copy(LPv[:, h], LGc[:, h])
            v.drain().then_inc(S_("sm_lg"), 1)
            v.wait_ge(S_("scan_ids"), 16 * 24)
            v.tensor_tensor(SAME, IDS[:, 1:SCAN + 2], IDS[:, 0:SCAN + 1], ALU.is_equal)
            v.tensor_tensor(ccol[0:64, 4:5], IDS[:, 1:2], IDS[:, SCAN:SCAN + 1], ALU.is_equal)
            v.drain()
            v.tensor_scalar(NEG, SAME, -1.0, -LOW, ALU.add, ALU.mult)
            v.tensor_copy(ccol[0:64, 2:3], SAME[:, 0:1])
            v.tensor_copy(ccol[0:64, 3:4], SAME[:, SCAN:SCAN + 1])
            v.drain()
            v.wait_ge(S_("sm_in"), 7)
            segment_ends(v, SL, ALU.add, ALU.max, LOW, NEG)
            row_carry(v, 0, True)
            v.tensor_tensor_scan(SP_, NEG[:, 0:SCAN], SL, ccol[0:64, 5:6], ALU.add, ALU.max)
            v.drain()
            v.tensor_tensor_scan(SQn[:, ::-1], NEG[:, 1:SCAN + 1][:, ::-1], SP_[:, ::-1], ccol[0:64, 6:7], ALU.add, ALU.max)
            v.drain()
            v.tensor_tensor(SL, SL, SQn, ALU.subtract).then_inc(S_("sm_sub"), 1)
            v.memset(BT, 0.0)
            v.wait_ge(S_("sm_exp"), 1)
            segment_ends(v, SL, ALU.mult, ALU.add, 0.0, SAME)
            row_carry(v, 1, False)
            v.tensor_tensor_scan(SP_, SAME[:, 0:SCAN], SL, ccol[0:64, 5:6], ALU.mult, ALU.add)
            v.tensor_tensor_scan(SQn[:, ::-1], SAME[:, 1:SCAN + 1][:, ::-1], SL[:, ::-1], ccol[0:64, 6:7], ALU.mult, ALU.add)
            v.drain()
            v.tensor_tensor(SP_, SP_, SQn, ALU.add)
            v.drain()
            v.tensor_tensor(SP_, SP_, SL, ALU.subtract)
            v.drain()
            v.reciprocal(SP_, SP_)
            v.drain()
            v.tensor_tensor(SL, SL, SP_, ALU.mult).then_inc(S_("sm_alpha"), 1)
            BTv = BT.rearrange("p (c k) h -> p k h c", c=HC)
            for q in range(4):
                n_ = min(8, KC - 8 * q)
                v.wait_ge(S_("sm_back"), q + 1)
                B = bank[4 + q % 2][0:TE, 0:n_ * 64].rearrange("p (k r h c) -> p k r h c", r=2, h=HEADS, c=HC)
                for k in range(n_):
                    v.tensor_copy(BTv[0:TE, 8 * q + k], B[:, k, 0])
                v.drain()
                for k in range(n_):
                    ins = v.tensor_tensor(BTv[0:TE, 8 * q + k], BTv[0:TE, 8 * q + k], B[:, k, 1], ALU.add)
                ins.then_inc(S_("alpha_out"), 1)
            v.drain()
            build_S_dve(v, "s0", 0)

            def weigh(c, b, j):
                if not early(c):
                    v.wait_ge(S_("m_tp"), c - 1)
                v.tensor_tensor(Zs[b], big1[:, tiles(c), :].unsqueeze(2).broadcast_to([P, C, HEADS, F]),
                                bc(BT[:, tiles(c), :], F), ALU.mult).then_inc(S_("m_z"), 1)
            pipelined(v, [(0, weigh)])
            v.wait_ge(S_("flags0"), 16)
            carry_dve(v, "m")

            def guard(c, b, j):
                v.wait_ge(S_("n_sum"), c + 1)
                x_ = bank[b][:, 0:C * F]
                hi, lo = pairs(VS[:, b]), pairs(XC[:, b, :, 0, :].rearrange("p c f -> p c f")) if False else SQ[:, b].rearrange("p c d f -> p (c d f)")[:, 0:C * F]
                v.tensor_scalar(hi, x_, 0.0, HUGE, ALU.max, ALU.min)
                v.tensor_scalar(lo, x_, 0.0, -HUGE, ALU.min, ALU.max)
                v.drain()
                v.tensor_tensor(hi, hi, lo, ALU.add).then_inc(S_("n_safe"), 1)

            def renew(c, b, j):
                v.wait_ge(S_("n_proj"), c + 1)
                if not early(c):
                    v.wait_ge(S_(f"n_out{b}"), j * (16 * C))
                v.tensor_tensor(G[:, b, :, 0, :], bank[4 + b][:, 0:C * F].rearrange("p (c f) -> p c f", f=F), big2[:, tiles(c), :], ALU.add)
                v.tensor_copy(idx_s[:, b, 0, :], scat_i[0][:, tiles(c)])
                v.drain().then_inc(S_("n_rows"), 1)
            pipelined(v, [(0, guard), (2, renew)])

        def L0_act(s_):
            def step(c, b, j):
                norm_act(s_, "g", c, b, j)
                s_.wait_ge(S_("g_tp"), c + 1)
                s_.activation(pairs(TS[:, b]), bank[b][:, 0:C * F], ACT.Copy).then_inc(S_("g_dt"), 1)
                s_.activation(big1[:, tiles(c), :], VS[:, b], ACT.Copy)
                s_.wait_ge(S_("g_lg"), c + 1)
                s_.sem_inc(S_("act_turn"), 1)
                s_.activation(LG[:, tiles(c), :], bank[2 + b][:, 0:C * H8].rearrange("p (c h) -> p c h", h=H8), ACT.Copy).then_inc(S_("g_raw"), 1)
            s_.wait_ge(S_("scores_c"), 2)
            pipelined(s_, [(0, step)])
            SLk = SL.rearrange("q (k e) -> q k e", e=TE)
            for q in range(7):
                n_ = min(4, KC - 4 * q)
                s_.wait_ge(S_("sm_t"), q + 1)
                s_.activation(SLk[:, 4 * q:4 * q + n_, :], bank[q % 2][0:64, 0:n_ * P].rearrange("q (k e) -> q k e", e=P)[:, :, 0:TE], ACT.Copy).then_inc(S_("sm_in"), 1)
            s_.wait_ge(S_("sm_sub"), 1)
            s_.activation(SL, SL, ACT.Exp).then_inc(S_("sm_exp"), 1)

            def out_t(c, b, j):
                s_.wait_ge(S_("m_tp"), c + 1)
                s_.activation(ZTs[b][:, 0:512], bank[2 * b][:, :], ACT.Copy)
                s_.activation(ZTs[b][:, 512:1024], bank[2 * b + 1][:, :], ACT.Copy).then_inc(S_("m_ev"), 1)

            def out_v(c, b, j):
                s_.wait_ge(S_("m_mm"), c + 1)
                s_.activation(pairs(VS[:, b]), bank[4 + b][:, 0:C * F], ACT.Copy, scale=1.0 / HEADS).then_inc(S_("m_v"), 1)
                s_.activation(big1[:, tiles(c), :], bank[4 + b][:, 0:C * F].rearrange("p (c f) -> p c f", f=F), ACT.Copy, scale=1.0 / HEADS).then_inc(S_("m_b1"), 1)

            pipelined(s_, [(0, out_t), (1, out_v), (2, lambda c, b, j: ends_act(s_, "m", c, b, j))])

            def widen(c, b, j):
                if not early(c):
                    s_.wait_ge(S_("n_sum"), c - 1)
                    s_.sem_inc(S_("act_turn"), 1)
                s_.activation(STg[b], S[:, tiles(c), :], ACT.Copy).then_inc(S_("n_st"), 1)

            def out_g(c, b, j):
                s_.wait_ge(S_("n_tp"), c + 1)
                s_.activation(pairs(TS[:, b]), bank[2 + b][:, 0:C * F], ACT.Copy).then_inc(S_("n_gt"), 1)
            s_.wait_ge(S_("m_carry_t"), 1)
            pipelined(s_, [(0, widen), (1, out_g)])

        def ends_act(s_, tag, c, b, j, base=0):
            s_.wait_ge(S_(f"{tag}_fl"), c + (base + 1))
            s_.sem_inc(S_("act_turn"), 1)
            s_.activation(FLS[:, tiles(c), :], bank[6 + b][0:F, 0:2 * C].rearrange("f (c k) -> f c k", k=2), ACT.Copy).then_inc(S_(f"{tag}_fl_c"), 1)

        def ends_pe(pe, tag, ready, c, b, j, base=0):
            pe.wait_ge(S_(ready), c + (base + 1))
            if not early(c):
                pe.wait_ge(S_(f"{tag}_fl_c"), c + (base - 1))
            pe.sem_inc(S_("pe_turn"), 1)
            for k in range(C):
                ins = pe.matmul(bank[6 + b][0:F, 2 * k:2 * k + 2], VS[:, b, k, :], SE[:, one(c, k), :].rearrange("p o k -> p (o k)"), start=True, stop=True)
            ins.then_inc(S_(f"{tag}_fl"), 1)

        def L0_pe(pe):
            def turn(c, b, j):
                pe.wait_ge(S_("g_dl"), c + 1)
                for q in range(C // 2):
                    ins = pe.transpose(bank[b][:, q * P:(q + 1) * P], pairs(VS[:, b, 2 * q:2 * q + 2, :]), ident[:, :])
                ins.then_inc(S_("g_tp"), 1)
                pe.wait_ge(S_("g_dt"), c + 1)
                for q in range(C // 2):
                    ins = pe.matmul(bank[2 + b][:, q * 2 * H8:(q + 1) * 2 * H8], pairs(TS[:, b, 2 * q:2 * q + 2, :]), A2[:, :], start=True, stop=True)
                ins.then_inc(S_("g_lg"), 1)
            pe.wait_ge(S_("scores_c"), 2)
            pipelined(pe, [(0, turn)])
            pe.wait_ge(S_("sm_lg"), 1)
            for k in range(KC):
                q = k // 4
                if q >= 2 and k % 4 == 0:
                    pe.wait_ge(S_("sm_in"), q - 1)
                ins = pe.transpose(bank[q % 2][0:64, (k % 4) * P:(k % 4 + 1) * P], LGP[:, k * 64:(k + 1) * 64], ident[:, :])
                if k % 4 == 3 or k == KC - 1:
                    ins.then_inc(S_("sm_t"), 1)
            pe.wait_ge(S_("sm_alpha"), 1)
            SLk = SL.rearrange("q (k e) -> q k e", e=TE)
            for k in range(KC):
                q = k // 8
                if q >= 2 and k % 8 == 0:
                    pe.wait_ge(S_("alpha_out"), q - 1)
                ins = pe.transpose(bank[4 + q % 2][0:TE, (k % 8) * 64:(k % 8 + 1) * 64], SLk[:, k, :], ident[0:64, 0:64])
                if k % 8 == 7 or k == KC - 1:
                    ins.then_inc(S_("sm_back"), 1)

            def turn_z(c, b, j):
                pe.wait_ge(S_("m_z"), c + 1)
                for q in range(2):
                    for k in range(C):
                        ins = pe.transpose(bank[2 * b + q][:, k * P:(k + 1) * P], Zs[b][:, k, 2 * q:2 * q + 2, :].rearrange("p h f -> p (h f)"), ident[:, :])
                ins.then_inc(S_("m_tp"), 1)

            def project(c, b, j):
                pe.wait_ge(S_("m_ev"), c + 1)
                for k in range(C):
                    for q in range(2):
                        ins = pe.matmul(bank[4 + b][:, k * F:(k + 1) * F], ZTs[b][:, q * 512 + k * P:q * 512 + (k + 1) * P], wm[:, q, :],
                                        start=(q == 0), stop=(q == 1))
                ins.then_inc(S_("m_mm"), 1)
            pe.wait_ge(S_("s0_S"), 1)
            pipelined(pe, [(0, turn_z), (1, project), (2, lambda c, b, j: ends_pe(pe, "m", "m_v", c, b, j))])
            carry_pe(pe, "m")

            def total(c, b, j):
                pe.wait_ge(S_("n_st"), c + 1)
                for k in range(C):
                    ins = pe.matmul(bank[b][:, k * F:(k + 1) * F], STg[b][:, k, :], big1[:, one(c, k), :].rearrange("p o f -> p (o f)"), start=True, stop=True)
                ins.then_inc(S_("n_sum"), 1)

            def turn_g(c, b, j):
                pe.wait_ge(S_("n_safe"), c + 1)
                for q in range(C // 2):
                    ins = pe.transpose(bank[2 + b][:, q * P:(q + 1) * P], pairs(VS[:, b, 2 * q:2 * q + 2, :]), ident[:, :])
                ins.then_inc(S_("n_tp"), 1)

            def out_proj(c, b, j):
                pe.wait_ge(S_("n_gt"), c + 1)
                if not early(c):
                    pe.wait_ge(S_("n_rows"), c - 1)
                for q in range(C // 2):
                    ins = pe.matmul(bank[4 + b][:, q * P:(q + 1) * P], pairs(TS[:, b, 2 * q:2 * q + 2, :]), wo[:, :], start=True, stop=True)
                ins.then_inc(S_("n_proj"), 1)
            pe.wait_ge(S_("m_carried"), 16 * 4)
            pipelined(pe, [(0, total), (1, turn_g), (2, out_proj)])


        def rows_of(ap, c):
            return ap[0:SLOTS, :].rearrange("(t e) f -> e t f", e=TE)[:, tiles(c), :]

        def L1_pool(g, top, narrow):
            gather_pair(g, top, "h", x1_d, None)
            for l in range(LAYERS):
                if l:
                    def step(c, b, j, l=l):
                        g.wait_ge(S_(f"h_free{b}"), j + (26 * l + 1))
                        g.sem_inc(S_("pool_turn"), 1)
                        for k in range(C):
                            g.indirect_dma_start(G[:, b, k, 1, :], None, xt_d[l - 1],
                                                 bass.IndirectOffsetOnAxis(ap=idx_s[:, b, 0, k:k + 1], axis=0),
                                                 bounds_check=top, oob_is_err=False).then_inc(S_(f"h_in{b}"), 16)
                    pipelined(g, [(0, step)])
                g.wait_ge(S_("r_stored"), 16 * (l + 1))
                narrow(4 + l, pos_i, small_v1, gather_from=dt_d[l], into=DCc[:, :].unsqueeze(2))
                g.sem_inc(S_("deg_done"), 1)

            def last(c, b, j):
                g.wait_ge(S_("q2_fin"), c + 1)
                g.sem_inc(S_("pool_turn"), 1)
                for k in range(C):
                    g.indirect_dma_start(out, bass.IndirectOffsetOnAxis(ap=idx_s[:, b, 0, k:k + 1], axis=0), G[:, b, k, 0, :], None,
                                         bounds_check=top, oob_is_err=False).then_inc(S_(f"f_out{b}"), 16)
            pipelined(g, [(0, last)])
            for b in range(2):
                g.wait_ge(S_(f"f_out{b}"), 16 * C * (NCH // 2))

        def L1_sp(sp):
            sp.wait_ge(S_("n_rows"), NCH)
            sp.dma_start(FLB[0][:, :, :], at(flag_d, 2 * T, [[0, F], [1, 2 * T]])).then_inc(S_("flags1"), 16)
            build_S_sp(sp, "s1", 1)

            def store_base(c, b, j):
                sp.wait_ge(S_("h_base"), c + 1)
                sp.dma_start(rows_of(base_d, c), VS[0:TE, b]).then_inc(S_(f"h_stored{b}"), 16)
            pipelined(sp, [(0, store_base)])
            for l in range(LAYERS):
                sp.wait_ge(S_("r_ends"), l + 1)
                for h in range(2):
                    sp.dma_start(crow[0:1, h * T:(h + 1) * T], ccol[0:HT, 2 * h:2 * h + 2]).then_inc(S_("r_row"), 16)
                sp.wait_ge(S_("r_carry"), l + 1)
                for h in range(2):
                    sp.dma_start(ccol[0:HT, 4 + 2 * h:6 + 2 * h], carr[0:1, h * T:(h + 1) * T]).then_inc(S_("r_col"), 16)
                sp.wait_ge(S_("r_d"), l + 1)
                sp.dma_start(at(dt_d[l], 0, [[TE, HT], [HT * TE, 2], [1, TE]]), PB_).then_inc(S_("r_stored"), 16)
                sp.wait_ge(S_("r_stored"), 16 * (l + 1))
                if l == 0:
                    sp.wait_ge(S_("r_val"), 1)
                    sp.wait_ge(S_("x1_fixed"), 1)
                    dense_sp(sp, "b", x1_d, out)
                carry_sp(sp, "p", big1, l)
                if l < 2:
                    def store(c, b, j, l=l):
                        sp.wait_ge(S_("q_out"), c + (l * NCH + 1))
                        sp.dma_start(rows_of(xt_d[l], c), TS[0:TE, b]).then_inc(S_(f"q_stored{b}"), 16)
                    pipelined(sp, [(0, store)])
                    for b in range(2):
                        sp.wait_ge(S_(f"q_stored{b}"), 16 * (NCH // 2) * (l + 1))
                    sp.sem_inc(S_("table"), 1)
                else:
                    for b in range(2):
                        sp.wait_ge(S_(f"h_stored{b}"), 16 * (NCH // 2))

                    def load(c, b, j):
                        if not early(c):
                            sp.wait_ge(S_("q2_fin"), c - 1)
                        for n_, t_ in enumerate((base_d, xt_d[0], xt_d[1])):
                            sp.dma_start(LR[b][0:TE, n_], rows_of(t_, c)).then_inc(S_(f"q2_ld{b}"), 16)
                    pipelined(sp, [(0, load)])

        def L1_dve(v):
            v.wait_ge(S_("x1_fixed"), 1)
            idx = (own_i[1], far_i[1])
            for b in range(2):
                stage_indices(v, "h", idx, b, b)
            build_S_dve(v, "s1", 1)

            def step0(c, b, j, l=0):
                if not early(c):
                    v.wait_ge(S_("h_t"), c + (l * NCH - 1))
                    v.wait_ge(S_("h_cc"), c + (l * NCH - 1))
                norm_dve(v, "h", c, b, j)
                if not early(c):
                    v.wait_ge(S_(f"h_stored{b}"), j * 16)
                v.tensor_tensor(VS[:, b], G[:, b, :, 0, :], XC[:, b, :, 0, :], ALU.add).then_inc(S_("h_base"), 1)
                v.drain().then_inc(S_("h_xc"), 1)
                stage_indices(v, "h", idx, c + 2, b)
            pipelined(v, [(0, step0)])

            for l in range(LAYERS):
                if l:
                    v.wait_ge(S_("table"), l)
                    for b in range(2):
                        stage_indices(v, "h", (pos_i,), b, b)

                    def step(c, b, j, l=l):
                        v.wait_ge(S_(f"h_in{b}"), (j + (25 * (l + 1) + 1)) * (16 * C))
                        v.tensor_copy(G[:, b, :, 0, :], big2[:, tiles(c), :]).then_inc(S_("h_xc"), 1)

                    def refill(c, b, j, l=l):
                        v.wait_ge(S_("h_t"), c + (l * NCH + 1))
                        v.wait_ge(S_("h_cc"), c + (l * NCH + 1))
                        stage_indices(v, "h", (pos_i,), c + 2, b)
                    pipelined(v, [(0, step), (1, refill)])
                rowsum_dve(v, l)
                if l == 0:
                    dense_dve(v, "b")
                    for k in range(3):
                        v.wait_ge(S_(f"db_out{k}"), 16 * (DCH // 3 + (k < 2)))
                v.wait_ge(S_("deg_done"), l + 1)
                v.tensor_tensor(VAL0[:, :], VAL0[:, :], DCc[:, :], ALU.mult)
                v.drain()
                v.tensor_scalar(VAL1[:, :], VAL0[:, :], em[:, 0:1], None, ALU.add)
                v.drain()

                def value(tag, V_, done, sig):
                    def fn(c, b, j, l=l):
                        if not early(c):
                            v.wait_ge(S_(done), c + (l * NCH - 1))
                        v.tensor_tensor(VS[:, b], big1[:, tiles(c), :], bc(V_[:, tiles(c)], F), ALU.mult).then_inc(S_(sig), 1)
                    return fn
                pipelined(v, [(0, value("p", VAL0, "p_fl", "p_v"))])
                carry_dve(v, "p", l)
                v.wait_ge(S_("p_carried"), 64 * (l + 1))
                stages = [(0, value("q", VAL1, "q_sum", "q_v"))]
                if l == 2:
                    def final(c, b, j, l=l):
                        v.wait_ge(S_(f"q2_ld{b}"), (j + 1) * 48)
                        v.tensor_tensor(LR[b][0:TE, 1], LR[b][0:TE, 1], LR[b][0:TE, 2], ALU.add)
                        v.wait_ge(S_("q_sum"), c + (l * NCH + 1))
                        if not early(c):
                            v.wait_ge(S_(f"f_out{b}"), j * (16 * C))
                        v.tensor_tensor(G[0:TE, b, :, 0, :], bank[b][0:TE, 0:C * F].rearrange("p (c f) -> p c f", f=F), LR[b][0:TE, 0], ALU.add)
                        v.drain()
                        v.tensor_tensor(G[0:TE, b, :, 0, :], G[0:TE, b, :, 0, :], LR[b][0:TE, 1], ALU.add)
                        v.tensor_copy(idx_s[:, b, 0, :], scat_i[1][:, tiles(c)])
                        v.drain().then_inc(S_("q2_fin"), 1)
                    stages.append((1, final))
                pipelined(v, stages)

        def rowsum_dve(v, l):
            v.wait_ge(S_("r_sig"), l + 1)
            v.tensor_scalar(MSK[:, :], MSK[:, :], ZETA - GAMMA, GAMMA, ALU.mult, ALU.add)
            v.memset(VAL0[:, :], 0.0)
            v.drain()
            v.tensor_scalar(MSK[:, :], MSK[:, :], 0.0, 1.0, ALU.max, ALU.min).then_inc(S_("r_m"), 1)
            v.wait_ge(S_("r_t"), 2 * l + 1)
            v.tensor_copy(MT, bank[0][0:HT, 0:256].rearrange("r (h e) -> r h e", h=2)[:, :, 0:TE])
            v.drain()

            def both(i0, i1):
                for h in range(2):
                    v.tensor_tensor_scan(PF[:, h, :], smr[:, h, 0:TE], MT[:, h, :], i0[h], ALU.mult, ALU.add)
                    v.tensor_tensor_scan(PB_[:, h, ::-1], smr[:, h, 1:TE + 1][:, ::-1], MT[:, h, ::-1], i1[h], ALU.mult, ALU.add)
                v.drain()
            both((0.0, 0.0), (0.0, 0.0))
            for h in range(2):
                v.tensor_copy(ccol[0:HT, 2 * h:2 * h + 1], PF[:, h, TE - 1:TE])
                v.tensor_copy(ccol[0:HT, 2 * h + 1:2 * h + 2], PB_[:, h, 0:1])
            v.drain().then_inc(S_("r_ends"), 1)
            m = T - 1
            nl, fu = FLB[0][0:1, 0, :], FLB[0][0:1, 1, :]
            A_, B_, A2_, B2_ = [den[0:1, 800 + k * 200:800 + k * 200 + m] for k in range(4)]
            R = crow.rearrange("o (t k) -> o t k", k=2)
            O = carr.rearrange("o (t k) -> o t k", k=2)
            if l == 0:
                v.wait_ge(S_("flags1"), 16)
            v.memset(carr, 0.0)
            v.tensor_tensor(A_, nl[:, 0:m], fu[:, 0:m], ALU.mult)
            v.tensor_tensor(A2_, nl[:, 0:m], fu[:, 1:T], ALU.mult)
            v.wait_ge(S_("r_row"), 32 * (l + 1))
            v.tensor_tensor(B_, nl[:, 0:m], R[:, 0:m, 0], ALU.mult)
            v.tensor_tensor(B2_, nl[:, 0:m], R[:, 1:T, 1], ALU.mult)
            v.drain()
            v.tensor_tensor_scan(O[:, 1:T, 0], A_, B_, 0.0, ALU.mult, ALU.add)
            v.tensor_tensor_scan(O[:, 0:m, 1][:, ::-1], A2_[:, ::-1], B2_[:, ::-1], 0.0, ALU.mult, ALU.add)
            v.drain().then_inc(S_("r_carry"), 1)
            v.wait_ge(S_("r_col"), 32 * (l + 1))
            both([ccol[0:HT, 4 + 2 * h:5 + 2 * h] for h in range(2)], [ccol[0:HT, 5 + 2 * h:6 + 2 * h] for h in range(2)])
            v.tensor_tensor(PF, PF, PB_, ALU.add)
            v.drain()
            v.tensor_tensor(PF, PF, MT, ALU.subtract).then_inc(S_("r_total"), 1)
            v.wait_ge(S_("r_root"), l + 1)
            v.reciprocal(PB_, PB_)
            v.drain()
            v.tensor_scalar(PB_, PB_, 10.0, None, ALU.min).then_inc(S_("r_d"), 1)
            v.wait_ge(S_("r_t"), 2 * l + 2)
            v.tensor_tensor(VAL0[0:TE, :], MSK[0:TE, :], bank[1][0:TE, 0:T], ALU.mult)
            v.drain().then_inc(S_("r_val"), 1)

        def L1_act(s_):
            for l in range(LAYERS):

                def fill(c, b, j, l=l):
                    if l == 0:
                        norm_act(s_, "h", c, b, j)
                    s_.wait_ge(S_("h_xc"), c + (l * NCH + 1))
                    s_.sem_inc(S_("act_turn"), 1)
                    s_.activation(big1[:, tiles(c), :], (XC if l == 0 else G)[:, b, :, 1, :], ACT.Copy).then_inc(S_("h_cc"), 1)
                    s_.wait_ge(S_("h_t"), c + (l * NCH + 1))
                    s_.activation(TT[b][0], bank[b][:, :], ACT.Copy).then_inc(S_("h_e1"), 1)

                def e2(c, b, j, l=l):
                    s_.wait_ge(S_("h_m1"), c + (l * NCH + 1))
                    s_.activation(TT[b][1], bank[2 + b][:, :], ACT.Relu, bias=bias1[:, l:l + 1]).then_inc(S_("h_e2"), 1)

                def e3(c, b, j, l=l):
                    s_.wait_ge(S_("h_m2"), c + (l * NCH + 1))
                    s_.activation(TT[b][2][0:F], bank[4 + b][0:F, :], ACT.Relu, bias=bias2[:, l:l + 1]).then_inc(S_("h_e3"), 1)

                def e4(c, b, j, l=l):
                    s_.wait_ge(S_("h_m3"), c + (l * NCH + 1))
                    s_.sem_inc(S_("act_turn"), 1)
                    s_.activation(MSK[:, tiles(c)], bank[6 + b][:, 0:C], ACT.Copy).then_inc(S_("h_e4"), 1)
                pipelined(s_, [(0, fill), (1, e2), (2, e3), (3, e4)])
                s_.drain()
                s_.activation(MSK[:, :], MSK[:, :], ACT.Sigmoid, bias=bias3[:, l:l + 1]).then_inc(S_("r_sig"), 1)
                s_.wait_ge(S_("r_total"), l + 1)
                s_.activation(PB_, PF, ACT.Sqrt, bias=tiny_c[0:HT, :]).then_inc(S_("r_root"), 1)
                if l == 0:
                    dense_act(s_, "b")
                pipelined(s_, [(0, lambda c, b, j, l=l: ends_act(s_, "p", c, b, j, l * NCH))])

                def widen(c, b, j, l=l):
                    if not early(c):
                        s_.wait_ge(S_("q_sum"), c + (l * NCH - 1))
                        s_.sem_inc(S_("act_turn"), 1)
                    s_.activation(STg[b], S[:, tiles(c), :], ACT.Copy).then_inc(S_("q_st"), 1)

                def copy_out(c, b, j, l=l):
                    if not early(c):
                        s_.wait_ge(S_(f"q_stored{b}"), (j + 25 * l) * 16)
                    s_.wait_ge(S_("q_sum"), c + (l * NCH + 1))
                    s_.sem_inc(S_("act_turn"), 1)
                    s_.activation(pairs(TS[:, b]), bank[b][:, 0:C * F], ACT.Copy).then_inc(S_("q_out"), 1)
                    s_.activation(big2[:, tiles(c), :], bank[b][:, 0:C * F].rearrange("p (c f) -> p c f", f=F), ACT.Copy).then_inc(S_("q_b2"), 1)
                s_.wait_ge(S_("p_carry_t"), l + 1)
                pipelined(s_, [(0, widen)] + ([(1, copy_out)] if l < 2 else []))

        def L1_pe(pe):
            pe.wait_ge(S_("s1_S"), 1)
            for l in range(LAYERS):

                def turn(c, b, j, l=l):
                    pe.wait_ge(S_("h_xc"), c + (l * NCH + 1))
                    for k in range(C):
                        ins = pe.transpose(bank[b][:, k * P:(k + 1) * P], (XC if l == 0 else G)[:, b, k].rearrange("p d f -> p (d f)"), ident[:, :])
                    ins.then_inc(S_("h_t"), 1)

                def m1(c, b, j, l=l):
                    pe.wait_ge(S_("h_e1"), c + (l * NCH + 1))
                    pe.matmul(bank[2 + b][:, :], wb[:, l, :], TT[b][0], start=True, stop=True).then_inc(S_("h_m1"), 1)

                def m2(c, b, j, l=l):
                    pe.wait_ge(S_("h_e2"), c + (l * NCH + 1))
                    pe.matmul(bank[4 + b][0:F, :], at1[:, l, :], TT[b][1], start=True, stop=True).then_inc(S_("h_m2"), 1)

                def m3(c, b, j, l=l):
                    pe.wait_ge(S_("h_e3"), c + (l * NCH + 1))
                    if not early(c):
                        pe.wait_ge(S_("h_e4"), c + (l * NCH - 1))
                    for k in range(C):
                        ins = pe.matmul(bank[6 + b][:, k:k + 1], TT[b][2][0:F, k * P:(k + 1) * P], at2[:, l:l + 1], start=True, stop=True)
                    ins.then_inc(S_("h_m3"), 1)
                if l:
                    pe.wait_ge(S_("q_b2"), l * NCH)
                pipelined(pe, [(0, turn), (1, m1), (2, m2), (3, m3)])
                pe.wait_ge(S_("r_m"), l + 1)
                for h in range(2):
                    ins = pe.transpose(bank[0][0:HT, h * P:(h + 1) * P], MSK[:, h * HT:(h + 1) * HT], ident[:, :])
                ins.then_inc(S_("r_t"), 1)
                pe.wait_ge(S_("r_d"), l + 1)
                for h in range(2):
                    ins = pe.transpose(bank[1][0:TE, h * HT:(h + 1) * HT], PB_[:, h, :], ident[0:HT, 0:HT])
                ins.then_inc(S_("r_t"), 1)
                pipelined(pe, [(0, lambda c, b, j, l=l: ends_pe(pe, "p", "p_v", c, b, j, l * NCH))])
                carry_pe(pe, "p", l)

                def total(c, b, j, l=l):
                    pe.wait_ge(S_("q_v"), c + (l * NCH + 1))
                    if not early(c):
                        pe.wait_ge(S_("q2_fin" if l == 2 else "q_b2"), c + ((l * NCH if l < 2 else 0) - 1))
                    pe.wait_ge(S_("q_st"), c + (l * NCH + 1))
                    for k in range(C):
                        ins = pe.matmul(bank[b][:, k * F:(k + 1) * F], STg[b][:, k, :], VS[:, b, k, :], start=True, stop=True)
                    ins.then_inc(S_("q_sum"), 1)
                pipelined(pe, [(0, total)])

        @block.sync
        def _(sp):
            sp.wait_ge(S_("pads_set"), 1)
            full, part = E // SW, E % SW
            for o, name in enumerate(("dst", "src")):
                sp.dma_start(NI[0:full, o * SW:(o + 1) * SW], a[name][0:full * SW].rearrange("(p j) -> p j", j=SW)).then_inc(S_("ids_in"), 16)
                sp.dma_start(NI[full:full + 1, o * SW:o * SW + part], a[name][full * SW:E].rearrange("(p j) -> p j", p=1)).then_inc(S_("ids_in"), 16)
            sp.dma_start(EW[0:full, :], a["edge_weight"][0:full * SW].rearrange("(p j) -> p j", j=SW)).then_inc(S_("ids_in"), 16)
            sp.dma_start(EW[full:full + 1, 0:part], a["edge_weight"][full * SW:E].rearrange("(p j) -> p j", p=1)).then_inc(S_("ids_in"), 16)
            wi = S_("weights_in")
            wpj, wout = a["L0_gnn_w_proj"], a["L0_gnn_w_out"]
            for r in range(2):
                half = slice(r * F, (r + 1) * F)
                sp.dma_start(wp4[half], wpj.rearrange("h f g -> f h g")).then_inc(wi, 16)
                sp.dma_start(wm[half], wpj.rearrange("(q r) f g -> r f q g", r=2)[r]).then_inc(wi, 16)
                sp.dma_start(wo[half, half], wout).then_inc(wi, 16)
                sp.dma_start(wb[half, :, half], a[("L1_gnn_nb_W", "L1_gnn_self_W")[r]].rearrange("l i o -> i l o")).then_inc(wi, 16)
                sp.dma_start(bias1[half, :], a[("L1_gnn_nb_b", "L1_gnn_self_b")[r]].rearrange("l f -> f l"), allow_slow_non_contiguous=True).then_inc(wi, 16)
                sp.dma_start(rsT[:, r * HEADS:(r + 1) * HEADS], a[("L0_gnn_radial_score", "L0_gnn_tangential_score")[r]].rearrange("h f -> f h"), allow_slow_non_contiguous=True).then_inc(wi, 16)
            sp.dma_start(at1[:, :, :], a["L1_gnn_att1_W"].rearrange("l i o -> i l o")).then_inc(wi, 16)
            sp.dma_start(at2[:, :], a["L1_gnn_att2_W"].rearrange("l f o -> f (l o)"), allow_slow_non_contiguous=True).then_inc(wi, 16)
            sp.dma_start(bias2[:, :], a["L1_gnn_att1_b"].rearrange("l f -> f l"), allow_slow_non_contiguous=True).then_inc(wi, 16)
            sp.dma_start(bias3[:, :], at(a["L1_gnn_att2_b"], 0, [[0, P], [1, LAYERS]])).then_inc(wi, 16)
            sp.dma_start(rscale[:, :], at(a["L0_gnn_radial_distance_scale"], 0, [[0, P], [1, 1]])).then_inc(wi, 16)
            for l in range(2):
                sp.dma_start(xt_d[l][SLOTS:SLOTS + 8, :], zrow).then_inc(S_("tables_out"), 16)
            for l in range(LAYERS):
                sp.dma_start(at(dt_d[l], SLOTS, [[1, 8], [1, 1]]), zrow_ten).then_inc(S_("tables_out"), 16)
            sp.wait_ge(S_("payload_made"), 1)
            sp.dma_start(pay_d[0:full * SW, :].rearrange("(p j) w -> p j w", j=SW), PAYT[0:full]).then_inc(S_("tables_out"), 16)
            sp.dma_start(pay_d[full * SW:E, :].rearrange("(p j) w -> p j w", p=1), PAYT[full:full + 1, 0:part, :]).then_inc(S_("tables_out"), 16)
            sp.dma_start(dstf_d[0:full * SW, :].rearrange("(p j) w -> p (j w)", j=SW), NF[0:full, 0:SW]).then_inc(S_("tables_out"), 16)
            sp.dma_start(dstf_d[full * SW:E, :].rearrange("(p j) w -> p (j w)", p=1), NF[full:full + 1, 0:part]).then_inc(S_("tables_out"), 16)
            sp.dma_start(pos_d.rearrange("(p j) w -> p (j w)", p=100), INIT).then_inc(S_("tables_out"), 16)
            sp.wait_ge(S_("sorted"), 1)
            for o in range(2):
                sp.dma_start(key_d[o].rearrange("(p j) -> p j", p=P), KA[:, o * SW:(o + 1) * SW]).then_inc(S_("keys_out"), 16)
            sp.wait_ge(S_("keys_out"), 32)
            for o in range(2):
                sp.dma_start(TR[:, o * 254:(o + 1) * 254].rearrange("r (h j) -> r h j", h=2).bitcast(F32),
                             at(key_d, o * SORT, [[TE, HT], [HT * TE, 2], [1, 127]])).then_inc(S_("keys_back"), 16)
            sp.wait_ge(S_("decoded"), 1)
            for o in range(2):
                sp.dma_start(at(node_d, o * NTROW + 128, [[128, HT], [HT * 128, 2], [1, 128]]), NTt[:, 2 * o:2 * o + 2, :]).then_inc(S_("nodes_out"), 16)
                for k, t_ in enumerate((NLt, FUt)):
                    sp.dma_start(at(flag_d, (2 * o + k) * T, [[1, HT], [HT, 2]]), t_[:, 2 * o:2 * o + 2], allow_slow_non_contiguous=True).then_inc(S_("nodes_out"), 16)
            for off in (0, 128 + T * 128):
                sp.dma_start(at(node_d, off, [[NTROW, 2], [1, 128]]), PADT).then_inc(S_("nodes_out"), 16)
            dense_sp(sp, "a", a["x"], x1_d)
            if rest(3):
                L0_sp(sp)
            if rest(5):
                L1_sp(sp)
            sp.wait_ge(S_("nodes_out"), 16 * 8)
            sp.wait_ge(S_("tables_out"), 16 * 10)

        @block.vector
        def _(v):
            v.memset(NI, N)
            v.memset(EW, 0.0)
            v.memset(eps_c[:, :], LN_EPS)
            v.memset(PADT, -1.0)
            v.memset(zrow, 0.0)
            v.memset(zrow_ten, 10.0)
            v.memset(tiny_c[:, :], 1e-6)
            v.memset(A2[:, :], 0.0)
            v.memset(wo[:, :], 0.0)
            v.memset(wb[:, :, :], 0.0)
            v.memset(INIT, float(ZERO_ROW))
            v.memset(SIt, NOWHERE)
            v.memset(Et, 0.0).then_inc(S_("pads_set"), 1)
            v.wait_ge(S_("ids_in"), 16 * 6)
            v.tensor_copy(NF, NI)
            v.drain()
            v.tensor_copy(PAYT[:, :, 0], NF[:, SW:2 * SW])
            v.tensor_copy(PAYT[:, :, 1], EW).then_inc(S_("payload_made"), 1)
            v.tensor_scalar(T1t, NF, float(HALF), None, ALU.is_ge)
            v.tensor_scalar(KA, NF, float(-HALF), None, ALU.add)
            v.tensor_scalar(KB, NF, -1.0, float(HALF - 1), ALU.mult, ALU.add)
            v.drain()
            v.tensor_tensor(KA, KA, KB, ALU.max)
            v.tensor_scalar(T2t.bitcast(I32), T1t, -1.0, None, ALU.add)
            v.drain()
            v.tensor_scalar(NI, KA, float(OFFSET >> 15), None, ALU.add)
            v.tensor_scalar(T2t.bitcast(I32), T2t.bitcast(I32), FLIP, None, ALU.bitwise_and)
            v.drain()
            v.tensor_scalar(NI, NI, 15, None, ALU.logical_shift_left)
            v.wait_ge(S_("iotas"), 1)
            v.drain()
            v.tensor_tensor(NI, NI, EI, ALU.bitwise_or)
            v.drain()
            v.tensor_tensor(KA.bitcast(I32), NI, T2t.bitcast(I32), ALU.bitwise_xor)
            v.tensor_scalar(em[:, :], PI, float(TE), None, ALU.is_ge)
            for b in range(7):
                v.tensor_scalar(PB[:, b:b + 1], PI, b, 1, ALU.logical_shift_right, ALU.bitwise_and)
            v.drain()
            v.tensor_scalar(SG[:, 0:7], PB, -2.0, 1.0, ALU.mult, ALU.add)
            v.drain()
            v.tensor_tensor(SG[:, 8:14], SG[:, 0:6], SG[:, 1:7], ALU.mult)
            v.tensor_scalar(SG[:, 7:8], SG[:, 0:1], -1.0, None, ALU.mult)
            cur, oth = KA, KB
            v4 = cur.rearrange("p (g q) -> p g q", q=4)[:, :, 2:4]
            v.drain()
            v.tensor_scalar(v4, v4, -1.0, None, ALU.mult)

            def exchange(cur, oth, d):
                x = cur.rearrange("p (g t d) -> p g t d", t=2, d=d)
                y = oth.rearrange("p (g t d) -> p g t d", t=2, d=d)
                v.drain()
                v.tensor_tensor(y[:, :, 0, :], x[:, :, 0, :], x[:, :, 1, :], ALU.min)
                v.tensor_tensor(y[:, :, 1, :], x[:, :, 0, :], x[:, :, 1, :], ALU.max)
                return oth, cur

            turns = 0
            for k in range(1, 16):
                if k >= 9:
                    v.drain().then_inc(S_("turn_in"), 1)
                    turns += 1
                    v.wait_ge(S_("turned"), 2 * turns - 1)
                    v.tensor_copy(cur, bank[0][:, :])
                    for st in range(k - 9, -1, -1):
                        cur, oth = exchange(cur, oth, 1 << st)
                    sides.append((turns, 0 if cur is KA else 1))
                    v.drain().then_inc(S_("turn_in"), 1)
                    v.wait_ge(S_("turned"), 2 * turns)
                    v.tensor_copy(cur, bank[1][:, :])
                for st in range(min(k, 8) - 1, -1, -1):
                    cur, oth = exchange(cur, oth, 1 << st)
                side_in.append(0 if cur is KA else 1)
                v.drain()
                if k <= 6:
                    w = 1 << k
                    m = cur.rearrange("p (g q) -> p g q", q=4 * w)[:, :, w:3 * w]
                    v.tensor_scalar(m, m, -1.0, None, ALU.mult)
                elif k == 7:
                    m = cur.rearrange("p (g q) -> p g q", q=256)
                    v.tensor_scalar(m[:, :, 0:128], m[:, :, 0:128], SG[:, 0:1], None, ALU.mult)
                    v.tensor_scalar(m[:, :, 128:256], m[:, :, 128:256], SG[:, 7:8], None, ALU.mult)
                elif k <= 13:
                    v.tensor_scalar(cur, cur, SG[:, k:k + 1], None, ALU.mult)
                elif k == 14:
                    v.tensor_scalar(cur, cur, SG[:, 6:7], None, ALU.mult)
            if cur is not KA:
                v.tensor_copy(KA, cur)
            v.drain().then_inc(S_("sorted"), 1)

            v.wait_ge(S_("keys_back"), 32)
            v.tensor_scalar(D1, TR, 31, None, ALU.arith_shift_right)
            v.drain()
            v.tensor_scalar(D2, D1, FLIP, None, ALU.bitwise_and)
            v.tensor_copy(D3, D1)
            v.drain()
            v.tensor_tensor(D1, TR, D2, ALU.bitwise_xor)
            v.drain()
            v.tensor_scalar(D2, D1, 32767, None, ALU.bitwise_and)
            v.tensor_scalar(D1, D1, 15, None, ALU.logical_shift_right)
            v.drain()
            v.tensor_scalar(D4, D3, 2.0, 1.0, ALU.mult, ALU.add)
            v.drain()
            v.scalar_tensor_tensor(D4, D1, float(-(OFFSET >> 15)), D4, ALU.add, ALU.mult)
            v.drain()
            ndf = ND.rearrange("r q j -> r (q j)")
            v.scalar_tensor_tensor(ndf, D3, float(HALF), D4, ALU.add, ALU.add)
            v.tensor_scalar(Et[:, :, 0:TE], D2.rearrange("r (q j) -> r q j", j=127)[:, :, 0:TE], float(E - 1), None, ALU.min)
            v.drain()
            v.tensor_copy(NTt[:, :, 0:TE], ND[:, :, 0:TE])
            v.tensor_copy(NTt[:, :, TE:TE + 1], ND[:, :, 0:1])
            v.tensor_copy(NTt[:, :, TE + 1:TE + 2], ND[:, :, TE - 1:TE])
            v.tensor_tensor(NE, ND[:, :, 0:TE], ND[:, :, 1:TE + 1], ALU.not_equal)
            v.tensor_tensor(FUt, ND[:, :, 0], ND[:, :, TE - 1], ALU.is_equal)
            v.drain()
            v.tensor_scalar(NLt, NE[:, :, TE - 1], -1.0, 1.0, ALU.mult, ALU.add)
            v.tensor_scalar(SIt[:, :, 0:TE], NE, -FAR, FAR, ALU.mult, ALU.add)
            v.drain()
            v.tensor_tensor(SIt[:, :, 0:TE], SIt[:, :, 0:TE], ND[:, :, 0:TE], ALU.add)
            v.memset(smr[:, :, 0:1], 1.0)
            v.tensor_scalar(smr[:, :, 1:TE + 1], NE[:, 2:4, :], -1.0, 1.0, ALU.mult, ALU.add)
            v.drain().then_inc(S_("decoded"), 1)
            for o in range(2):
                v.memset(scat_i[o][:, T:], 0)
                v.memset(own_i[o][:, T:], 0)
                v.memset(perm_i[o][:, T:], 0)
            v.wait_ge(S_("tiles_turned"), 1)
            for o in range(2):
                v.tensor_copy(node[o][:, :], bank[3 * o][:, 0:T])
                v.tensor_scalar(own_i[o][:, 0:T], bank[3 * o][:, 0:T], float(N - 1), None, ALU.min)
                v.tensor_copy(scat_i[o][:, 0:T], bank[3 * o + 1][:, 0:T])
                v.tensor_copy(perm_i[o][:, 0:T], bank[3 * o + 2][:, 0:T])
            v.drain().then_inc(S_("indices_ready"), 1)
            dense_dve(v, "a")
            if rest(3):
                L0_dve(v)
            if rest(5):
                L1_dve(v)

        @block.scalar
        def _(s_):
            s_.wait_ge(S_("scores_t"), 1)
            s_.activation(wT, bank[6][0:F, :], ACT.Copy).then_inc(S_("scores_c"), 1)
            s_.wait_ge(S_("scores_t"), 2)
            s_.activation(A2[0:F, 0:H8], bank[7][0:F, 0:H8], ACT.Copy)
            s_.activation(A2[F:P, H8:], bank[7][F:P, 0:H8], ACT.Copy).then_inc(S_("scores_c"), 1)
            dense_act(s_, "a")
            if rest(3):
                L0_act(s_)
            if rest(5):
                L1_act(s_)

        @block.tensor
        def _(pe):
            pe.wait_ge(S_("iotas"), 1)
            pe.wait_ge(S_("weights_in"), 16 * 17)
            for h in range(HEADS):
                ins = pe.transpose(bank[6][0:F, h * P:(h + 1) * P], wp4[:, h, :], ident[:, :])
            ins.then_inc(S_("scores_t"), 1)
            pe.wait_ge(S_("scores_c"), 1)
            for h in range(H8):
                ins = pe.matmul(bank[7][:, h:h + 1], wT[:, (h % HEADS) * P:(h % HEADS + 1) * P], rsT[:, h:h + 1], start=True, stop=True)
            ins.then_inc(S_("scores_t"), 1)
            for turn in range(1, 8):
                src = (KA, KB)[side_in[7 + turn - 1]]
                pe.wait_ge(S_("turn_in"), 2 * turn - 1)
                for q in range(4):
                    ins = pe.transpose(bank[0][:, q * P:(q + 1) * P], src[:, q * P:(q + 1) * P], ident[:, :])
                ins.then_inc(S_("turned"), 1)
                src = (KA, KB)[sides[turn - 1][1]]
                pe.wait_ge(S_("turn_in"), 2 * turn)
                for q in range(4):
                    ins = pe.transpose(bank[1][:, q * P:(q + 1) * P], src[:, q * P:(q + 1) * P], ident[:, :])
                ins.then_inc(S_("turned"), 1)
            pe.wait_ge(S_("decoded"), 1)
            for o in range(2):
                for n_, t_ in enumerate((NTt, SIt, Et)):
                    for h in range(2):
                        ins = pe.transpose(bank[3 * o + n_][:, h * HT:(h + 1) * HT], t_[:, 2 * o + h, :], ident[0:HT, 0:HT])
            ins.then_inc(S_("tiles_turned"), 1)
            if rest(3):
                L0_pe(pe)
            if rest(5):
                L1_pe(pe)

        @block.gpsimd
        def _(g):
            top = g.to_reg(N - 1)
            for o in range(2):
                g.iota(EI[:, o * SW:(o + 1) * SW], [[1, SW]], base=0, channel_multiplier=SW)
            g.iota(PI, [[0, 1]], base=0, channel_multiplier=1)
            g.iota(posn, [[TE, T]], base=0, channel_multiplier=1)
            g.memset(ident[:, :], 0.0)
            g.drain()
            g.tensor_copy(posv[:, :, 0], posn)
            g.affine_select(ident[:, :], ident[:, :], [[-1, P]], ALU.not_equal, 1.0, base=0, channel_multiplier=1)
            g.drain().then_inc(S_("iotas"), 1)

            def narrow(n_before, idx, slot_v, gather_from=None, into=None, scatter_to=None, source=None, w=1):
                def take(b, c):
                    if into is not None:
                        g.tensor_copy(into[:, c * SMALL:(c + 1) * SMALL] if isinstance(c, int) else into[:, ds(c * SMALL, SMALL)], slot_v[:, b])

                def issue(b, c):
                    sl = slice(c * SMALL, (c + 1) * SMALL) if isinstance(c, int) else ds(c * SMALL, SMALL)
                    g.tensor_copy(small_i[:, b], idx[:, sl])
                    if source is not None:
                        g.tensor_copy(slot_v[:, b], source[:, sl])
                    g.drain()
                    for k in range(SMALL):
                        off = bass.IndirectOffsetOnAxis(ap=small_i[:, b, k:k + 1], axis=0)
                        if gather_from is not None:
                            g.indirect_dma_start(slot_v[:, b, k], None, gather_from, off, bounds_check=top, oob_is_err=False).then_inc(S_(f"narrow{b}"), 16)
                        else:
                            g.indirect_dma_start(scatter_to, off, slot_v[:, b, k], None, bounds_check=top, oob_is_err=False).then_inc(S_(f"narrow{b}"), 16)

                for b in range(2):
                    issue(b, b)
                with g.Fori(1, NSM // 2) as j:
                    for b in range(2):
                        g.wait_ge(S_(f"narrow{b}"), (j + n_before * (NSM // 2)) * (16 * SMALL))
                        g.sem_inc(S_("pool_turn"), 1)
                        take(b, j * 2 + (b - 2))
                        g.drain()
                        issue(b, j * 2 + b)
                for b in range(2):
                    g.wait_ge(S_(f"narrow{b}"), 16 * SMALL * (NSM // 2) * (n_before + 1))
                    take(b, NSM - 2 + b)
                g.drain()

            g.wait_ge(S_("indices_ready"), 1)
            g.wait_ge(S_("tables_out"), 16 * 10)
            narrow(0, perm_i[0], small_v, gather_from=pay_d, into=payg, w=2)
            g.tensor_copy(far_i[0][:, 0:T], payg[:, :, 0])
            narrow(1, perm_i[1], small_v1, gather_from=dstf_d, into=dstg)
            g.tensor_copy(far_i[1][:, 0:T], dstg[:, :, 0])
            narrow(2, scat_i[1], small_v1, scatter_to=pos_d, source=posv)
            g.drain()
            narrow(3, far_i[1], small_v1, gather_from=pos_d, into=posg)
            g.tensor_copy(pos_i[:, 0:T], posg[:, :, 0]).then_inc(S_("small_done"), 1)
            if rest(3):
                L0_pool(g, top)
            if rest(5):
                L1_pool(g, top, narrow)


sides, side_in = [], []

_INS = ["x", "src", "dst", "edge_weight", "L0_gnn_w_proj", "L0_gnn_radial_score", "L0_gnn_tangential_score",
        "L0_gnn_radial_distance_scale", "L0_gnn_w_out", "L1_gnn_nb_W", "L1_gnn_nb_b", "L1_gnn_self_W",
        "L1_gnn_self_b", "L1_gnn_att1_W", "L1_gnn_att1_b", "L1_gnn_att2_W", "L1_gnn_att2_b"]
STOP = 99


def kernel(**inputs):
    import concourse.bacc as bacc
    from concourse.bass_utils import run_bass_kernel_spmd
    nc = bacc.Bacc("TRN2", target_bir_lowering=False, num_devices=1)
    arrays, a = {}, {}
    for name in _INS:
        value = np.ascontiguousarray(inputs[name])
        if value.ndim == 0:
            value = value.reshape(1)
        arrays["in_" + name] = value
        a[name] = nc.dram_tensor("in_" + name, value.shape, mybir.dt.from_np(value.dtype), kind="ExternalInput").ap()
    out = nc.dram_tensor("out_0", (N, F), F32, kind="ExternalOutput").ap()
    del sides[:], side_in[:]
    build(nc, a, out, STOP, "ExternalOutput" if STOP < 99 else "Internal")
    r = run_bass_kernel_spmd(nc, [arrays], core_ids=[0])
    return r.results[0]["out_0"]
```

```python
from contextlib import ExitStack

import numpy as np
import concourse.bass as bass
from concourse import mybir

F32 = mybir.dt.float32
BF16 = mybir.dt.bfloat16
I32 = mybir.dt.int32
ALU = mybir.AluOpType
ACT = mybir.ActivationFunctionType
AX = mybir.AxisListType
ds = bass.ds

P = 128
N, F = 100000, 64
E = 25000
HEADS, LAYERS = 4, 3
H8 = 2 * HEADS
GAMMA, ZETA = -0.45, 1.05
LN_EPS = 1e-5

TE = 126
CARRY = TE
T = 200
HT = T // 2
SLOTS = T * TE
C = 4
NCH = T // C
SMALL = 20
NSM = T // SMALL
SORT = 32768
SW = SORT // P
HALF = N // 2
OFFSET = 1 << 23
FLIP = -2147483648 + 32767
NOWHERE = 2.0e6
FAR = 1.0e6
ZERO_ROW = SLOTS
DSMALL = 14
BY_DMA = 4 * DSMALL
NLK = (T - BY_DMA) // C
assert NLK % 2 == 0
DEG = T + 1
LOW = -1.0e38
HUGE = 3.4028234663852886e38
HC = 8
KC = T // HC
SCAN = KC * TE

RW = 8
DCH = 96
DB = NCH
DA = DCH - DB
TAILP = (N - P * RW * DCH) // (2 * RW)
assert P * RW * DCH + 2 * RW * TAILP == N


def build(nc, a, out, STOP, scratch_kind):
    ctx = ExitStack()
    with ctx:
        def sb(name, shape, dt=F32):
            return ctx.enter_context(nc.sbuf_tensor(name, shape, dt))

        def sem(name):
            return ctx.enter_context(nc.semaphore(name))

        def dram(name, shape, dt=F32):
            return nc.dram_tensor("out_dbg_" + name if scratch_kind == "ExternalOutput" else name,
                                  shape, dt, kind=scratch_kind).ap()

        def at(ap, offset, pattern):
            return bass.AP(tensor=ap.tensor, offset=offset, ap=pattern)

        key_d = dram("keys", (2, SORT))
        pay_d = dram("payload", (E, 2))
        dstf_d = dram("dst_float", (E, 1))
        NTROW = 128 + T * 128 + 128
        node_d = dram("tile_nodes", (2, NTROW))
        flag_d = dram("tile_flags", (2, 2, T))
        pos_d = dram("position_of", (N, 1))
        x1_d = dram("x_after_layer0", (N, F))
        xt_d = [dram(f"layer_rows{l}", (SLOTS + 8, F)) for l in range(2)]
        dt_d = [dram(f"degree_rows{l}", (SLOTS + 8, 1)) for l in range(LAYERS)]
        base_d = dram("base_rows", (SLOTS, F))
        row_d = dram("row_of_far_degree", (1, T * P), BF16)

        big1 = sb("big1", [P, T, F])
        big2 = sb("big2", [P, T, F])
        regs = sb("regs", [P, T * F])
        den = sb("den", [P, 9 * RW * F + 192])
        S = regs[:, :].bitcast(BF16).rearrange("p (t e) -> p t e", e=P)
        b2 = big2[:, :, :].rearrange("p t f -> p (t f)")
        b1 = big1[:, :, :].rearrange("p t f -> p (t f)")
        dX = [den[:, (3 * k) * 512:(3 * k + 1) * 512].rearrange("p (r f) -> p r f", f=F) for k in range(3)]
        dC = [den[:, (3 * k + 1) * 512:(3 * k + 2) * 512].rearrange("p (r f) -> p r f", f=F) for k in range(3)]
        dQ = [den[:, (3 * k + 2) * 512:(3 * k + 3) * 512].rearrange("p (r f) -> p r f", f=F) for k in range(3)]
        dstat = sb("dstat", [P, 3, 3, RW])

        KA, KB = b1[:, 0:512], b1[:, 512:1024]
        NI = b1[:, 1024:1536].bitcast(I32)
        NF = b1[:, 1536:2048]
        EI = b1[:, 2048:2560].bitcast(I32)
        T1t, T2t = b1[:, 2560:3072], b1[:, 3072:3584]
        EW = b1[:, 3584:3840]
        PAYT = b1[:, 3840:4352].rearrange("p (j w) -> p j w", w=2)
        SG = b1[:, 4352:4368]
        PI = b1[:, 4368:4369].bitcast(I32)
        PB = b1[:, 4369:4376].bitcast(I32)
        TR = b1[0:HT, 4400:4400 + 508].bitcast(I32)
        D1 = b1[0:HT, 4920:4920 + 508].bitcast(I32)
        D2 = b1[0:HT, 5440:5440 + 508].bitcast(I32)
        D3 = b1[0:HT, 5960:5960 + 508]
        D4 = b1[0:HT, 6480:6480 + 508]
        ND = b1[0:HT, 7000:7000 + 508].rearrange("r (q j) -> r q j", j=127)
        NTt = b1[0:HT, 7520:7520 + 512].rearrange("r (q j) -> r q j", j=128)
        SIt = b1[0:HT, 8040:8040 + 512].rearrange("r (q j) -> r q j", j=128)
        Et = b1[0:HT, 8560:8560 + 512].rearrange("r (q j) -> r q j", j=128)
        NE = b1[0:HT, 9080:9080 + 504].rearrange("r (q j) -> r q j", j=126)
        NLt = b1[0:HT, 9600:9604]
        FUt = b1[0:HT, 9604:9608]
        PADT = b1[0:2, 9700:9828]
        INIT = b1[0:100, 10000:11000]

        node = [sb(f"node{o}", [P, T]) for o in range(2)]
        scat_i = [sb(f"scat_i{o}", [P, T + 8], I32) for o in range(2)]
        own_i = [sb(f"own_i{o}", [P, T + 8], I32) for o in range(2)]
        far_i = [sb(f"far_i{o}", [P, T + 8], I32) for o in range(2)]
        pos_i = sb("pos_i", [P, T + 8], I32)
        wneg = sb("wneg", [P, T])
        perm0 = b2[:, 0:T].bitcast(I32)
        payg = b2[:, 416:816].rearrange("p (t w) -> p t w", w=2)
        posn = b2[:, 1416:1616].bitcast(I32)
        small_v = sb("small_v", [P, 2, SMALL, 2])
        small_i = sb("small_i", [P, 2, SMALL], I32)
        small_v1 = sb("small_v1", [P, 2, SMALL, 1])

        G = sb("G", [P, 2, C, 2, F])
        XC = sb("XC", [P, 2, C, 2, F])
        SQ = sb("SQ", [P, 2, C, 2, F])
        VS = sb("VS", [P, 2, C, F])
        TS = sb("TS", [P, 2, C, F])
        stat = sb("stat", [P, 2, 3, 2 * C])
        idx_s = sb("idx_s", [P, 2, 2, C], I32)
        SE = sb("SE", [P, T, 2])
        Zs = [t_[:, :, :, :, :].rearrange("p b c d f -> p (b c d f)").rearrange("p (c h f) -> p c h f", c=C, f=F) for t_ in (G, XC)]
        ZTs = [SQ[:, :, :, :, :].rearrange("p b c d f -> p (b c d f)"), den[:, 1024:2048]]
        LG = den[:, 3200:4800].rearrange("p (t h) -> p t h", h=H8)
        LGP = regs[:, 9480:9480 + T * H8]
        BT = den[:, 3200:4000].rearrange("p (t h) -> p t h", h=HEADS)
        NB = [den[:, k * 512:(k + 1) * 512].rearrange("p (t e) -> p t e", e=P) for k in range(2)]
        NBL = [den[:, 3072 + k * 512:3584 + k * 512].rearrange("p (t e) -> p t e", e=P) for k in range(2)]
        STg = [den[:, 2048 + k * 512:2560 + k * 512].rearrange("p (t e) -> p t e", e=P) for k in range(2)]
        IDS = den[0:64, 0:SCAN + 2]
        SQn = den[0:64, 0:SCAN]
        SAME = regs[0:64, 0:SCAN + 1]
        NEG = regs[0:64, 3160:3160 + SCAN + 1]
        SL = regs[0:64, 6320:6320 + SCAN]
        SP_ = regs[0:64, 9480:9480 + SCAN]
        ccol = sb("ccol", [P, 8])
        crow = den[0:1, 4000:4400]
        carr = den[0:1, 4400:4800]
        FLS = den[0:F, 4000:4400].rearrange("f (t k) -> f t k", k=2)
        AF, AB, BF_, BB = [den[0:F, k * 200:(k + 1) * 200] for k in range(4)]
        CF = den[0:F, 1024:1424].rearrange("f (k t) -> f k t", k=2)
        CT = den[0:HT, 1424:1680].rearrange("r (q f) -> r q f", f=F)
        FLB = [sb(f"FLB{o}", [F, 2, T]) for o in range(1)]
        TT = [[den[:, (3 * b + k) * 512:(3 * b + k + 1) * 512] for k in range(3)] for b in range(2)]
        LR = [den[:, 3072 + b * 768:3072 + (b + 1) * 768].rearrange("p (n c f) -> p n c f", n=3, f=F) for b in range(2)]
        MT, PF, PB_ = [den[0:HT, k * 256:k * 256 + 252].rearrange("r (h e) -> r h e", h=2) for k in range(3)]
        MSK = sb("MSK", [P, T])
        VAL0 = sb("VAL0", [P, T])
        VAL1 = sb("VAL1", [P, T])
        DCc = sb("DCc", [P, T])
        DG = den[:, 1024:1327].bitcast(BF16).rearrange("p (k t) -> p k t", k=3)
        RB = [den[:, 1536 + k * 256:1792 + k * 256].bitcast(BF16) for k in range(2)]
        OH = [den[:, 2048 + k * 256:2304 + k * 256].bitcast(BF16) for k in range(2)]
        PICK = [den[:, 2560 + k * 202:2560 + k * 202 + DEG] for k in range(C)]
        RES = [den[:, 3072 + k * 202:3072 + k * 202 + T] for k in range(2)]
        QI = [den[:, 2560 + k * 202:2560 + k * 202 + T].bitcast(I32) for k in range(2)]
        ER = den[0:HT, 3500:3628].bitcast(BF16).rearrange("r (q j) -> r q j", q=2)
        tile_far = wneg
        steps_i = own_i[0][:, 0:DEG]
        steps = far_i[0][:, 0:DEG].bitcast(F32)
        pnum = sb("pnum", [P, 1])
        perm_i = [perm0, VAL1[:, :].bitcast(I32)]
        posv = VAL0[:, :].unsqueeze(2)
        smr = sb("smr", [HT, 2, TE + 1])
        em = sb("em", [P, 1])
        tiny_c = sb("tiny_c", [P, 1])

        wp = SQ[:, 0, :, 0, :]
        wp4 = sb("wp4", [P, HEADS, F])
        wm = sb("wm", [P, 2, F])
        rsT = sb("rsT", [F, H8])
        A2 = sb("A2", [P, 2 * H8])
        wo = sb("wo", [P, P])
        wb = sb("wb", [P, LAYERS, P])
        at1 = sb("at1", [P, LAYERS, F])
        at2 = sb("at2", [F, LAYERS])
        bias1 = sb("bias1", [P, LAYERS])
        bias2 = sb("bias2", [F, LAYERS])
        bias3 = sb("bias3", [P, LAYERS])
        rscale = sb("rscale", [P, 1])
        wT = b1[0:F, 11100:11100 + 512]
        zrow = b1[0:8, 11700:11764]
        zrow_ten = b1[0:8, 11764:11765]

        ident = sb("ident", [P, P])
        eps_c = sb("eps_c", [P, 1])

        bank = [ctx.enter_context(nc.psum_tensor(f"bank{i}", [P, 512], F32)) for i in range(8)]

        s = {}

        def S_(name):
            if name not in s:
                s[name] = sem(name)
            return s[name]

        def pipelined(eng, stages, n=NCH):
            deep = max(lag for lag, _ in stages)
            peel = (deep + 3) // 2 * 2
            for c in range(peel):
                for lag, fn in stages:
                    if c - lag >= 0:
                        fn(c - lag, (c - lag) % 2, (c - lag) // 2)
            with eng.Fori(peel // 2, n // 2) as j:
                for b in range(2):
                    for lag, fn in stages:
                        fn(j * 2 + (b - lag), (b - lag) % 2, j + (b - lag) // 2)
            for c in range(n, n + deep):
                for lag, fn in stages:
                    if c - lag < n:
                        fn(c - lag, (c - lag) % 2, (c - lag) // 2)

        def early(c):
            return isinstance(c, int) and c < 2

        def tiles(c, shift=0):
            return slice(c * C + shift, c * C + shift + C) if isinstance(c, int) else ds(c * C + shift, C)

        def one(c, k):
            return slice(c * C + k, c * C + k + 1) if isinstance(c, int) else ds(c * C + k, 1)

        def bc(ap, n):
            return ap.unsqueeze(len(ap.shape)).broadcast_to([*ap.shape, n])

        BLOCK3 = at

        ctx.enter_context(nc.allow_non_contiguous_dma(reason="columns of flags, biases and ends of tiles"))
        block = ctx.enter_context(nc.Block())

        def rest(n):
            return STOP >= n

        def dense_rows(ap, c):
            if isinstance(c, int):
                return ap[0:P * RW * DCH, :].rearrange("(p c r) f -> c p r f", c=DCH, r=RW)[c]
            return ap[0:P * RW * DCH, :].rearrange("(p c r) f -> c p r f", c=DCH, r=RW)[ds(c, 1)].rearrange("o p r f -> (o p) r f")

        def dense_tail(ap, u):
            return ap[P * RW * DCH:N, :].rearrange("(p u r) f -> u p r f", u=2, r=RW)[u]

        dBuf = list(zip(dX, dC, dQ))
        bBuf = [tuple(b2[:, (3 * k + i) * 512:(3 * k + i + 1) * 512].rearrange("p (r f) -> p r f", f=F) for i in range(3))
                for k in range(2)]

        assert all(len(range(k, DA + 2, 3)) == (DA + 2) // 3 for k in range(3))
        RUN_A, RUN_B = ("da", 0, 0), ("da", DA + 2, (DA + 2) // 3)
        LOOP_A, LOOP_B = ("dl", 0, 0), ("dl", DB, DB // 2)

        def dense_stores(k):
            return len(range(k, DA + 2, 3))

        def dense_first(v, tag, c, k, n, j, buf):
            X_, C_, _ = buf[k]
            v.wait_ge(S_(f"{tag[0]}_in{k}"), (j + (tag[2] + 1)) * 16)
            v.tensor_reduce(dstat[0:n, k, 0], X_[0:n], AX.X, ALU.add)
            v.drain()
            v.scalar_tensor_tensor(C_[0:n], dstat[0:n, k, 0].unsqueeze(2).broadcast_to([n, RW, F]), -1.0 / F,
                                   X_[0:n], ALU.mult, ALU.add).then_inc(S_(f"{tag[0]}_cen"), 1)

        def dense_second(v, tag, c, k, n, buf):
            v.wait_ge(S_(f"{tag[0]}_sq"), c + (tag[1] + 1))
            v.tensor_reduce(dstat[0:n, k, 1], buf[k][2][0:n], AX.X, ALU.add).then_inc(S_(f"{tag[0]}_var"), 1)

        def dense_third(v, tag, c, k, n, buf):
            X_, C_, _ = buf[k]
            v.wait_ge(S_(f"{tag[0]}_std"), c + (tag[1] + 1))
            v.reciprocal(dstat[0:n, k, 2], dstat[0:n, k, 2])
            v.drain()
            v.scalar_tensor_tensor(C_[0:n], C_[0:n], 0.0,
                                   dstat[0:n, k, 2].unsqueeze(2).broadcast_to([n, RW, F]), ALU.max, ALU.mult)
            v.drain()
            v.tensor_tensor(X_[0:n], X_[0:n], C_[0:n], ALU.add).then_inc(S_(f"{tag[0]}_done"), 1)

        def dense_square(s_, tag, c, k, n, buf):
            s_.wait_ge(S_(f"{tag[0]}_cen"), c + (tag[1] + 1))
            s_.activation(buf[k][2][0:n], buf[k][1][0:n], ACT.Square).then_inc(S_(f"{tag[0]}_sq"), 1)

        def dense_root(s_, tag, c, k, n, buf):
            s_.wait_ge(S_(f"{tag[0]}_var"), c + (tag[1] + 1))
            s_.activation(dstat[0:n, k, 2], dstat[0:n, k, 1], ACT.Sqrt, bias=eps_c[0:n, :], scale=1.0 / F).then_inc(S_(f"{tag[0]}_std"), 1)

        def dense_sp(sp, tag, src, dst):
            t_ = tag

            def load(c, k, j):
                if j is not None:
                    sp.wait_ge(S_(f"{t_[0]}_out{k}"), (j + t_[2]) * 16)
                if isinstance(c, int) and c >= DA:
                    sp.dma_start(dX[k][0:TAILP], dense_tail(src, c - DA)).then_inc(S_(f"{t_[0]}_in{k}"), 16)
                else:
                    sp.dma_start(dX[k], dense_rows(src, c)).then_inc(S_(f"{t_[0]}_in{k}"), 16)

            def store(c, k):
                sp.wait_ge(S_(f"{t_[0]}_done"), c + (t_[1] + 1))
                if isinstance(c, int) and c >= DA:
                    sp.dma_start(dense_tail(dst, c - DA), dX[k][0:TAILP]).then_inc(S_(f"{t_[0]}_out{k}"), 16)
                else:
                    sp.dma_start(dense_rows(dst, c), dX[k]).then_inc(S_(f"{t_[0]}_out{k}"), 16)

            for c in range(3):
                load(c, c, None)
            turns = (DA - 3) // 3
            with sp.Fori(0, turns) as j:
                for k in range(3):
                    store(j * 3 + k, k)
                    load(j * 3 + k + 3, k, j + 1)
            for c in range(3 * turns, DA + 2):
                store(c, c % 3)
                if c + 3 < DA + 2:
                    load(c + 3, c % 3, c // 3 + 1)
            for k in range(3):
                sp.wait_ge(S_(f"{t_[0]}_out{k}"), 16 * (dense_stores(k) + t_[2]))

        def dense_dve(v, tag):
            t_, parts = tag, lambda c: P if not isinstance(c, int) or c < DA else TAILP
            dense_first(v, t_, 0, 0, P, 0, dBuf)
            dense_first(v, t_, 1, 1, P, 0, dBuf)
            dense_second(v, t_, 0, 0, P, dBuf)
            turns = (DA - 2) // 3
            with v.Fori(0, turns) as j:
                for k in range(3):
                    c, slot = j * 3 + k + 2, (k + 2) % 3
                    dense_third(v, t_, j * 3 + k, (slot + 1) % 3, P, dBuf)
                    dense_first(v, t_, c, slot, P, j + (k + 2) // 3, dBuf)
                    dense_second(v, t_, j * 3 + k + 1, (slot + 2) % 3, P, dBuf)
            for c in range(3 * turns + 2, DA + 4):
                dense_third(v, t_, c - 2, (c - 2) % 3, parts(c - 2), dBuf)
                if c < DA + 2:
                    dense_first(v, t_, c, c % 3, parts(c), c // 3, dBuf)
                if c - 1 < DA + 2:
                    dense_second(v, t_, c - 1, (c - 1) % 3, parts(c - 1), dBuf)

        def dense_act(s_, tag):
            t_, parts = tag, lambda c: P if not isinstance(c, int) or c < DA else TAILP
            dense_square(s_, t_, 0, 0, P, dBuf)
            turns = (DA - 1) // 3
            with s_.Fori(0, turns) as j:
                for k in range(3):
                    dense_square(s_, t_, j * 3 + k + 1, (k + 1) % 3, P, dBuf)
                    dense_root(s_, t_, j * 3 + k, k, P, dBuf)
            for c in range(3 * turns, DA + 2):
                if c + 1 < DA + 2:
                    dense_square(s_, t_, c + 1, (c + 1) % 3, parts(c + 1), dBuf)
                dense_root(s_, t_, c, c % 3, parts(c), dBuf)

        def dense_in_loop_sp(sp, tag, src, dst, buf, others=()):
            def load(c, b, j):
                if not early(c):
                    sp.wait_ge(S_(f"{tag[0]}_out{b}"), (j + tag[2]) * 16)
                sp.dma_start(buf[b][0], dense_rows(src, c + DA)).then_inc(S_(f"{tag[0]}_in{b}"), 16)

            def store(c, b, j):
                sp.wait_ge(S_(f"{tag[0]}_done"), c + (tag[1] + 1))
                sp.dma_start(dense_rows(dst, c + DA), buf[b][0]).then_inc(S_(f"{tag[0]}_out{b}"), 16)
            pipelined(sp, [(0, load), (1, store), *others])

        def gather_pair(g, top, tag, table, free):
            def step(c, b, j):
                g.wait_ge(S_(f"{tag}_free{b}"), j + 1)
                g.sem_inc(S_("turn"), 1)
                for k in range(C):
                    for d in range(2):
                        g.indirect_dma_start(G[:, b, k, d, :], None, table,
                                             bass.IndirectOffsetOnAxis(ap=idx_s[:, b, d, k:k + 1], axis=0),
                                             bounds_check=top, oob_is_err=False).then_inc(S_(f"{tag}_in{b}"), 16)
            pipelined(g, [(0, step)])

        def stage_indices(v, tag, idx, c, b):
            for d, ix in enumerate(idx[:-1]):
                v.tensor_copy(idx_s[:, b, d, :], ix[:, tiles(c)])
            v.tensor_copy(idx_s[:, b, len(idx) - 1, :], idx[-1][:, tiles(c)]).then_inc(S_(f"{tag}_free{b}"), 1)

        def norm_dve(v, tag, c, b, j, dtag, buf):
            flat = lambda t_: t_[:, b].rearrange("p c d f -> p (c d) f")
            v.wait_ge(S_(f"{tag}_in{b}"), (j + 1) * (32 * C))
            v.tensor_reduce(stat[:, b, 0], flat(G), AX.X, ALU.add)
            v.drain()
            v.scalar_tensor_tensor(flat(XC), bc(stat[:, b, 0], F), -1.0 / F, flat(G), ALU.mult, ALU.add).then_inc(S_(f"{tag}_cen"), 1)
            if not (isinstance(c, int) and c == 0):
                dense_third(v, dtag, c + (-1), 1 - b, P, buf)
            v.wait_ge(S_(f"{tag}_sq"), c + 1)
            v.tensor_reduce(stat[:, b, 1], flat(SQ), AX.X, ALU.add).then_inc(S_(f"{tag}_var"), 1)
            dense_first(v, dtag, c, b, P, j, buf)
            v.wait_ge(S_(f"{tag}_std"), c + 1)
            v.reciprocal(stat[:, b, 2], stat[:, b, 2])
            v.drain()
            v.scalar_tensor_tensor(flat(XC), flat(XC), 0.0, bc(stat[:, b, 2], F), ALU.max, ALU.mult)
            v.drain()

        def norm_act(s_, tag, c, b, j, dtag, buf):
            if not (isinstance(c, int) and c == 0):
                dense_root(s_, dtag, c + (-1), 1 - b, P, buf)
            s_.wait_ge(S_(f"{tag}_cen"), c + 1)
            s_.activation(SQ[:, b], XC[:, b], ACT.Square).then_inc(S_(f"{tag}_sq"), 1)
            s_.wait_ge(S_(f"{tag}_var"), c + 1)
            s_.activation(stat[:, b, 2], stat[:, b, 1], ACT.Sqrt, bias=eps_c[:, :], scale=1.0 / F).then_inc(S_(f"{tag}_std"), 1)
            dense_square(s_, dtag, c, b, P, buf)

        def pairs(ap):
            return ap.rearrange("p c f -> p (c f)")

        def build_S_sp(sp, tag, o):
            def step(c, b, j):
                if not early(c):
                    sp.wait_ge(S_(f"{tag}_made{b}"), j)
                off = 128 + c * 512
                src = node_d[o:o + 1, off:off + 512] if isinstance(c, int) else node_d[o:o + 1, ds(off, 512)]
                sp.dma_start(NB[b].rearrange("p t e -> p (t e)"), src.broadcast_to([P, 512])).then_inc(S_(f"{tag}_ids{b}"), 16)
            pipelined(sp, [(0, step)])

        def build_S_dve(v, tag, o):
            def step(c, b, j):
                v.wait_ge(S_(f"{tag}_ids{b}"), (j + 1) * 16)
                v.tensor_tensor(S[:, tiles(c), :], NB[b], bc(node[o][:, tiles(c)], P), ALU.is_equal).then_inc(S_(f"{tag}_made{b}"), 1)
            pipelined(v, [(0, step)])
            v.drain()
            v.tensor_copy(SE[:, :, :], S[:, :, TE:])
            v.drain().then_inc(S_(f"{tag}_S"), 1)

        def carry_dve(v, tag, i=0):
            nl, fu = FLB[0][:, 0, :], FLB[0][:, 1, :]
            m = T - 1
            v.wait_ge(S_(f"{tag}_fl_c"), NCH * (i + 1))
            v.tensor_tensor(AF, nl, fu, ALU.mult)
            v.tensor_tensor(AB[:, 0:m], nl[:, 0:m], fu[:, 1:T], ALU.mult)
            v.tensor_tensor(BF_[:, 0:m], nl[:, 0:m], FLS[:, 0:m, 1], ALU.mult)
            v.tensor_tensor(BB[:, 0:m], nl[:, 0:m], FLS[:, 1:T, 0], ALU.mult)
            v.memset(CF[:, :, :], 0.0)
            v.drain()
            v.tensor_tensor_scan(CF[:, 0, 1:T], AF[:, 0:m], BF_[:, 0:m], 0.0, ALU.mult, ALU.add)
            v.tensor_tensor_scan(CF[:, 1, 0:m][:, ::-1], AB[:, 0:m][:, ::-1], BB[:, 0:m][:, ::-1], 0.0, ALU.mult, ALU.add)
            v.drain().then_inc(S_(f"{tag}_carry"), 1)
            v.wait_ge(S_(f"{tag}_carry_t"), i + 1)
            v.tensor_copy(CT.rearrange("r q f -> r (q f)"), bank[0][0:HT, 0:256]).then_inc(S_(f"{tag}_carry"), 1)

        def carry_pe(pe, tag, i=0):
            pe.wait_ge(S_(f"{tag}_carry"), 2 * i + 1)
            for q in range(4):
                ins = pe.transpose(bank[0][0:HT, q * F:(q + 1) * F], CF[:, q // 2, (q % 2) * HT:(q % 2 + 1) * HT], ident[0:F, 0:F])
            ins.then_inc(S_(f"{tag}_carry_t"), 1)

        def carry_sp(sp, tag, big, i=0):
            sp.wait_ge(S_(f"{tag}_carry"), 2 * i + 2)
            for q in range(4):
                sp.dma_start(big[CARRY + q // 2:CARRY + q // 2 + 1, (q % 2) * HT:(q % 2 + 1) * HT, :].rearrange("o t f -> o (t f)"),
                             CT[:, q, :]).then_inc(S_(f"{tag}_carried"), 16)

        def L0_sp(sp):
            sp.wait_ge(S_("sm_lg"), 1)
            for h in range(H8):
                rows = slice(h * HC, (h + 1) * HC)
                sp.dma_start(IDS[rows, 1:SCAN + 1].rearrange("c (k e) -> c k e", k=KC),
                             at(node_d, 128, [[KC * 128, HC], [128, KC], [1, TE]])).then_inc(S_("scan_ids"), 16)
                sp.dma_start(IDS[rows, 0:1], at(node_d, TE - 1, [[KC * 128, HC], [1, 1]])).then_inc(S_("scan_ids"), 16)
                sp.dma_start(IDS[rows, SCAN + 1:SCAN + 2], at(node_d, 128 + KC * 128, [[KC * 128, HC], [1, 1]])).then_inc(S_("scan_ids"), 16)
            for n_ in range(2):
                sp.wait_ge(S_("ends_up"), n_ + 1)
                sp.dma_start(crow[0:1, 0:320], ccol[0:64, 0:5]).then_inc(S_("ends_row"), 16)
                sp.wait_ge(S_("carry_row"), n_ + 1)
                sp.dma_start(ccol[0:64, 5:7], carr[0:1, 0:128]).then_inc(S_("carry_col"), 16)
            sp.dma_start(FLB[0][:, :, :], at(flag_d, 0, [[0, F], [1, 2 * T]])).then_inc(S_("flags"), 16)
            sp.wait_ge(S_("alpha_out"), 4)
            build_S_sp(sp, "s0", 0)
            carry_sp(sp, "m", big1)

        def L0_pool(g, top):
            def step(c, b, j):
                g.wait_ge(S_("n_rows"), c + 1)
                g.sem_inc(S_("turn"), 1)
                for k in range(C):
                    g.indirect_dma_start(x1_d, bass.IndirectOffsetOnAxis(ap=idx_s[:, b, 0, k:k + 1], axis=0), G[:, b, k, 0, :], None,
                                         bounds_check=top, oob_is_err=False).then_inc(S_(f"n_out{b}"), 16)
            pipelined(g, [(0, step)])
            for b in range(2):
                g.wait_ge(S_(f"n_out{b}"), 16 * C * (NCH // 2))
            g.sem_inc(S_("x1_fixed"), 1)

        def segment_ends(v, data, op0, op1, first, mask):
            v.tensor_tensor_scan(SP_, mask[:, 0:SCAN], data, first, op0, op1)
            v.tensor_tensor_scan(SQn[:, ::-1], mask[:, 1:SCAN + 1][:, ::-1], data[:, ::-1], first, op0, op1)
            v.drain()
            v.tensor_copy(ccol[0:64, 0:1], SP_[:, SCAN - 1:SCAN])
            v.tensor_copy(ccol[0:64, 1:2], SQn[:, 0:1]).then_inc(S_("ends_up"), 1)

        def row_carry(v, n_, is_max):
            R = crow[0:1, 0:320].rearrange("o (q k) -> o q k", k=5)
            last, frst, lp, ln_, full = [R[:, :, k] for k in range(5)]
            m = 63
            A_, B_ = carr[0:1, 128:192], carr[0:1, 192:256]
            A2_, B2_ = carr[0:1, 256:320], carr[0:1, 320:384]
            O = carr[0:1, 0:128].rearrange("o (q k) -> o q k", k=2)
            first = LOW if is_max else 0.0
            v.wait_ge(S_("ends_row"), 16 * (n_ + 1))
            v.memset(O, first)
            v.tensor_tensor(A_[:, 0:m], lp[:, 1:64], full[:, 0:m], ALU.mult)
            v.tensor_tensor(A2_[:, 0:m], ln_[:, 0:m], full[:, 1:64], ALU.mult)
            if is_max:
                v.tensor_scalar(B_[:, 0:m], lp[:, 1:64], -1.0, -LOW, ALU.add, ALU.mult)
                v.tensor_scalar(B2_[:, 0:m], ln_[:, 0:m], -1.0, -LOW, ALU.add, ALU.mult)
                v.drain()
                v.tensor_scalar(A_[:, 0:m], A_[:, 0:m], -1.0, -LOW, ALU.add, ALU.mult)
                v.tensor_scalar(A2_[:, 0:m], A2_[:, 0:m], -1.0, -LOW, ALU.add, ALU.mult)
                v.tensor_tensor(B_[:, 0:m], B_[:, 0:m], last[:, 0:m], ALU.add)
                v.tensor_tensor(B2_[:, 0:m], B2_[:, 0:m], frst[:, 1:64], ALU.add)
                op0, op1 = ALU.add, ALU.max
            else:
                v.tensor_tensor(B_[:, 0:m], lp[:, 1:64], last[:, 0:m], ALU.mult)
                v.tensor_tensor(B2_[:, 0:m], ln_[:, 0:m], frst[:, 1:64], ALU.mult)
                op0, op1 = ALU.mult, ALU.add
            v.drain()
            v.tensor_tensor_scan(O[:, 1:64, 0], A_[:, 0:m], B_[:, 0:m], first, op0, op1)
            v.tensor_tensor_scan(O[:, 0:m, 1][:, ::-1], A2_[:, 0:m][:, ::-1], B2_[:, 0:m][:, ::-1], first, op0, op1)
            v.drain().then_inc(S_("carry_row"), 1)
            v.wait_ge(S_("carry_col"), 16 * (n_ + 1))

        def L0_dve(v):
            v.wait_ge(S_("payload_in"), 1)
            v.wait_ge(S_("nodes_out"), 16 * 8)
            v.wait_ge(S_("weights_in"), 16 * 17)
            for k in range(3):
                v.wait_ge(S_(f"da_out{k}"), 16 * dense_stores(k))
            v.tensor_scalar(wneg[:, :], payg[:, :, 1], rscale[:, 0:1], -1.0, ALU.mult, ALU.mult)
            v.drain()
            idx = (own_i[0], far_i[0])
            for b in range(2):
                stage_indices(v, "g", idx, b, b)

            def step(c, b, j):
                norm_dve(v, "g", c, b, j, LOOP_A, dBuf)
                if not early(c):
                    v.wait_ge(S_("g_raw"), c - 1)
                v.tensor_tensor(VS[:, b], XC[:, b, :, 1, :], XC[:, b, :, 0, :], ALU.subtract).then_inc(S_("g_dl"), 1)
                v.tensor_tensor(big2[:, tiles(c), :], G[:, b, :, 0, :], XC[:, b, :, 0, :], ALU.add)
                v.drain()
                stage_indices(v, "g", idx, c + 2, b)
                dense_second(v, LOOP_A, c, b, P, dBuf)
            pipelined(v, [(0, step)])
            dense_third(v, LOOP_A, NCH - 1, 1, P, dBuf)
            for b in range(2):
                v.wait_ge(S_(f"dl_out{b}"), 16 * (NCH // 2))

            v.wait_ge(S_("g_raw"), NCH)
            LGc, LPv = LG.rearrange("p (c k) h -> p h k c", c=HC), LGP.rearrange("p (k h c) -> p h k c", k=KC, h=H8)
            wv = wneg[:, :].rearrange("p (c k) -> p k c", c=HC)
            for h in range(H8):
                if h < HEADS:
                    v.tensor_tensor(LPv[:, h], LGc[:, h], wv, ALU.add)
                else:
                    v.tensor_copy(LPv[:, h], LGc[:, h])
            v.drain().then_inc(S_("sm_lg"), 1)
            v.wait_ge(S_("scan_ids"), 16 * 24)
            v.tensor_tensor(SAME, IDS[:, 1:SCAN + 2], IDS[:, 0:SCAN + 1], ALU.is_equal)
            v.tensor_tensor(ccol[0:64, 4:5], IDS[:, 1:2], IDS[:, SCAN:SCAN + 1], ALU.is_equal)
            v.drain()
            v.tensor_scalar(NEG, SAME, -1.0, -LOW, ALU.add, ALU.mult)
            v.tensor_copy(ccol[0:64, 2:3], SAME[:, 0:1])
            v.tensor_copy(ccol[0:64, 3:4], SAME[:, SCAN:SCAN + 1])
            v.drain()
            v.wait_ge(S_("sm_in"), 7)
            segment_ends(v, SL, ALU.add, ALU.max, LOW, NEG)
            row_carry(v, 0, True)
            v.tensor_tensor_scan(SP_, NEG[:, 0:SCAN], SL, ccol[0:64, 5:6], ALU.add, ALU.max)
            v.drain()
            v.tensor_tensor_scan(SQn[:, ::-1], NEG[:, 1:SCAN + 1][:, ::-1], SP_[:, ::-1], ccol[0:64, 6:7], ALU.add, ALU.max)
            v.drain()
            v.tensor_tensor(SL, SL, SQn, ALU.subtract).then_inc(S_("sm_sub"), 1)
            v.memset(BT, 0.0)
            v.wait_ge(S_("sm_exp"), 1)
            segment_ends(v, SL, ALU.mult, ALU.add, 0.0, SAME)
            row_carry(v, 1, False)
            v.tensor_tensor_scan(SP_, SAME[:, 0:SCAN], SL, ccol[0:64, 5:6], ALU.mult, ALU.add)
            v.tensor_tensor_scan(SQn[:, ::-1], SAME[:, 1:SCAN + 1][:, ::-1], SL[:, ::-1], ccol[0:64, 6:7], ALU.mult, ALU.add)
            v.drain()
            v.tensor_tensor(SP_, SP_, SQn, ALU.add)
            v.drain()
            v.tensor_tensor(SP_, SP_, SL, ALU.subtract)
            v.drain()
            v.reciprocal(SP_, SP_)
            v.drain()
            v.tensor_tensor(SL, SL, SP_, ALU.mult).then_inc(S_("sm_alpha"), 1)
            BTv = BT.rearrange("p (c k) h -> p k h c", c=HC)
            for q in range(4):
                n_ = min(8, KC - 8 * q)
                v.wait_ge(S_("sm_back"), q + 1)
                B = bank[4 + q % 2][0:TE, 0:n_ * 64].rearrange("p (k r h c) -> p k r h c", r=2, h=HEADS, c=HC)
                for k in range(n_):
                    v.tensor_copy(BTv[0:TE, 8 * q + k], B[:, k, 0])
                v.drain()
                for k in range(n_):
                    ins = v.tensor_tensor(BTv[0:TE, 8 * q + k], BTv[0:TE, 8 * q + k], B[:, k, 1], ALU.add)
                ins.then_inc(S_("alpha_out"), 1)
            v.drain()
            build_S_dve(v, "s0", 0)

            def weigh(c, b, j):
                if not early(c):
                    v.wait_ge(S_("m_tp"), c - 1)
                v.tensor_tensor(Zs[b], big1[:, tiles(c), :].unsqueeze(2).broadcast_to([P, C, HEADS, F]),
                                bc(BT[:, tiles(c), :], F), ALU.mult).then_inc(S_("m_z"), 1)
            pipelined(v, [(0, weigh)])
            v.wait_ge(S_("flags"), 16)
            carry_dve(v, "m")

            def guard(c, b, j):
                v.wait_ge(S_("n_sum"), c + 1)
                x_ = bank[b][:, 0:C * F]
                hi, lo = pairs(VS[:, b]), pairs(XC[:, b, :, 0, :].rearrange("p c f -> p c f")) if False else SQ[:, b].rearrange("p c d f -> p (c d f)")[:, 0:C * F]
                v.tensor_scalar(hi, x_, 0.0, HUGE, ALU.max, ALU.min)
                v.tensor_scalar(lo, x_, 0.0, -HUGE, ALU.min, ALU.max)
                v.drain()
                v.tensor_tensor(hi, hi, lo, ALU.add).then_inc(S_("n_safe"), 1)

            def renew(c, b, j):
                v.wait_ge(S_("n_proj"), c + 1)
                if not early(c):
                    v.wait_ge(S_(f"n_out{b}"), j * (16 * C))
                v.tensor_tensor(G[:, b, :, 0, :], bank[4 + b][:, 0:C * F].rearrange("p (c f) -> p c f", f=F), big2[:, tiles(c), :], ALU.add)
                v.tensor_copy(idx_s[:, b, 0, :], scat_i[0][:, tiles(c)])
                v.drain().then_inc(S_("n_rows"), 1)
            pipelined(v, [(0, guard), (2, renew)])

        def L0_act(s_):
            def step(c, b, j):
                norm_act(s_, "g", c, b, j, LOOP_A, dBuf)
                s_.wait_ge(S_("g_tp"), c + 1)
                s_.activation(pairs(TS[:, b]), bank[b][:, 0:C * F], ACT.Copy).then_inc(S_("g_dt"), 1)
                s_.activation(big1[:, tiles(c), :], VS[:, b], ACT.Copy)
                s_.wait_ge(S_("g_lg"), c + 1)
                s_.sem_inc(S_("turn"), 1)
                s_.activation(LG[:, tiles(c), :], bank[2 + b][:, 0:C * H8].rearrange("p (c h) -> p c h", h=H8), ACT.Copy).then_inc(S_("g_raw"), 1)
            s_.wait_ge(S_("scores_c"), 2)
            pipelined(s_, [(0, step)])
            dense_root(s_, LOOP_A, NCH - 1, 1, P, dBuf)
            SLk = SL.rearrange("q (k e) -> q k e", e=TE)
            for q in range(7):
                n_ = min(4, KC - 4 * q)
                s_.wait_ge(S_("sm_t"), q + 1)
                s_.activation(SLk[:, 4 * q:4 * q + n_, :], bank[q % 2][0:64, 0:n_ * P].rearrange("q (k e) -> q k e", e=P)[:, :, 0:TE], ACT.Copy).then_inc(S_("sm_in"), 1)
            s_.wait_ge(S_("sm_sub"), 1)
            s_.activation(SL, SL, ACT.Exp).then_inc(S_("sm_exp"), 1)

            def out_t(c, b, j):
                s_.wait_ge(S_("m_tp"), c + 1)
                s_.activation(ZTs[b][:, 0:512], bank[2 * b][:, :], ACT.Copy)
                s_.activation(ZTs[b][:, 512:1024], bank[2 * b + 1][:, :], ACT.Copy).then_inc(S_("m_ev"), 1)

            def out_v(c, b, j):
                s_.wait_ge(S_("m_mm"), c + 1)
                s_.activation(pairs(VS[:, b]), bank[4 + b][:, 0:C * F], ACT.Copy, scale=1.0 / HEADS).then_inc(S_("m_v"), 1)
                s_.activation(big1[:, tiles(c), :], bank[4 + b][:, 0:C * F].rearrange("p (c f) -> p c f", f=F), ACT.Copy, scale=1.0 / HEADS)

            pipelined(s_, [(0, out_t), (1, out_v), (2, lambda c, b, j: ends_act(s_, "m", c, b, j))])

            def widen(c, b, j):
                if not early(c):
                    s_.wait_ge(S_("n_sum"), c - 1)
                    s_.sem_inc(S_("turn"), 1)
                s_.activation(STg[b], S[:, tiles(c), :], ACT.Copy).then_inc(S_("n_st"), 1)

            def out_g(c, b, j):
                s_.wait_ge(S_("n_tp"), c + 1)
                s_.activation(pairs(TS[:, b]), bank[2 + b][:, 0:C * F], ACT.Copy).then_inc(S_("n_gt"), 1)
            s_.wait_ge(S_("m_carry_t"), 1)
            pipelined(s_, [(0, widen), (1, out_g)])

        def ends_act(s_, tag, c, b, j, base=0):
            s_.wait_ge(S_(f"{tag}_fl"), c + (base + 1))
            s_.sem_inc(S_("turn"), 1)
            s_.activation(FLS[:, tiles(c), :], bank[6 + b][0:F, 0:2 * C].rearrange("f (c k) -> f c k", k=2), ACT.Copy).then_inc(S_(f"{tag}_fl_c"), 1)

        def ends_pe(pe, tag, ready, c, b, j, base=0, base2=0):
            pe.wait_ge(S_(ready), c + (base + 1))
            if not early(c):
                pe.wait_ge(S_(f"{tag}_fl_c"), c + (base2 - 1))
            pe.sem_inc(S_("turn"), 1)
            for k in range(C):
                ins = pe.matmul(bank[6 + b][0:F, 2 * k:2 * k + 2], VS[:, b, k, :], SE[:, one(c, k), :].rearrange("p o k -> p (o k)"), start=True, stop=True)
            ins.then_inc(S_(f"{tag}_fl"), 1)

        def L0_pe(pe):
            def turn(c, b, j):
                pe.wait_ge(S_("g_dl"), c + 1)
                for q in range(C // 2):
                    ins = pe.transpose(bank[b][:, q * P:(q + 1) * P], pairs(VS[:, b, 2 * q:2 * q + 2, :]), ident[:, :])
                ins.then_inc(S_("g_tp"), 1)
                pe.wait_ge(S_("g_dt"), c + 1)
                for q in range(C // 2):
                    ins = pe.matmul(bank[2 + b][:, q * 2 * H8:(q + 1) * 2 * H8], pairs(TS[:, b, 2 * q:2 * q + 2, :]), A2[:, :], start=True, stop=True)
                ins.then_inc(S_("g_lg"), 1)
            pe.wait_ge(S_("scores_c"), 2)
            pipelined(pe, [(0, turn)])
            pe.wait_ge(S_("sm_lg"), 1)
            for k in range(KC):
                q = k // 4
                if q >= 2 and k % 4 == 0:
                    pe.wait_ge(S_("sm_in"), q - 1)
                ins = pe.transpose(bank[q % 2][0:64, (k % 4) * P:(k % 4 + 1) * P], LGP[:, k * 64:(k + 1) * 64], ident[:, :])
                if k % 4 == 3 or k == KC - 1:
                    ins.then_inc(S_("sm_t"), 1)
            pe.wait_ge(S_("sm_alpha"), 1)
            SLk = SL.rearrange("q (k e) -> q k e", e=TE)
            for k in range(KC):
                q = k // 8
                if q >= 2 and k % 8 == 0:
                    pe.wait_ge(S_("alpha_out"), q - 1)
                ins = pe.transpose(bank[4 + q % 2][0:TE, (k % 8) * 64:(k % 8 + 1) * 64], SLk[:, k, :], ident[0:64, 0:64])
                if k % 8 == 7 or k == KC - 1:
                    ins.then_inc(S_("sm_back"), 1)

            def turn_z(c, b, j):
                pe.wait_ge(S_("m_z"), c + 1)
                for q in range(2):
                    for k in range(C):
                        ins = pe.transpose(bank[2 * b + q][:, k * P:(k + 1) * P], Zs[b][:, k, 2 * q:2 * q + 2, :].rearrange("p h f -> p (h f)"), ident[:, :])
                ins.then_inc(S_("m_tp"), 1)

            def project(c, b, j):
                pe.wait_ge(S_("m_ev"), c + 1)
                for k in range(C):
                    for q in range(2):
                        ins = pe.matmul(bank[4 + b][:, k * F:(k + 1) * F], ZTs[b][:, q * 512 + k * P:q * 512 + (k + 1) * P], wm[:, q, :],
                                        start=(q == 0), stop=(q == 1))
                ins.then_inc(S_("m_mm"), 1)
            pe.wait_ge(S_("s0_S"), 1)
            pipelined(pe, [(0, turn_z), (1, project), (2, lambda c, b, j: ends_pe(pe, "m", "m_v", c, b, j))])
            carry_pe(pe, "m")

            def total(c, b, j):
                pe.wait_ge(S_("n_st"), c + 1)
                for k in range(C):
                    ins = pe.matmul(bank[b][:, k * F:(k + 1) * F], STg[b][:, k, :], big1[:, one(c, k), :].rearrange("p o f -> p (o f)"), start=True, stop=True)
                ins.then_inc(S_("n_sum"), 1)

            def turn_g(c, b, j):
                pe.wait_ge(S_("n_safe"), c + 1)
                for q in range(C // 2):
                    ins = pe.transpose(bank[2 + b][:, q * P:(q + 1) * P], pairs(VS[:, b, 2 * q:2 * q + 2, :]), ident[:, :])
                ins.then_inc(S_("n_tp"), 1)

            def out_proj(c, b, j):
                pe.wait_ge(S_("n_gt"), c + 1)
                if not early(c):
                    pe.wait_ge(S_("n_rows"), c - 1)
                for q in range(C // 2):
                    ins = pe.matmul(bank[4 + b][:, q * P:(q + 1) * P], pairs(TS[:, b, 2 * q:2 * q + 2, :]), wo[:, :], start=True, stop=True)
                ins.then_inc(S_("n_proj"), 1)
            pe.wait_ge(S_("m_carried"), 16 * 4)
            pipelined(pe, [(0, total), (1, turn_g), (2, out_proj)])


        def rows_of(ap, c):
            return ap[0:SLOTS, :].rearrange("(t e) f -> e t f", e=TE)[:, tiles(c), :]

        def L1_pool(g, top, narrow):
            gather_pair(g, top, "h", x1_d, None)
            g.iota(steps_i, [[1, DEG]], base=0, channel_multiplier=0)
            g.drain()
            g.tensor_copy(steps, steps_i)
            narrow(3 * T // 2, far_i[1], small_v1, gather_from=pos_d, into=pos_i)
            g.sem_inc(S_("pos_in"), 1)
            g.wait_ge(S_("pos_split"), 1)
            for l in range(LAYERS):
                if l:
                    def step(c, b, j, l=l):
                        g.wait_ge(S_(f"h_free{b}"), j + (26 * l + 1))
                        g.sem_inc(S_("turn"), 1)
                        for k in range(C):
                            g.indirect_dma_start(G[:, b, k, 1, :], None, xt_d[l - 1],
                                                 bass.IndirectOffsetOnAxis(ap=idx_s[:, b, 0, k:k + 1], axis=0),
                                                 bounds_check=top, oob_is_err=False).then_inc(S_(f"h_in{b}"), 16)
                    pipelined(g, [(0, step)])
                g.wait_ge(S_("r_stored"), 16 * (l + 1))
                narrow(4 * T // 2 + l * BY_DMA // 2, pos_i, small_v1, gather_from=dt_d[l],
                       into=DCc[:, :].unsqueeze(2), units=BY_DMA // DSMALL, size=DSMALL)
                g.sem_inc(S_("deg_done"), 1)

            def last(c, b, j):
                g.wait_ge(S_("q2_fin"), c + 1)
                g.sem_inc(S_("turn"), 1)
                for k in range(C):
                    g.indirect_dma_start(out, bass.IndirectOffsetOnAxis(ap=idx_s[:, b, 0, k:k + 1], axis=0), G[:, b, k, 0, :], None,
                                         bounds_check=top, oob_is_err=False).then_inc(S_(f"f_out{b}"), 16)
            pipelined(g, [(0, last)])
            for b in range(2):
                g.wait_ge(S_(f"f_out{b}"), 16 * C * (NCH // 2))

        def L1_sp(sp):
            sp.wait_ge(S_("n_rows"), NCH)
            sp.dma_start(FLB[0][:, :, :], at(flag_d, 2 * T, [[0, F], [1, 2 * T]])).then_inc(S_("flags"), 16)

            def near_ids(c, b, j):
                if not early(c):
                    sp.wait_ge(S_("s1_made"), c - 1)
                off = 128 + c * 512
                src = node_d[1:2, off:off + 512] if isinstance(c, int) else node_d[1:2, ds(off, 512)]
                sp.dma_start(NBL[b].rearrange("p t e -> p (t e)"), src.broadcast_to([P, 512])).then_inc(S_(f"s1_ids{b}"), 16)

            def store_base(c, b, j):
                sp.wait_ge(S_("h_base"), c + 1)
                sp.dma_start(rows_of(base_d, c), VS[0:TE, b]).then_inc(S_(f"h_stored{b}"), 16)
            sp.wait_ge(S_("x1_fixed"), 1)
            dense_in_loop_sp(sp, LOOP_B, x1_d, out, bBuf, [(0, near_ids), (1, store_base)])
            for l in range(LAYERS):
                sp.wait_ge(S_("r_ends"), l + 1)
                for h in range(2):
                    sp.dma_start(crow[0:1, h * T:(h + 1) * T], ccol[0:HT, 2 * h:2 * h + 2]).then_inc(S_("r_row"), 16)
                sp.wait_ge(S_("r_carry"), l + 1)
                for h in range(2):
                    sp.dma_start(ccol[0:HT, 4 + 2 * h:6 + 2 * h], carr[0:1, h * T:(h + 1) * T]).then_inc(S_("r_col"), 16)
                sp.wait_ge(S_("r_d"), l + 1)
                sp.dma_start(at(dt_d[l], 0, [[TE, HT], [HT * TE, 2], [1, TE]]), PB_).then_inc(S_("r_stored"), 16)
                sp.wait_ge(S_("r_stored"), 16 * (l + 1))
                if l == 0:
                    sp.wait_ge(S_("r_val"), 1)
                    sp.wait_ge(S_("x1_fixed"), 1)
                    dense_sp(sp, RUN_B, x1_d, out)
                    sp.wait_ge(S_("pos_split"), 2)
                    sp.dma_start(at(row_d, 0, [[P, HT], [HT * P, 2], [1, P]]), ER).then_inc(S_("flags"), 16)
                    sp.wait_ge(S_("flags"), 48)

                def spread(c, b, j, l=l):
                    if not early(c):
                        sp.wait_ge(S_("o_hot"), c + (l * NLK - 1))
                    off = c * (C * P) + BY_DMA * P
                    src = row_d[:, off:off + C * P] if isinstance(c, int) else row_d[:, ds(off, C * P)]
                    sp.dma_start(RB[b], src.broadcast_to([P, C * P])).then_inc(S_(f"o_ids{b}"), 16)
                pipelined(sp, [(0, spread)], NLK)
                carry_sp(sp, "m", big1, l + 1)
                if l < 2:
                    def store(c, b, j, l=l):
                        sp.wait_ge(S_("q_out"), c + (l * NCH + 1))
                        sp.dma_start(rows_of(xt_d[l], c), TS[0:TE, b]).then_inc(S_(f"q_stored{b}"), 16)
                    pipelined(sp, [(0, store)])
                    for b in range(2):
                        sp.wait_ge(S_(f"q_stored{b}"), 16 * (NCH // 2) * (l + 1))
                    sp.sem_inc(S_("table"), 1)
                else:
                    for b in range(2):
                        sp.wait_ge(S_(f"h_stored{b}"), 16 * (NCH // 2))

                    def load(c, b, j):
                        if not early(c):
                            sp.wait_ge(S_("q2_fin"), c - 1)
                        for n_, t_ in enumerate((base_d, xt_d[0], xt_d[1])):
                            sp.dma_start(LR[b][0:TE, n_], rows_of(t_, c)).then_inc(S_(f"q2_ld{b}"), 16)
                    pipelined(sp, [(0, load)])

        def L1_dve(v):
            v.wait_ge(S_("x1_fixed"), 1)
            idx = (own_i[1], far_i[1])
            for b in range(2):
                stage_indices(v, "h", idx, b, b)
            def step0(c, b, j, l=0):
                if not early(c):
                    v.wait_ge(S_("h_t"), c + (l * NCH - 1))
                    v.wait_ge(S_("h_cc"), c + (l * NCH - 1))
                norm_dve(v, "h", c, b, j, LOOP_B, bBuf)
                if not early(c):
                    v.wait_ge(S_(f"h_stored{b}"), j * 16)
                v.tensor_tensor(VS[:, b], G[:, b, :, 0, :], XC[:, b, :, 0, :], ALU.add).then_inc(S_("h_base"), 1)
                v.drain().then_inc(S_("h_xc"), 1)
                stage_indices(v, "h", idx, c + 2, b)
                dense_second(v, LOOP_B, c, b, P, bBuf)
                v.wait_ge(S_(f"s1_ids{b}"), (j + 1) * 16)
                v.tensor_tensor(S[:, tiles(c), :], NBL[b], bc(node[1][:, tiles(c)], P), ALU.is_equal).then_inc(S_("s1_made"), 1)
            pipelined(v, [(0, step0)])
            dense_third(v, LOOP_B, NCH - 1, 1, P, bBuf)
            v.drain()
            v.tensor_copy(SE[:, :, :], S[:, :, TE:])
            v.drain().then_inc(S_("s1_S"), 1)
            for b in range(2):
                v.wait_ge(S_(f"dl_out{b}"), 16 * NCH)

            for l in range(LAYERS):
                if l:
                    v.wait_ge(S_("table"), l)
                    for b in range(2):
                        stage_indices(v, "h", (pos_i,), b, b)

                    def step(c, b, j, l=l):
                        v.wait_ge(S_(f"h_in{b}"), (j + (25 * (l + 1) + 1)) * (16 * C))
                        v.tensor_copy(G[:, b, :, 0, :], big2[:, tiles(c), :]).then_inc(S_("h_xc"), 1)

                    def refill(c, b, j, l=l):
                        v.wait_ge(S_("h_t"), c + (l * NCH + 1))
                        v.wait_ge(S_("h_cc"), c + (l * NCH + 1))
                        stage_indices(v, "h", (pos_i,), c + 2, b)
                    pipelined(v, [(0, step), (1, refill)])
                rowsum_dve(v, l)
                if l == 0:
                    dense_dve(v, RUN_B)
                    for k in range(3):
                        v.wait_ge(S_(f"da_out{k}"), 32 * dense_stores(k))
                    v.wait_ge(S_("pos_in"), 1)
                    v.tensor_scalar(QI[0], pos_i[:, 0:T], 7, None, ALU.logical_shift_right)
                    v.tensor_scalar(QI[1], pos_i[:, 0:T], P - 1, None, ALU.bitwise_and)
                    v.tensor_copy(RES[0], pos_i[:, 0:T])
                    v.drain()
                    v.tensor_copy(tile_far[:, :], QI[0])
                    v.tensor_copy(RES[1], QI[1])
                    v.drain()
                    v.scalar_tensor_tensor(pos_i[:, 0:T], tile_far[:, :], float(TE - P), RES[0], ALU.mult, ALU.add)
                    v.drain().then_inc(S_("pos_split"), 1)
                    v.wait_ge(S_("tiles_turned"), 2)
                    v.tensor_copy(ER, bank[0][0:HT, 256:512].rearrange("r (q j) -> r q j", q=2))
                    v.drain().then_inc(S_("pos_split"), 1)
                lookup_dve(v, l)
                v.wait_ge(S_("deg_done"), l + 1)
                v.tensor_tensor(VAL0[:, :], VAL0[:, :], DCc[:, :], ALU.mult)
                v.drain()
                v.tensor_scalar(VAL1[:, :], VAL0[:, :], em[:, 0:1], None, ALU.add)
                v.drain()

                def value(tag, V_, done, sig, more=0):
                    def fn(c, b, j, l=l):
                        if not early(c):
                            v.wait_ge(S_(done), c + (l * NCH + more - 1))
                        v.tensor_tensor(VS[:, b], big1[:, tiles(c), :], bc(V_[:, tiles(c)], F), ALU.mult).then_inc(S_(sig), 1)
                    return fn
                pipelined(v, [(0, value("p", VAL0, "m_fl", "p_v", NCH))])
                carry_dve(v, "m", l + 1)
                v.wait_ge(S_("m_carried"), 64 * (l + 2))
                stages = [(0, value("q", VAL1, "q_sum", "q_v"))]
                if l == 2:
                    def final(c, b, j, l=l):
                        v.wait_ge(S_(f"q2_ld{b}"), (j + 1) * 48)
                        v.tensor_tensor(LR[b][0:TE, 1], LR[b][0:TE, 1], LR[b][0:TE, 2], ALU.add)
                        v.wait_ge(S_("q_sum"), c + (l * NCH + 1))
                        if not early(c):
                            v.wait_ge(S_(f"f_out{b}"), j * (16 * C))
                        v.tensor_tensor(G[0:TE, b, :, 0, :], bank[b][0:TE, 0:C * F].rearrange("p (c f) -> p c f", f=F), LR[b][0:TE, 0], ALU.add)
                        v.drain()
                        v.tensor_tensor(G[0:TE, b, :, 0, :], G[0:TE, b, :, 0, :], LR[b][0:TE, 1], ALU.add)
                        v.tensor_copy(idx_s[:, b, 0, :], scat_i[1][:, tiles(c)])
                        v.drain().then_inc(S_("q2_fin"), 1)
                    stages.append((1, final))
                pipelined(v, stages)

        def lookup_dve(v, l):
            v.memset(DG[:, :, :], 0.0)
            v.drain()
            v.tensor_copy(DG[0:TE, 0, 0:T], bank[1][0:TE, 0:T])
            v.memset(DG[0:1, 0, T:DEG], 10.0)
            v.drain()
            v.tensor_tensor(RES[0][0:TE], bank[1][0:TE, 0:T], DG[0:TE, 0, 0:T], ALU.subtract)
            v.drain()
            v.tensor_copy(DG[0:TE, 1, 0:T], RES[0][0:TE])
            v.drain()
            v.tensor_tensor(RES[0][0:TE], RES[0][0:TE], DG[0:TE, 1, 0:T], ALU.subtract)
            v.drain()
            v.tensor_copy(DG[0:TE, 2, 0:T], RES[0][0:TE])
            v.drain()

            def hot(c, b, j):
                v.wait_ge(S_(f"o_ids{b}"), (j + (l * (NLK // 2) + 1)) * 16)
                v.tensor_scalar(OH[b], RB[b], pnum[:, 0:1], None, ALU.is_equal).then_inc(S_("o_hot"), 1)

            def select(c, b, j):
                v.wait_ge(S_("o_mm"), c + (l * NLK + 1))
                for k in range(C):
                    col = one(c, k + BY_DMA)
                    v.scalar_tensor_tensor(PICK[k], steps, tile_far[:, col], bank[2 + 2 * b + k // 2][:, (k % 2) * 256:(k % 2) * 256 + DEG],
                                                 ALU.is_equal, ALU.mult, accum_out=DCc[:, col])
                v.drain().then_inc(S_("o_sel"), 1)
            pipelined(v, [(0, hot), (1, select)], NLK)

        def lookup_pe(pe, l):
            def bring(c, b, j):
                pe.wait_ge(S_("o_hot"), c + (l * NLK + 1))
                if not early(c):
                    pe.wait_ge(S_("o_sel"), c + (l * NLK - 1))
                for k in range(C):
                    for part in range(3):
                        ins = pe.matmul(bank[2 + 2 * b + k // 2][:, (k % 2) * 256:(k % 2) * 256 + DEG], OH[b][0:TE, k * P:(k + 1) * P],
                                        DG[0:TE, part, 0:DEG], start=(part == 0), stop=(part == 2))
                ins.then_inc(S_("o_mm"), 1)
            pipelined(pe, [(0, bring)], NLK)

        def rowsum_dve(v, l):
            v.wait_ge(S_("r_sig"), l + 1)
            v.tensor_scalar(MSK[:, :], MSK[:, :], ZETA - GAMMA, GAMMA, ALU.mult, ALU.add)
            v.memset(VAL0[:, :], 0.0)
            v.drain()
            v.tensor_scalar(MSK[:, :], MSK[:, :], 0.0, 1.0, ALU.max, ALU.min).then_inc(S_("r_m"), 1)
            v.wait_ge(S_("r_t"), 2 * l + 1)
            v.tensor_copy(MT, bank[0][0:HT, 0:256].rearrange("r (h e) -> r h e", h=2)[:, :, 0:TE])
            v.drain()

            def both(i0, i1):
                for h in range(2):
                    v.tensor_tensor_scan(PF[:, h, :], smr[:, h, 0:TE], MT[:, h, :], i0[h], ALU.mult, ALU.add)
                    v.tensor_tensor_scan(PB_[:, h, ::-1], smr[:, h, 1:TE + 1][:, ::-1], MT[:, h, ::-1], i1[h], ALU.mult, ALU.add)
                v.drain()
            both((0.0, 0.0), (0.0, 0.0))
            for h in range(2):
                v.tensor_copy(ccol[0:HT, 2 * h:2 * h + 1], PF[:, h, TE - 1:TE])
                v.tensor_copy(ccol[0:HT, 2 * h + 1:2 * h + 2], PB_[:, h, 0:1])
            v.drain().then_inc(S_("r_ends"), 1)
            m = T - 1
            nl, fu = FLB[0][0:1, 0, :], FLB[0][0:1, 1, :]
            A_, B_, A2_, B2_ = [den[0:1, 800 + k * 200:800 + k * 200 + m] for k in range(4)]
            R = crow.rearrange("o (t k) -> o t k", k=2)
            O = carr.rearrange("o (t k) -> o t k", k=2)
            if l == 0:
                v.wait_ge(S_("flags"), 32)
            v.memset(carr, 0.0)
            v.tensor_tensor(A_, nl[:, 0:m], fu[:, 0:m], ALU.mult)
            v.tensor_tensor(A2_, nl[:, 0:m], fu[:, 1:T], ALU.mult)
            v.wait_ge(S_("r_row"), 32 * (l + 1))
            v.tensor_tensor(B_, nl[:, 0:m], R[:, 0:m, 0], ALU.mult)
            v.tensor_tensor(B2_, nl[:, 0:m], R[:, 1:T, 1], ALU.mult)
            v.drain()
            v.tensor_tensor_scan(O[:, 1:T, 0], A_, B_, 0.0, ALU.mult, ALU.add)
            v.tensor_tensor_scan(O[:, 0:m, 1][:, ::-1], A2_[:, ::-1], B2_[:, ::-1], 0.0, ALU.mult, ALU.add)
            v.drain().then_inc(S_("r_carry"), 1)
            v.wait_ge(S_("r_col"), 32 * (l + 1))
            both([ccol[0:HT, 4 + 2 * h:5 + 2 * h] for h in range(2)], [ccol[0:HT, 5 + 2 * h:6 + 2 * h] for h in range(2)])
            v.tensor_tensor(PF, PF, PB_, ALU.add)
            v.drain()
            v.tensor_tensor(PF, PF, MT, ALU.subtract).then_inc(S_("r_total"), 1)
            v.wait_ge(S_("r_root"), l + 1)
            v.reciprocal(PB_, PB_)
            v.drain()
            v.tensor_scalar(PB_, PB_, 10.0, None, ALU.min).then_inc(S_("r_d"), 1)
            v.wait_ge(S_("r_t"), 2 * l + 2)
            v.tensor_tensor(VAL0[0:TE, :], MSK[0:TE, :], bank[1][0:TE, 0:T], ALU.mult)
            v.drain().then_inc(S_("r_val"), 1)

        def L1_act(s_):
            for l in range(LAYERS):

                def fill(c, b, j, l=l):
                    if l == 0:
                        norm_act(s_, "h", c, b, j, LOOP_B, bBuf)
                    s_.wait_ge(S_("h_xc"), c + (l * NCH + 1))
                    s_.sem_inc(S_("turn"), 1)
                    s_.activation(big1[:, tiles(c), :], (XC if l == 0 else G)[:, b, :, 1, :], ACT.Copy).then_inc(S_("h_cc"), 1)
                    s_.wait_ge(S_("h_t"), c + (l * NCH + 1))
                    s_.activation(TT[b][0], bank[b][:, :], ACT.Copy).then_inc(S_("h_e1"), 1)

                def e2(c, b, j, l=l):
                    s_.wait_ge(S_("h_m1"), c + (l * NCH + 1))
                    s_.activation(TT[b][1], bank[2 + b][:, :], ACT.Relu, bias=bias1[:, l:l + 1]).then_inc(S_("h_e2"), 1)

                def e3(c, b, j, l=l):
                    s_.wait_ge(S_("h_m2"), c + (l * NCH + 1))
                    s_.activation(TT[b][2][0:F], bank[4 + b][0:F, :], ACT.Relu, bias=bias2[:, l:l + 1]).then_inc(S_("h_e3"), 1)

                def e4(c, b, j, l=l):
                    s_.wait_ge(S_("h_m3"), c + (l * NCH + 1))
                    s_.sem_inc(S_("turn"), 1)
                    s_.activation(MSK[:, tiles(c)], bank[6 + b][:, 0:C], ACT.Copy).then_inc(S_("h_e4"), 1)
                pipelined(s_, [(0, fill), (1, e2), (2, e3), (3, e4)])
                if l == 0:
                    dense_root(s_, LOOP_B, NCH - 1, 1, P, bBuf)
                s_.drain()
                s_.activation(MSK[:, :], MSK[:, :], ACT.Sigmoid, bias=bias3[:, l:l + 1]).then_inc(S_("r_sig"), 1)
                s_.wait_ge(S_("r_total"), l + 1)
                s_.activation(PB_, PF, ACT.Sqrt, bias=tiny_c[0:HT, :]).then_inc(S_("r_root"), 1)
                if l == 0:
                    dense_act(s_, RUN_B)
                pipelined(s_, [(0, lambda c, b, j, l=l: ends_act(s_, "m", c, b, j, (l + 1) * NCH))])

                def widen(c, b, j, l=l):
                    if not early(c):
                        s_.wait_ge(S_("q_sum"), c + (l * NCH - 1))
                        s_.sem_inc(S_("turn"), 1)
                    s_.activation(STg[b], S[:, tiles(c), :], ACT.Copy).then_inc(S_("q_st"), 1)

                def copy_out(c, b, j, l=l):
                    if not early(c):
                        s_.wait_ge(S_(f"q_stored{b}"), (j + 25 * l) * 16)
                    s_.wait_ge(S_("q_sum"), c + (l * NCH + 1))
                    s_.sem_inc(S_("turn"), 1)
                    s_.activation(pairs(TS[:, b]), bank[b][:, 0:C * F], ACT.Copy).then_inc(S_("q_out"), 1)
                    s_.activation(big2[:, tiles(c), :], bank[b][:, 0:C * F].rearrange("p (c f) -> p c f", f=F), ACT.Copy).then_inc(S_("q_b2"), 1)
                s_.wait_ge(S_("m_carry_t"), l + 2)
                pipelined(s_, [(0, widen)] + ([(1, copy_out)] if l < 2 else []))

        def L1_pe(pe):
            for l in range(LAYERS):

                def turn(c, b, j, l=l):
                    pe.wait_ge(S_("h_xc"), c + (l * NCH + 1))
                    for k in range(C):
                        ins = pe.transpose(bank[b][:, k * P:(k + 1) * P], (XC if l == 0 else G)[:, b, k].rearrange("p d f -> p (d f)"), ident[:, :])
                    ins.then_inc(S_("h_t"), 1)

                def m1(c, b, j, l=l):
                    pe.wait_ge(S_("h_e1"), c + (l * NCH + 1))
                    pe.matmul(bank[2 + b][:, :], wb[:, l, :], TT[b][0], start=True, stop=True).then_inc(S_("h_m1"), 1)

                def m2(c, b, j, l=l):
                    pe.wait_ge(S_("h_e2"), c + (l * NCH + 1))
                    pe.matmul(bank[4 + b][0:F, :], at1[:, l, :], TT[b][1], start=True, stop=True).then_inc(S_("h_m2"), 1)

                def m3(c, b, j, l=l):
                    pe.wait_ge(S_("h_e3"), c + (l * NCH + 1))
                    if not early(c):
                        pe.wait_ge(S_("h_e4"), c + (l * NCH - 1))
                    for k in range(C):
                        ins = pe.matmul(bank[6 + b][:, k:k + 1], TT[b][2][0:F, k * P:(k + 1) * P], at2[:, l:l + 1], start=True, stop=True)
                    ins.then_inc(S_("h_m3"), 1)
                if l:
                    pe.wait_ge(S_("q_b2"), l * NCH)
                pipelined(pe, [(0, turn), (1, m1), (2, m2), (3, m3)])
                pe.wait_ge(S_("r_m"), l + 1)
                for h in range(2):
                    ins = pe.transpose(bank[0][0:HT, h * P:(h + 1) * P], MSK[:, h * HT:(h + 1) * HT], ident[:, :])
                ins.then_inc(S_("r_t"), 1)
                pe.wait_ge(S_("r_d"), l + 1)
                for h in range(2):
                    ins = pe.transpose(bank[1][0:TE, h * HT:(h + 1) * HT], PB_[:, h, :], ident[0:HT, 0:HT])
                ins.then_inc(S_("r_t"), 1)
                if l == 0:
                    pe.wait_ge(S_("pos_split"), 1)
                    for h in range(2):
                        ins = pe.transpose(bank[0][0:HT, 256 + h * P:256 + (h + 1) * P], RES[1][:, h * HT:(h + 1) * HT], ident[:, :])
                    ins.then_inc(S_("tiles_turned"), 1)
                lookup_pe(pe, l)
                if l == 0:
                    pe.wait_ge(S_("s1_S"), 1)
                pipelined(pe, [(0, lambda c, b, j, l=l: ends_pe(pe, "m", "p_v", c, b, j, l * NCH, (l + 1) * NCH))])
                carry_pe(pe, "m", l + 1)

                def total(c, b, j, l=l):
                    pe.wait_ge(S_("q_v"), c + (l * NCH + 1))
                    if not early(c):
                        pe.wait_ge(S_("q2_fin" if l == 2 else "q_b2"), c + ((l * NCH if l < 2 else 0) - 1))
                    pe.wait_ge(S_("q_st"), c + (l * NCH + 1))
                    for k in range(C):
                        ins = pe.matmul(bank[b][:, k * F:(k + 1) * F], STg[b][:, k, :], VS[:, b, k, :], start=True, stop=True)
                    ins.then_inc(S_("q_sum"), 1)
                pipelined(pe, [(0, total)])

        @block.sync
        def _(sp):
            sp.wait_ge(S_("pads_set"), 1)
            full, part = E // SW, E % SW
            for o, name in enumerate(("dst", "src")):
                sp.dma_start(NI[0:full, o * SW:(o + 1) * SW], a[name][0:full * SW].rearrange("(p j) -> p j", j=SW)).then_inc(S_("ids_in"), 16)
                sp.dma_start(NI[full:full + 1, o * SW:o * SW + part], a[name][full * SW:E].rearrange("(p j) -> p j", p=1)).then_inc(S_("ids_in"), 16)
            sp.dma_start(EW[0:full, :], a["edge_weight"][0:full * SW].rearrange("(p j) -> p j", j=SW)).then_inc(S_("ids_in"), 16)
            sp.dma_start(EW[full:full + 1, 0:part], a["edge_weight"][full * SW:E].rearrange("(p j) -> p j", p=1)).then_inc(S_("ids_in"), 16)
            wi = S_("weights_in")
            wpj, wout = a["L0_gnn_w_proj"], a["L0_gnn_w_out"]
            for r in range(2):
                half = slice(r * F, (r + 1) * F)
                sp.dma_start(wp4[half], wpj.rearrange("h f g -> f h g")).then_inc(wi, 16)
                sp.dma_start(wm[half], wpj.rearrange("(q r) f g -> r f q g", r=2)[r]).then_inc(wi, 16)
                sp.dma_start(wo[half, half], wout).then_inc(wi, 16)
                sp.dma_start(wb[half, :, half], a[("L1_gnn_nb_W", "L1_gnn_self_W")[r]].rearrange("l i o -> i l o")).then_inc(wi, 16)
                sp.dma_start(bias1[half, :], a[("L1_gnn_nb_b", "L1_gnn_self_b")[r]].rearrange("l f -> f l"), allow_slow_non_contiguous=True).then_inc(wi, 16)
                sp.dma_start(rsT[:, r * HEADS:(r + 1) * HEADS], a[("L0_gnn_radial_score", "L0_gnn_tangential_score")[r]].rearrange("h f -> f h"), allow_slow_non_contiguous=True).then_inc(wi, 16)
            sp.dma_start(at1[:, :, :], a["L1_gnn_att1_W"].rearrange("l i o -> i l o")).then_inc(wi, 16)
            sp.dma_start(at2[:, :], a["L1_gnn_att2_W"].rearrange("l f o -> f (l o)"), allow_slow_non_contiguous=True).then_inc(wi, 16)
            sp.dma_start(bias2[:, :], a["L1_gnn_att1_b"].rearrange("l f -> f l"), allow_slow_non_contiguous=True).then_inc(wi, 16)
            sp.dma_start(bias3[:, :], at(a["L1_gnn_att2_b"], 0, [[0, P], [1, LAYERS]])).then_inc(wi, 16)
            sp.dma_start(rscale[:, :], at(a["L0_gnn_radial_distance_scale"], 0, [[0, P], [1, 1]])).then_inc(wi, 16)
            for l in range(2):
                sp.dma_start(xt_d[l][SLOTS:SLOTS + 8, :], zrow).then_inc(S_("tables_out"), 16)
            for l in range(LAYERS):
                sp.dma_start(at(dt_d[l], SLOTS, [[1, 8], [1, 1]]), zrow_ten).then_inc(S_("tables_out"), 16)
            sp.wait_ge(S_("payload_made"), 1)
            sp.dma_start(pay_d[0:full * SW, :].rearrange("(p j) w -> p j w", j=SW), PAYT[0:full]).then_inc(S_("tables_out"), 16)
            sp.dma_start(pay_d[full * SW:E, :].rearrange("(p j) w -> p j w", p=1), PAYT[full:full + 1, 0:part, :]).then_inc(S_("tables_out"), 16)
            sp.dma_start(dstf_d[0:full * SW, :].rearrange("(p j) w -> p (j w)", j=SW), NF[0:full, 0:SW]).then_inc(S_("tables_out"), 16)
            sp.dma_start(dstf_d[full * SW:E, :].rearrange("(p j) w -> p (j w)", p=1), NF[full:full + 1, 0:part]).then_inc(S_("tables_out"), 16)
            sp.dma_start(pos_d.rearrange("(p j) w -> p (j w)", p=100), INIT).then_inc(S_("tables_out"), 16)
            sp.wait_ge(S_("sorted"), 1)
            for o in range(2):
                sp.dma_start(key_d[o].rearrange("(p j) -> p j", p=P), KA[:, o * SW:(o + 1) * SW]).then_inc(S_("keys_out"), 16)
            sp.wait_ge(S_("keys_out"), 32)
            for o in range(2):
                sp.dma_start(TR[:, o * 254:(o + 1) * 254].rearrange("r (h j) -> r h j", h=2).bitcast(F32),
                             at(key_d, o * SORT, [[TE, HT], [HT * TE, 2], [1, 127]])).then_inc(S_("keys_back"), 16)
            sp.wait_ge(S_("decoded"), 1)
            for o in range(2):
                sp.dma_start(at(node_d, o * NTROW + 128, [[128, HT], [HT * 128, 2], [1, 128]]), NTt[:, 2 * o:2 * o + 2, :]).then_inc(S_("nodes_out"), 16)
                for k, t_ in enumerate((NLt, FUt)):
                    sp.dma_start(at(flag_d, (2 * o + k) * T, [[1, HT], [HT, 2]]), t_[:, 2 * o:2 * o + 2], allow_slow_non_contiguous=True).then_inc(S_("nodes_out"), 16)
            for off in (0, 128 + T * 128):
                sp.dma_start(at(node_d, off, [[NTROW, 2], [1, 128]]), PADT).then_inc(S_("nodes_out"), 16)
            dense_sp(sp, RUN_A, a["x"], x1_d)
            dense_in_loop_sp(sp, LOOP_A, a["x"], x1_d, dBuf)
            if rest(3):
                L0_sp(sp)
            if rest(5):
                L1_sp(sp)
            sp.wait_ge(S_("nodes_out"), 16 * 8)
            sp.wait_ge(S_("tables_out"), 16 * 10)

        @block.vector
        def _(v):
            v.memset(NI, N)
            v.memset(EW, 0.0)
            v.memset(eps_c[:, :], LN_EPS)
            v.memset(PADT, -1.0)
            v.memset(zrow, 0.0)
            v.memset(zrow_ten, 10.0)
            v.memset(tiny_c[:, :], 1e-6)
            v.memset(A2[:, :], 0.0)
            v.memset(wo[:, :], 0.0)
            v.memset(wb[:, :, :], 0.0)
            v.memset(INIT, float(T * P))
            v.memset(SIt, NOWHERE)
            v.memset(Et, 0.0).then_inc(S_("pads_set"), 1)
            v.wait_ge(S_("ids_in"), 16 * 6)
            v.tensor_copy(NF, NI)
            v.drain()
            v.tensor_copy(PAYT[:, :, 0], NF[:, SW:2 * SW])
            v.tensor_copy(PAYT[:, :, 1], EW).then_inc(S_("payload_made"), 1)
            v.tensor_scalar(T1t, NF, float(HALF), None, ALU.is_ge)
            v.tensor_scalar(KA, NF, float(-HALF), None, ALU.add)
            v.tensor_scalar(KB, NF, -1.0, float(HALF - 1), ALU.mult, ALU.add)
            v.drain()
            v.tensor_tensor(KA, KA, KB, ALU.max)
            v.tensor_scalar(T2t.bitcast(I32), T1t, -1.0, None, ALU.add)
            v.drain()
            v.tensor_scalar(NI, KA, float(OFFSET >> 15), None, ALU.add)
            v.tensor_scalar(T2t.bitcast(I32), T2t.bitcast(I32), FLIP, None, ALU.bitwise_and)
            v.drain()
            v.tensor_scalar(NI, NI, 15, None, ALU.logical_shift_left)
            v.wait_ge(S_("iotas"), 1)
            v.drain()
            v.tensor_tensor(NI, NI, EI, ALU.bitwise_or)
            v.drain()
            v.tensor_tensor(KA.bitcast(I32), NI, T2t.bitcast(I32), ALU.bitwise_xor)
            v.tensor_scalar(em[:, :], PI, float(TE), None, ALU.is_ge)
            for b in range(7):
                v.tensor_scalar(PB[:, b:b + 1], PI, b, 1, ALU.logical_shift_right, ALU.bitwise_and)
            v.drain()
            v.tensor_scalar(SG[:, 0:7], PB, -2.0, 1.0, ALU.mult, ALU.add)
            v.drain()
            v.tensor_tensor(SG[:, 8:14], SG[:, 0:6], SG[:, 1:7], ALU.mult)
            v.tensor_scalar(SG[:, 7:8], SG[:, 0:1], -1.0, None, ALU.mult)
            cur, oth = KA, KB
            v4 = cur.rearrange("p (g q) -> p g q", q=4)[:, :, 2:4]
            v.drain()
            v.tensor_scalar(v4, v4, -1.0, None, ALU.mult)

            def exchange(cur, oth, d):
                x = cur.rearrange("p (g t d) -> p g t d", t=2, d=d)
                y = oth.rearrange("p (g t d) -> p g t d", t=2, d=d)
                v.drain()
                v.tensor_tensor(y[:, :, 0, :], x[:, :, 0, :], x[:, :, 1, :], ALU.min)
                v.tensor_tensor(y[:, :, 1, :], x[:, :, 0, :], x[:, :, 1, :], ALU.max)
                return oth, cur

            turns = 0
            for k in range(1, 16):
                if k >= 9:
                    v.drain().then_inc(S_("turn_in"), 1)
                    turns += 1
                    v.wait_ge(S_("turned"), 2 * turns - 1)
                    v.tensor_copy(cur, bank[0][:, :])
                    for st in range(k - 9, -1, -1):
                        cur, oth = exchange(cur, oth, 1 << st)
                    sides.append((turns, 0 if cur is KA else 1))
                    v.drain().then_inc(S_("turn_in"), 1)
                    v.wait_ge(S_("turned"), 2 * turns)
                    v.tensor_copy(cur, bank[1][:, :])
                for st in range(min(k, 8) - 1, -1, -1):
                    cur, oth = exchange(cur, oth, 1 << st)
                side_in.append(0 if cur is KA else 1)
                v.drain()
                if k <= 6:
                    w = 1 << k
                    m = cur.rearrange("p (g q) -> p g q", q=4 * w)[:, :, w:3 * w]
                    v.tensor_scalar(m, m, -1.0, None, ALU.mult)
                elif k == 7:
                    m = cur.rearrange("p (g q) -> p g q", q=256)
                    v.tensor_scalar(m[:, :, 0:128], m[:, :, 0:128], SG[:, 0:1], None, ALU.mult)
                    v.tensor_scalar(m[:, :, 128:256], m[:, :, 128:256], SG[:, 7:8], None, ALU.mult)
                elif k <= 13:
                    v.tensor_scalar(cur, cur, SG[:, k:k + 1], None, ALU.mult)
                elif k == 14:
                    v.tensor_scalar(cur, cur, SG[:, 6:7], None, ALU.mult)
            if cur is not KA:
                v.tensor_copy(KA, cur)
            v.drain().then_inc(S_("sorted"), 1)

            v.wait_ge(S_("keys_back"), 32)
            v.tensor_scalar(D1, TR, 31, None, ALU.arith_shift_right)
            v.drain()
            v.tensor_scalar(D2, D1, FLIP, None, ALU.bitwise_and)
            v.tensor_copy(D3, D1)
            v.drain()
            v.tensor_tensor(D1, TR, D2, ALU.bitwise_xor)
            v.drain()
            v.tensor_scalar(D2, D1, 32767, None, ALU.bitwise_and)
            v.tensor_scalar(D1, D1, 15, None, ALU.logical_shift_right)
            v.drain()
            v.tensor_scalar(D4, D3, 2.0, 1.0, ALU.mult, ALU.add)
            v.drain()
            v.scalar_tensor_tensor(D4, D1, float(-(OFFSET >> 15)), D4, ALU.add, ALU.mult)
            v.drain()
            ndf = ND.rearrange("r q j -> r (q j)")
            v.scalar_tensor_tensor(ndf, D3, float(HALF), D4, ALU.add, ALU.add)
            v.tensor_scalar(Et[:, :, 0:TE], D2.rearrange("r (q j) -> r q j", j=127)[:, :, 0:TE], float(E - 1), None, ALU.min)
            v.drain()
            v.tensor_copy(NTt[:, :, 0:TE], ND[:, :, 0:TE])
            v.tensor_copy(NTt[:, :, TE:TE + 1], ND[:, :, 0:1])
            v.tensor_copy(NTt[:, :, TE + 1:TE + 2], ND[:, :, TE - 1:TE])
            v.tensor_tensor(NE, ND[:, :, 0:TE], ND[:, :, 1:TE + 1], ALU.not_equal)
            v.tensor_tensor(FUt, ND[:, :, 0], ND[:, :, TE - 1], ALU.is_equal)
            v.drain()
            v.tensor_scalar(NLt, NE[:, :, TE - 1], -1.0, 1.0, ALU.mult, ALU.add)
            v.tensor_scalar(SIt[:, :, 0:TE], NE, -FAR, FAR, ALU.mult, ALU.add)
            v.drain()
            v.tensor_tensor(SIt[:, :, 0:TE], SIt[:, :, 0:TE], ND[:, :, 0:TE], ALU.add)
            v.memset(smr[:, :, 0:1], 1.0)
            v.tensor_scalar(smr[:, :, 1:TE + 1], NE[:, 2:4, :], -1.0, 1.0, ALU.mult, ALU.add)
            v.drain().then_inc(S_("decoded"), 1)
            for ix in (*scat_i, *own_i, *far_i, pos_i):
                v.memset(ix[:, T:], 0)
            v.wait_ge(S_("tiles_turned"), 1)
            for o in range(2):
                v.tensor_copy(node[o][:, :], bank[3 * o][:, 0:T])
                v.tensor_scalar(own_i[o][:, 0:T], bank[3 * o][:, 0:T], float(N - 1), None, ALU.min)
                v.tensor_copy(scat_i[o][:, 0:T], bank[3 * o + 1][:, 0:T])
                v.tensor_copy(perm_i[o][:, 0:T], bank[3 * o + 2][:, 0:T])
            v.drain().then_inc(S_("indices_ready"), 1)
            dense_dve(v, RUN_A)
            if rest(3):
                L0_dve(v)
            if rest(5):
                L1_dve(v)

        @block.scalar
        def _(s_):
            s_.wait_ge(S_("scores_t"), 1)
            s_.activation(wT, bank[6][0:F, :], ACT.Copy).then_inc(S_("scores_c"), 1)
            s_.wait_ge(S_("scores_t"), 2)
            s_.activation(A2[0:F, 0:H8], bank[7][0:F, 0:H8], ACT.Copy)
            s_.activation(A2[F:P, H8:], bank[7][F:P, 0:H8], ACT.Copy).then_inc(S_("scores_c"), 1)
            dense_act(s_, RUN_A)
            if rest(3):
                L0_act(s_)
            if rest(5):
                L1_act(s_)

        @block.tensor
        def _(pe):
            pe.wait_ge(S_("iotas"), 1)
            pe.wait_ge(S_("weights_in"), 16 * 17)
            for h in range(HEADS):
                ins = pe.transpose(bank[6][0:F, h * P:(h + 1) * P], wp4[:, h, :], ident[:, :])
            ins.then_inc(S_("scores_t"), 1)
            pe.wait_ge(S_("scores_c"), 1)
            for h in range(H8):
                ins = pe.matmul(bank[7][:, h:h + 1], wT[:, (h % HEADS) * P:(h % HEADS + 1) * P], rsT[:, h:h + 1], start=True, stop=True)
            ins.then_inc(S_("scores_t"), 1)
            for turn in range(1, 8):
                src = (KA, KB)[side_in[7 + turn - 1]]
                pe.wait_ge(S_("turn_in"), 2 * turn - 1)
                for q in range(4):
                    ins = pe.transpose(bank[0][:, q * P:(q + 1) * P], src[:, q * P:(q + 1) * P], ident[:, :])
                ins.then_inc(S_("turned"), 1)
                src = (KA, KB)[sides[turn - 1][1]]
                pe.wait_ge(S_("turn_in"), 2 * turn)
                for q in range(4):
                    ins = pe.transpose(bank[1][:, q * P:(q + 1) * P], src[:, q * P:(q + 1) * P], ident[:, :])
                ins.then_inc(S_("turned"), 1)
            pe.wait_ge(S_("decoded"), 1)
            for o in range(2):
                for n_, t_ in enumerate((NTt, SIt, Et)):
                    for h in range(2):
                        ins = pe.transpose(bank[3 * o + n_][:, h * HT:(h + 1) * HT], t_[:, 2 * o + h, :], ident[0:HT, 0:HT])
            ins.then_inc(S_("tiles_turned"), 1)
            if rest(3):
                L0_pe(pe)
            if rest(5):
                L1_pe(pe)

        @block.gpsimd
        def _(g):
            top = g.to_reg(N - 1)
            for o in range(2):
                g.iota(EI[:, o * SW:(o + 1) * SW], [[1, SW]], base=0, channel_multiplier=SW)
            g.iota(PI, [[0, 1]], base=0, channel_multiplier=1)
            g.iota(posn, [[P, T]], base=0, channel_multiplier=1)
            g.memset(ident[:, :], 0.0)
            g.drain()
            g.tensor_copy(posv[:, :, 0], posn)
            g.tensor_copy(pnum[:, :], posn[:, 0:1])
            g.affine_select(ident[:, :], ident[:, :], [[-1, P]], ALU.not_equal, 1.0, base=0, channel_multiplier=1)
            g.drain().then_inc(S_("iotas"), 1)

            def narrow(before, idx, slot_v, gather_from=None, into=None, scatter_to=None, source=None, w=1, units=NSM, size=SMALL):
                slot_v, slot_i = slot_v[:, :, 0:size], small_i[:, :, 0:size]
                def take(b, c):
                    if into is not None:
                        sl = slice(c * size, (c + 1) * size) if isinstance(c, int) else ds(c * size, size)
                        g.tensor_copy(into[:, sl], slot_v[:, b] if len(into.shape) == 3 else slot_v[:, b, :, 0])

                def issue(b, c):
                    sl = slice(c * size, (c + 1) * size) if isinstance(c, int) else ds(c * size, size)
                    g.tensor_copy(slot_i[:, b], idx[:, sl])
                    if source is not None:
                        g.tensor_copy(slot_v[:, b], source[:, sl])
                    g.drain()
                    for k in range(size):
                        off = bass.IndirectOffsetOnAxis(ap=slot_i[:, b, k:k + 1], axis=0)
                        if gather_from is not None:
                            g.indirect_dma_start(slot_v[:, b, k], None, gather_from, off, bounds_check=top, oob_is_err=False).then_inc(S_(f"narrow{b}"), 16)
                        else:
                            g.indirect_dma_start(scatter_to, off, slot_v[:, b, k], None, bounds_check=top, oob_is_err=False).then_inc(S_(f"narrow{b}"), 16)

                for b in range(2):
                    issue(b, b)
                with g.Fori(1, units // 2) as j:
                    for b in range(2):
                        g.wait_ge(S_(f"narrow{b}"), j * (16 * size) + 16 * before)
                        g.sem_inc(S_("turn"), 1)
                        take(b, j * 2 + (b - 2))
                        g.drain()
                        issue(b, j * 2 + b)
                for b in range(2):
                    g.wait_ge(S_(f"narrow{b}"), 16 * (size * (units // 2) + before))
                    take(b, units - 2 + b)
                g.drain()

            g.wait_ge(S_("indices_ready"), 1)
            g.wait_ge(S_("tables_out"), 16 * 10)
            narrow(0, perm_i[0], small_v, gather_from=pay_d, into=payg, w=2)
            g.tensor_copy(far_i[0][:, 0:T], payg[:, :, 0]).then_inc(S_("payload_in"), 1)
            gather_pair(g, top, "g", a["x"], None)
            narrow(T // 2, perm_i[1], small_v1, gather_from=dstf_d, into=far_i[1])
            narrow(2 * T // 2, scat_i[1], small_v1, scatter_to=pos_d, source=posv)
            L0_pool(g, top)
            L1_pool(g, top, narrow)


sides, side_in = [], []

_INS = ["x", "src", "dst", "edge_weight", "L0_gnn_w_proj", "L0_gnn_radial_score", "L0_gnn_tangential_score",
        "L0_gnn_radial_distance_scale", "L0_gnn_w_out", "L1_gnn_nb_W", "L1_gnn_nb_b", "L1_gnn_self_W",
        "L1_gnn_self_b", "L1_gnn_att1_W", "L1_gnn_att1_b", "L1_gnn_att2_W", "L1_gnn_att2_b"]
STOP = 99


def kernel(**inputs):
    import concourse.bacc as bacc
    from concourse.bass_utils import run_bass_kernel_spmd
    nc = bacc.Bacc("TRN2", target_bir_lowering=False, num_devices=1)
    arrays, a = {}, {}
    for name in _INS:
        value = np.ascontiguousarray(inputs[name])
        if value.ndim == 0:
            value = value.reshape(1)
        arrays["in_" + name] = value
        a[name] = nc.dram_tensor("in_" + name, value.shape, mybir.dt.from_np(value.dtype), kind="ExternalInput").ap()
    out = nc.dram_tensor("out_0", (N, F), F32, kind="ExternalOutput").ap()
    del sides[:], side_in[:]
    build(nc, a, out, STOP, "ExternalOutput" if STOP < 99 else "Internal")
    r = run_bass_kernel_spmd(nc, [arrays], core_ids=[0])
    return r.results[0]["out_0"]
```

```python
from contextlib import ExitStack

import numpy as np
import concourse.bass as bass
from concourse import mybir

F32 = mybir.dt.float32
BF16 = mybir.dt.bfloat16
I32 = mybir.dt.int32
ALU = mybir.AluOpType
ACT = mybir.ActivationFunctionType
AX = mybir.AxisListType
ds = bass.ds

P = 128
N, F = 100000, 64
E = 25000
HEADS, LAYERS = 4, 3
H8 = 2 * HEADS
GAMMA, ZETA = -0.45, 1.05
LN_EPS = 1e-5

TE = 126
CARRY = TE
T = 200
HT = T // 2
SLOTS = T * TE
C = 4
NCH = T // C
SMALL = 20
NSM = T // SMALL
SORT = 32768
SW = SORT // P
HALF = N // 2
OFFSET = 1 << 23
FLIP = -2147483648 + 32767
NOWHERE = 2.0e6
FAR = 1.0e6
ZERO_ROW = SLOTS
DSMALL = 16
BY_DMA = 4 * DSMALL
NLK = (T - BY_DMA) // C
assert NLK % 2 == 0
DEG = T + 1
LOW = -1.0e38
HUGE = 3.4028234663852886e38
HC = 8
KC = T // HC
SCAN = KC * TE

RW = 8
DCH = 96
DB = NCH
DA = DCH - DB
TAILP = (N - P * RW * DCH) // (2 * RW)
assert P * RW * DCH + 2 * RW * TAILP == N


def build(nc, a, out):
    ctx = ExitStack()
    with ctx:
        def sb(name, shape, dt=F32):
            return ctx.enter_context(nc.sbuf_tensor(name, shape, dt))

        def sem(name):
            return ctx.enter_context(nc.semaphore(name))

        def dram(name, shape, dt=F32):
            return nc.dram_tensor(name, shape, dt, kind="Internal").ap()

        def at(ap, offset, pattern):
            return bass.AP(tensor=ap.tensor, offset=offset, ap=pattern)

        key_d = dram("keys", (2, SORT))
        pay_d = dram("payload", (E, 2))
        dstf_d = dram("dst_float", (E, 1))
        NTROW = 128 + T * 128 + 128
        node_d = dram("tile_nodes", (2, NTROW))
        flag_d = dram("tile_flags", (2, 2, T))
        pos_d = dram("position_of", (N, 1))
        x1_d = dram("x_after_layer0", (N, F))
        xt_d = [dram(f"layer_rows{l}", (SLOTS + 8, F)) for l in range(2)]
        dt_d = [dram(f"degree_rows{l}", (SLOTS + 8, 1)) for l in range(LAYERS)]
        base_d = dram("base_rows", (SLOTS, F))
        row_d = dram("row_of_far_degree", (1, T * P), BF16)

        big1 = sb("big1", [P, T, F])
        big2 = sb("big2", [P, T, F])
        regs = sb("regs", [P, T * F])
        den = sb("den", [P, 9 * RW * F + 192])
        S = regs[:, :].bitcast(BF16).rearrange("p (t e) -> p t e", e=P)
        b2 = big2[:, :, :].rearrange("p t f -> p (t f)")
        b1 = big1[:, :, :].rearrange("p t f -> p (t f)")
        dX = [den[:, (3 * k) * 512:(3 * k + 1) * 512].rearrange("p (r f) -> p r f", f=F) for k in range(3)]
        dC = [den[:, (3 * k + 1) * 512:(3 * k + 2) * 512].rearrange("p (r f) -> p r f", f=F) for k in range(3)]
        dQ = [den[:, (3 * k + 2) * 512:(3 * k + 3) * 512].rearrange("p (r f) -> p r f", f=F) for k in range(3)]
        dstat = sb("dstat", [P, 3, 3, RW])

        KA, KB = b1[:, 0:512], b1[:, 512:1024]
        NI = b1[:, 1024:1536].bitcast(I32)
        NF = b1[:, 1536:2048]
        EI = b1[:, 2048:2560].bitcast(I32)
        T1t, T2t = b1[:, 2560:3072], b1[:, 3072:3584]
        EW = b1[:, 3584:3840]
        PAYT = b1[:, 3840:4352].rearrange("p (j w) -> p j w", w=2)
        SG = b1[:, 4352:4368]
        PI = b1[:, 4368:4369].bitcast(I32)
        PB = b1[:, 4369:4376].bitcast(I32)
        TR = b1[0:HT, 4400:4400 + 508].bitcast(I32)
        D1 = b1[0:HT, 4920:4920 + 508].bitcast(I32)
        D2 = b1[0:HT, 5440:5440 + 508].bitcast(I32)
        D3 = b1[0:HT, 5960:5960 + 508]
        D4 = b1[0:HT, 6480:6480 + 508]
        ND = b1[0:HT, 7000:7000 + 508].rearrange("r (q j) -> r q j", j=127)
        NTt = b1[0:HT, 7520:7520 + 512].rearrange("r (q j) -> r q j", j=128)
        SIt = b1[0:HT, 8040:8040 + 512].rearrange("r (q j) -> r q j", j=128)
        Et = b1[0:HT, 8560:8560 + 512].rearrange("r (q j) -> r q j", j=128)
        NE = b1[0:HT, 9080:9080 + 504].rearrange("r (q j) -> r q j", j=126)
        NLt = b1[0:HT, 9600:9604]
        FUt = b1[0:HT, 9604:9608]
        PADT = b1[0:2, 9700:9828]
        INIT = b1[0:100, 10000:11000]

        node = [sb(f"node{o}", [P, T]) for o in range(2)]
        scat_i = [sb(f"scat_i{o}", [P, T + 8], I32) for o in range(2)]
        own_i = [sb(f"own_i{o}", [P, T + 8], I32) for o in range(2)]
        far_i = [sb(f"far_i{o}", [P, T + 8], I32) for o in range(2)]
        pos_i = sb("pos_i", [P, T + 8], I32)
        wneg = sb("wneg", [P, T])
        perm0 = b2[:, 0:T].bitcast(I32)
        payg = b2[:, 416:816].rearrange("p (t w) -> p t w", w=2)
        posn = b2[:, 1416:1616].bitcast(I32)
        small_v = sb("small_v", [P, 2, SMALL, 2])
        small_i = sb("small_i", [P, 2, SMALL], I32)
        small_v1 = sb("small_v1", [P, 2, SMALL, 1])

        G = sb("G", [P, 2, C, 2, F])
        XC = sb("XC", [P, 2, C, 2, F])
        SQ = sb("SQ", [P, 2, C, 2, F])
        VS = sb("VS", [P, 2, C, F])
        TS = sb("TS", [P, 2, C, F])
        stat = sb("stat", [P, 2, 3, 2 * C])
        idx_s = sb("idx_s", [P, 2, 2, C], I32)
        SE = sb("SE", [P, T, 2])
        Zs = [t_[:, :, :, :, :].rearrange("p b c d f -> p (b c d f)").rearrange("p (c h f) -> p c h f", c=C, f=F) for t_ in (G, XC)]
        ZTs = [SQ[:, :, :, :, :].rearrange("p b c d f -> p (b c d f)"), den[:, 1024:2048]]
        LG = den[:, 3200:4800].rearrange("p (t h) -> p t h", h=H8)
        LGP = regs[:, 9480:9480 + T * H8]
        BT = den[:, 3200:4000].rearrange("p (t h) -> p t h", h=HEADS)
        NB = [den[:, k * 512:(k + 1) * 512].rearrange("p (t e) -> p t e", e=P) for k in range(2)]
        NBL = [den[:, 3072 + k * 512:3584 + k * 512].rearrange("p (t e) -> p t e", e=P) for k in range(2)]
        STg = [den[:, 2048 + k * 512:2560 + k * 512].rearrange("p (t e) -> p t e", e=P) for k in range(2)]
        IDS = den[0:64, 0:SCAN + 2]
        SQn = den[0:64, 0:SCAN]
        SAME = regs[0:64, 0:SCAN + 1]
        NEG = regs[0:64, 3160:3160 + SCAN + 1]
        SL = regs[0:64, 6320:6320 + SCAN]
        SP_ = regs[0:64, 9480:9480 + SCAN]
        ccol = sb("ccol", [P, 8])
        crow = den[0:1, 4000:4400]
        carr = den[0:1, 4400:4800]
        FLS = den[0:F, 4000:4400].rearrange("f (t k) -> f t k", k=2)
        AF, AB, BF_, BB = [den[0:F, k * 200:(k + 1) * 200] for k in range(4)]
        CF = den[0:F, 1024:1424].rearrange("f (k t) -> f k t", k=2)
        CT = den[0:HT, 1424:1680].rearrange("r (q f) -> r q f", f=F)
        FLB = [sb(f"FLB{o}", [F, 2, T]) for o in range(1)]
        TT = [[den[:, (3 * b + k) * 512:(3 * b + k + 1) * 512] for k in range(3)] for b in range(2)]
        LR = [den[:, 3072 + b * 768:3072 + (b + 1) * 768].rearrange("p (n c f) -> p n c f", n=3, f=F) for b in range(2)]
        MT, PF, PB_ = [den[0:HT, k * 256:k * 256 + 252].rearrange("r (h e) -> r h e", h=2) for k in range(3)]
        MSK = sb("MSK", [P, T])
        VAL0 = sb("VAL0", [P, T])
        VAL1 = sb("VAL1", [P, T])
        DCc = sb("DCc", [P, T])
        DG = den[:, 1024:1327].bitcast(BF16).rearrange("p (k t) -> p k t", k=3)
        RB = [den[:, 1536 + k * 256:1792 + k * 256].bitcast(BF16) for k in range(2)]
        OH = [den[:, 2048 + k * 256:2304 + k * 256].bitcast(BF16) for k in range(2)]
        PICK = [den[:, 2560 + k * 202:2560 + k * 202 + DEG] for k in range(C)]
        RES = [den[:, 3072 + k * 202:3072 + k * 202 + T] for k in range(2)]
        QI = [den[:, 2560 + k * 202:2560 + k * 202 + T].bitcast(I32) for k in range(2)]
        ER = den[0:HT, 3500:3628].bitcast(BF16).rearrange("r (q j) -> r q j", q=2)
        tile_far = wneg
        steps_i = own_i[0][:, 0:DEG]
        steps = far_i[0][:, 0:DEG].bitcast(F32)
        pnum = sb("pnum", [P, 1])
        perm_i = [perm0, VAL1[:, :].bitcast(I32)]
        posv = VAL0[:, :].unsqueeze(2)
        smr = sb("smr", [HT, 2, TE + 1])
        em = sb("em", [P, 1])
        tiny_c = sb("tiny_c", [P, 1])

        wp4 = sb("wp4", [P, HEADS, F])
        wm = sb("wm", [P, 2, F])
        rsT = sb("rsT", [F, H8])
        A2 = sb("A2", [P, 2 * H8])
        wo = sb("wo", [P, P])
        wb = sb("wb", [P, LAYERS, P])
        at1 = sb("at1", [P, LAYERS, F])
        at2 = sb("at2", [F, LAYERS])
        bias1 = sb("bias1", [P, LAYERS])
        bias2 = sb("bias2", [F, LAYERS])
        bias3 = sb("bias3", [P, LAYERS])
        rscale = sb("rscale", [P, 1])
        wT = b1[0:F, 11100:11100 + 512]
        zrow = b1[0:8, 11700:11764]
        zrow_ten = b1[0:8, 11764:11765]

        ident = sb("ident", [P, P])
        eps_c = sb("eps_c", [P, 1])

        bank = [ctx.enter_context(nc.psum_tensor(f"bank{i}", [P, 512], F32)) for i in range(8)]

        s = {}

        def signal(name):
            if name not in s:
                s[name] = sem(name)
            return s[name]

        def pipelined(eng, stages, n=NCH):
            deep = max(lag for lag, _ in stages)
            peel = (deep + 3) // 2 * 2
            for c in range(peel):
                for lag, fn in stages:
                    if c - lag >= 0:
                        fn(c - lag, (c - lag) % 2, (c - lag) // 2)
            with eng.Fori(peel // 2, n // 2) as j:
                for b in range(2):
                    for lag, fn in stages:
                        fn(j * 2 + (b - lag), (b - lag) % 2, j + (b - lag) // 2)
            for c in range(n, n + deep):
                for lag, fn in stages:
                    if c - lag < n:
                        fn(c - lag, (c - lag) % 2, (c - lag) // 2)

        def early(c):
            return isinstance(c, int) and c < 2

        def tiles(c, shift=0):
            return slice(c * C + shift, c * C + shift + C) if isinstance(c, int) else ds(c * C + shift, C)

        def one(c, k):
            return slice(c * C + k, c * C + k + 1) if isinstance(c, int) else ds(c * C + k, 1)

        def bc(ap, n):
            return ap.unsqueeze(len(ap.shape)).broadcast_to([*ap.shape, n])

        ctx.enter_context(nc.allow_non_contiguous_dma(reason="columns of flags, biases and ends of tiles"))
        block = ctx.enter_context(nc.Block())

        def dense_rows(ap, c):
            if isinstance(c, int):
                return ap[0:P * RW * DCH, :].rearrange("(p c r) f -> c p r f", c=DCH, r=RW)[c]
            return ap[0:P * RW * DCH, :].rearrange("(p c r) f -> c p r f", c=DCH, r=RW)[ds(c, 1)].rearrange("o p r f -> (o p) r f")

        def dense_tail(ap, u):
            return ap[P * RW * DCH:N, :].rearrange("(p u r) f -> u p r f", u=2, r=RW)[u]

        dBuf = list(zip(dX, dC, dQ))
        bBuf = [tuple(b2[:, (3 * k + i) * 512:(3 * k + i + 1) * 512].rearrange("p (r f) -> p r f", f=F) for i in range(3))
                for k in range(2)]

        assert all(len(range(k, DA + 2, 3)) == (DA + 2) // 3 for k in range(3))
        RUN_A, RUN_B = ("da", 0, 0), ("da", DA + 2, (DA + 2) // 3)
        LOOP_A, LOOP_B = ("dl", 0, 0), ("dl", DB, DB // 2)

        def dense_stores(k):
            return len(range(k, DA + 2, 3))

        def dense_first(v, tag, c, k, n, j, buf):
            X_, C_, _ = buf[k]
            v.wait_ge(signal(f"{tag[0]}_in{k}"), (j + (tag[2] + 1)) * 16)
            v.tensor_reduce(dstat[0:n, k, 0], X_[0:n], AX.X, ALU.add)
            v.drain()
            v.scalar_tensor_tensor(C_[0:n], dstat[0:n, k, 0].unsqueeze(2).broadcast_to([n, RW, F]), -1.0 / F,
                                   X_[0:n], ALU.mult, ALU.add).then_inc(signal(f"{tag[0]}_cen"), 1)

        def dense_second(v, tag, c, k, n, buf):
            v.wait_ge(signal(f"{tag[0]}_sq"), c + (tag[1] + 1))
            v.tensor_reduce(dstat[0:n, k, 1], buf[k][2][0:n], AX.X, ALU.add).then_inc(signal(f"{tag[0]}_var"), 1)

        def dense_third(v, tag, c, k, n, buf):
            X_, C_, _ = buf[k]
            v.wait_ge(signal(f"{tag[0]}_std"), c + (tag[1] + 1))
            v.reciprocal(dstat[0:n, k, 2], dstat[0:n, k, 2])
            v.drain()
            v.scalar_tensor_tensor(C_[0:n], C_[0:n], 0.0,
                                   dstat[0:n, k, 2].unsqueeze(2).broadcast_to([n, RW, F]), ALU.max, ALU.mult)
            v.drain()
            v.tensor_tensor(X_[0:n], X_[0:n], C_[0:n], ALU.add).then_inc(signal(f"{tag[0]}_done"), 1)

        def dense_square(s_, tag, c, k, n, buf):
            s_.wait_ge(signal(f"{tag[0]}_cen"), c + (tag[1] + 1))
            s_.activation(buf[k][2][0:n], buf[k][1][0:n], ACT.Square).then_inc(signal(f"{tag[0]}_sq"), 1)

        def dense_root(s_, tag, c, k, n, buf):
            s_.wait_ge(signal(f"{tag[0]}_var"), c + (tag[1] + 1))
            s_.activation(dstat[0:n, k, 2], dstat[0:n, k, 1], ACT.Sqrt, bias=eps_c[0:n, :], scale=1.0 / F).then_inc(signal(f"{tag[0]}_std"), 1)

        def dense_sp(sp, tag, src, dst):
            t_ = tag

            def load(c, k, j):
                if j is not None:
                    sp.wait_ge(signal(f"{t_[0]}_out{k}"), (j + t_[2]) * 16)
                if isinstance(c, int) and c >= DA:
                    sp.dma_start(dX[k][0:TAILP], dense_tail(src, c - DA)).then_inc(signal(f"{t_[0]}_in{k}"), 16)
                else:
                    sp.dma_start(dX[k], dense_rows(src, c)).then_inc(signal(f"{t_[0]}_in{k}"), 16)

            def store(c, k):
                sp.wait_ge(signal(f"{t_[0]}_done"), c + (t_[1] + 1))
                if isinstance(c, int) and c >= DA:
                    sp.dma_start(dense_tail(dst, c - DA), dX[k][0:TAILP]).then_inc(signal(f"{t_[0]}_out{k}"), 16)
                else:
                    sp.dma_start(dense_rows(dst, c), dX[k]).then_inc(signal(f"{t_[0]}_out{k}"), 16)

            for c in range(3):
                load(c, c, None)
            turns = (DA - 3) // 3
            with sp.Fori(0, turns) as j:
                for k in range(3):
                    store(j * 3 + k, k)
                    load(j * 3 + k + 3, k, j + 1)
            for c in range(3 * turns, DA + 2):
                store(c, c % 3)
                if c + 3 < DA + 2:
                    load(c + 3, c % 3, c // 3 + 1)
            for k in range(3):
                sp.wait_ge(signal(f"{t_[0]}_out{k}"), 16 * (dense_stores(k) + t_[2]))

        def dense_dve(v, tag):
            t_, parts = tag, lambda c: P if not isinstance(c, int) or c < DA else TAILP
            dense_first(v, t_, 0, 0, P, 0, dBuf)
            dense_first(v, t_, 1, 1, P, 0, dBuf)
            dense_second(v, t_, 0, 0, P, dBuf)
            turns = (DA - 2) // 3
            with v.Fori(0, turns) as j:
                for k in range(3):
                    c, slot = j * 3 + k + 2, (k + 2) % 3
                    dense_third(v, t_, j * 3 + k, (slot + 1) % 3, P, dBuf)
                    dense_first(v, t_, c, slot, P, j + (k + 2) // 3, dBuf)
                    dense_second(v, t_, j * 3 + k + 1, (slot + 2) % 3, P, dBuf)
            for c in range(3 * turns + 2, DA + 4):
                dense_third(v, t_, c - 2, (c - 2) % 3, parts(c - 2), dBuf)
                if c < DA + 2:
                    dense_first(v, t_, c, c % 3, parts(c), c // 3, dBuf)
                if c - 1 < DA + 2:
                    dense_second(v, t_, c - 1, (c - 1) % 3, parts(c - 1), dBuf)

        def dense_act(s_, tag):
            t_, parts = tag, lambda c: P if not isinstance(c, int) or c < DA else TAILP
            dense_square(s_, t_, 0, 0, P, dBuf)
            turns = (DA - 1) // 3
            with s_.Fori(0, turns) as j:
                for k in range(3):
                    dense_square(s_, t_, j * 3 + k + 1, (k + 1) % 3, P, dBuf)
                    dense_root(s_, t_, j * 3 + k, k, P, dBuf)
            for c in range(3 * turns, DA + 2):
                if c + 1 < DA + 2:
                    dense_square(s_, t_, c + 1, (c + 1) % 3, parts(c + 1), dBuf)
                dense_root(s_, t_, c, c % 3, parts(c), dBuf)

        def dense_in_loop_sp(sp, tag, src, dst, buf, others=()):
            def load(c, b, j):
                if not early(c):
                    sp.wait_ge(signal(f"{tag[0]}_out{b}"), (j + tag[2]) * 16)
                sp.dma_start(buf[b][0], dense_rows(src, c + DA)).then_inc(signal(f"{tag[0]}_in{b}"), 16)

            def store(c, b, j):
                sp.wait_ge(signal(f"{tag[0]}_done"), c + (tag[1] + 1))
                sp.dma_start(dense_rows(dst, c + DA), buf[b][0]).then_inc(signal(f"{tag[0]}_out{b}"), 16)
            pipelined(sp, [(0, load), (1, store), *others])

        def gather_pair(g, top, tag, table):
            def step(c, b, j):
                g.wait_ge(signal(f"{tag}_free{b}"), j + 1)
                g.sem_inc(signal("turn"), 1)
                for k in range(C):
                    for d in range(2):
                        g.indirect_dma_start(G[:, b, k, d, :], None, table,
                                             bass.IndirectOffsetOnAxis(ap=idx_s[:, b, d, k:k + 1], axis=0),
                                             bounds_check=top, oob_is_err=False).then_inc(signal(f"{tag}_in{b}"), 16)
            pipelined(g, [(0, step)])

        def stage_indices(v, tag, idx, c, b):
            for d, ix in enumerate(idx[:-1]):
                v.tensor_copy(idx_s[:, b, d, :], ix[:, tiles(c)])
            v.tensor_copy(idx_s[:, b, len(idx) - 1, :], idx[-1][:, tiles(c)]).then_inc(signal(f"{tag}_free{b}"), 1)

        def norm_dve(v, tag, c, b, j, dtag, buf):
            flat = lambda t_: t_[:, b].rearrange("p c d f -> p (c d) f")
            v.wait_ge(signal(f"{tag}_in{b}"), (j + 1) * (32 * C))
            v.tensor_reduce(stat[:, b, 0], flat(G), AX.X, ALU.add)
            v.drain()
            v.scalar_tensor_tensor(flat(XC), bc(stat[:, b, 0], F), -1.0 / F, flat(G), ALU.mult, ALU.add).then_inc(signal(f"{tag}_cen"), 1)
            if not (isinstance(c, int) and c == 0):
                dense_third(v, dtag, c + (-1), 1 - b, P, buf)
            v.wait_ge(signal(f"{tag}_sq"), c + 1)
            v.tensor_reduce(stat[:, b, 1], flat(SQ), AX.X, ALU.add).then_inc(signal(f"{tag}_var"), 1)
            dense_first(v, dtag, c, b, P, j, buf)
            v.wait_ge(signal(f"{tag}_std"), c + 1)
            v.reciprocal(stat[:, b, 2], stat[:, b, 2])
            v.drain()
            v.scalar_tensor_tensor(flat(XC), flat(XC), 0.0, bc(stat[:, b, 2], F), ALU.max, ALU.mult)
            v.drain()

        def norm_act(s_, tag, c, b, j, dtag, buf):
            if not (isinstance(c, int) and c == 0):
                dense_root(s_, dtag, c + (-1), 1 - b, P, buf)
            s_.wait_ge(signal(f"{tag}_cen"), c + 1)
            s_.activation(SQ[:, b], XC[:, b], ACT.Square).then_inc(signal(f"{tag}_sq"), 1)
            s_.wait_ge(signal(f"{tag}_var"), c + 1)
            s_.activation(stat[:, b, 2], stat[:, b, 1], ACT.Sqrt, bias=eps_c[:, :], scale=1.0 / F).then_inc(signal(f"{tag}_std"), 1)
            dense_square(s_, dtag, c, b, P, buf)

        def pairs(ap):
            return ap.rearrange("p c f -> p (c f)")

        def build_S_sp(sp, tag, o):
            def step(c, b, j):
                if not early(c):
                    sp.wait_ge(signal(f"{tag}_made{b}"), j)
                off = 128 + c * 512
                src = node_d[o:o + 1, off:off + 512] if isinstance(c, int) else node_d[o:o + 1, ds(off, 512)]
                sp.dma_start(NB[b].rearrange("p t e -> p (t e)"), src.broadcast_to([P, 512])).then_inc(signal(f"{tag}_ids{b}"), 16)
            pipelined(sp, [(0, step)])

        def build_S_dve(v, tag, o):
            def step(c, b, j):
                v.wait_ge(signal(f"{tag}_ids{b}"), (j + 1) * 16)
                v.tensor_tensor(S[:, tiles(c), :], NB[b], bc(node[o][:, tiles(c)], P), ALU.is_equal).then_inc(signal(f"{tag}_made{b}"), 1)
            pipelined(v, [(0, step)])
            v.drain()
            v.tensor_copy(SE[:, :, :], S[:, :, TE:])
            v.drain().then_inc(signal(f"{tag}_S"), 1)

        def carry_dve(v, tag, i=0):
            nl, fu = FLB[0][:, 0, :], FLB[0][:, 1, :]
            m = T - 1
            v.wait_ge(signal(f"{tag}_fl_c"), NCH * (i + 1))
            v.tensor_tensor(AF, nl, fu, ALU.mult)
            v.tensor_tensor(AB[:, 0:m], nl[:, 0:m], fu[:, 1:T], ALU.mult)
            v.tensor_tensor(BF_[:, 0:m], nl[:, 0:m], FLS[:, 0:m, 1], ALU.mult)
            v.tensor_tensor(BB[:, 0:m], nl[:, 0:m], FLS[:, 1:T, 0], ALU.mult)
            v.memset(CF[:, :, :], 0.0)
            v.drain()
            v.tensor_tensor_scan(CF[:, 0, 1:T], AF[:, 0:m], BF_[:, 0:m], 0.0, ALU.mult, ALU.add)
            v.tensor_tensor_scan(CF[:, 1, 0:m][:, ::-1], AB[:, 0:m][:, ::-1], BB[:, 0:m][:, ::-1], 0.0, ALU.mult, ALU.add)
            v.drain().then_inc(signal(f"{tag}_carry"), 1)
            v.wait_ge(signal(f"{tag}_carry_t"), i + 1)
            v.tensor_copy(CT.rearrange("r q f -> r (q f)"), bank[0][0:HT, 0:256]).then_inc(signal(f"{tag}_carry"), 1)

        def carry_pe(pe, tag, i=0):
            pe.wait_ge(signal(f"{tag}_carry"), 2 * i + 1)
            for q in range(4):
                ins = pe.transpose(bank[0][0:HT, q * F:(q + 1) * F], CF[:, q // 2, (q % 2) * HT:(q % 2 + 1) * HT], ident[0:F, 0:F])
            ins.then_inc(signal(f"{tag}_carry_t"), 1)

        def carry_sp(sp, tag, big, i=0):
            sp.wait_ge(signal(f"{tag}_carry"), 2 * i + 2)
            for q in range(4):
                sp.dma_start(big[CARRY + q // 2:CARRY + q // 2 + 1, (q % 2) * HT:(q % 2 + 1) * HT, :].rearrange("o t f -> o (t f)"),
                             CT[:, q, :]).then_inc(signal(f"{tag}_carried"), 16)

        def L0_sp(sp):
            sp.wait_ge(signal("sm_lg"), 1)
            for h in range(H8):
                rows = slice(h * HC, (h + 1) * HC)
                sp.dma_start(IDS[rows, 1:SCAN + 1].rearrange("c (k e) -> c k e", k=KC),
                             at(node_d, 128, [[KC * 128, HC], [128, KC], [1, TE]])).then_inc(signal("scan_ids"), 16)
                sp.dma_start(IDS[rows, 0:1], at(node_d, TE - 1, [[KC * 128, HC], [1, 1]])).then_inc(signal("scan_ids"), 16)
                sp.dma_start(IDS[rows, SCAN + 1:SCAN + 2], at(node_d, 128 + KC * 128, [[KC * 128, HC], [1, 1]])).then_inc(signal("scan_ids"), 16)
            for n_ in range(2):
                sp.wait_ge(signal("ends_up"), n_ + 1)
                sp.dma_start(crow[0:1, 0:320], ccol[0:64, 0:5]).then_inc(signal("ends_row"), 16)
                sp.wait_ge(signal("carry_row"), n_ + 1)
                sp.dma_start(ccol[0:64, 5:7], carr[0:1, 0:128]).then_inc(signal("carry_col"), 16)
            sp.dma_start(FLB[0][:, :, :], at(flag_d, 0, [[0, F], [1, 2 * T]])).then_inc(signal("flags"), 16)
            sp.wait_ge(signal("alpha_out"), 4)
            build_S_sp(sp, "s0", 0)
            carry_sp(sp, "m", big1)

        def L0_pool(g, top):
            def step(c, b, j):
                g.wait_ge(signal("n_rows"), c + 1)
                g.sem_inc(signal("turn"), 1)
                for k in range(C):
                    g.indirect_dma_start(x1_d, bass.IndirectOffsetOnAxis(ap=idx_s[:, b, 0, k:k + 1], axis=0), G[:, b, k, 0, :], None,
                                         bounds_check=top, oob_is_err=False).then_inc(signal(f"n_out{b}"), 16)
            pipelined(g, [(0, step)])
            for b in range(2):
                g.wait_ge(signal(f"n_out{b}"), 16 * C * (NCH // 2))
            g.sem_inc(signal("x1_fixed"), 1)

        def segment_ends(v, data, op0, op1, first, mask):
            v.tensor_tensor_scan(SP_, mask[:, 0:SCAN], data, first, op0, op1)
            v.tensor_tensor_scan(SQn[:, ::-1], mask[:, 1:SCAN + 1][:, ::-1], data[:, ::-1], first, op0, op1)
            v.drain()
            v.tensor_copy(ccol[0:64, 0:1], SP_[:, SCAN - 1:SCAN])
            v.tensor_copy(ccol[0:64, 1:2], SQn[:, 0:1]).then_inc(signal("ends_up"), 1)

        def row_carry(v, n_, is_max):
            R = crow[0:1, 0:320].rearrange("o (q k) -> o q k", k=5)
            last, frst, lp, ln_, full = [R[:, :, k] for k in range(5)]
            m = 63
            A_, B_ = carr[0:1, 128:192], carr[0:1, 192:256]
            A2_, B2_ = carr[0:1, 256:320], carr[0:1, 320:384]
            O = carr[0:1, 0:128].rearrange("o (q k) -> o q k", k=2)
            first = LOW if is_max else 0.0
            v.wait_ge(signal("ends_row"), 16 * (n_ + 1))
            v.memset(O, first)
            v.tensor_tensor(A_[:, 0:m], lp[:, 1:64], full[:, 0:m], ALU.mult)
            v.tensor_tensor(A2_[:, 0:m], ln_[:, 0:m], full[:, 1:64], ALU.mult)
            if is_max:
                v.tensor_scalar(B_[:, 0:m], lp[:, 1:64], -1.0, -LOW, ALU.add, ALU.mult)
                v.tensor_scalar(B2_[:, 0:m], ln_[:, 0:m], -1.0, -LOW, ALU.add, ALU.mult)
                v.drain()
                v.tensor_scalar(A_[:, 0:m], A_[:, 0:m], -1.0, -LOW, ALU.add, ALU.mult)
                v.tensor_scalar(A2_[:, 0:m], A2_[:, 0:m], -1.0, -LOW, ALU.add, ALU.mult)
                v.tensor_tensor(B_[:, 0:m], B_[:, 0:m], last[:, 0:m], ALU.add)
                v.tensor_tensor(B2_[:, 0:m], B2_[:, 0:m], frst[:, 1:64], ALU.add)
                op0, op1 = ALU.add, ALU.max
            else:
                v.tensor_tensor(B_[:, 0:m], lp[:, 1:64], last[:, 0:m], ALU.mult)
                v.tensor_tensor(B2_[:, 0:m], ln_[:, 0:m], frst[:, 1:64], ALU.mult)
                op0, op1 = ALU.mult, ALU.add
            v.drain()
            v.tensor_tensor_scan(O[:, 1:64, 0], A_[:, 0:m], B_[:, 0:m], first, op0, op1)
            v.tensor_tensor_scan(O[:, 0:m, 1][:, ::-1], A2_[:, 0:m][:, ::-1], B2_[:, 0:m][:, ::-1], first, op0, op1)
            v.drain().then_inc(signal("carry_row"), 1)
            v.wait_ge(signal("carry_col"), 16 * (n_ + 1))

        def L0_dve(v):
            v.wait_ge(signal("payload_in"), 1)
            v.wait_ge(signal("nodes_out"), 16 * 8)
            v.wait_ge(signal("weights_in"), 16 * 17)
            for k in range(3):
                v.wait_ge(signal(f"da_out{k}"), 16 * dense_stores(k))
            v.tensor_scalar(wneg[:, :], payg[:, :, 1], rscale[:, 0:1], -1.0, ALU.mult, ALU.mult)
            v.drain()
            idx = (own_i[0], far_i[0])
            for b in range(2):
                stage_indices(v, "g", idx, b, b)

            def step(c, b, j):
                norm_dve(v, "g", c, b, j, LOOP_A, dBuf)
                if not early(c):
                    v.wait_ge(signal("g_raw"), c - 1)
                v.tensor_tensor(VS[:, b], XC[:, b, :, 1, :], XC[:, b, :, 0, :], ALU.subtract).then_inc(signal("g_dl"), 1)
                v.tensor_tensor(big2[:, tiles(c), :], G[:, b, :, 0, :], XC[:, b, :, 0, :], ALU.add)
                v.drain()
                stage_indices(v, "g", idx, c + 2, b)
                dense_second(v, LOOP_A, c, b, P, dBuf)
            pipelined(v, [(0, step)])
            dense_third(v, LOOP_A, NCH - 1, 1, P, dBuf)
            for b in range(2):
                v.wait_ge(signal(f"dl_out{b}"), 16 * (NCH // 2))

            v.wait_ge(signal("g_raw"), NCH)
            LGc, LPv = LG.rearrange("p (c k) h -> p h k c", c=HC), LGP.rearrange("p (k h c) -> p h k c", k=KC, h=H8)
            wv = wneg[:, :].rearrange("p (c k) -> p k c", c=HC)
            for h in range(H8):
                if h < HEADS:
                    v.tensor_tensor(LPv[:, h], LGc[:, h], wv, ALU.add)
                else:
                    v.tensor_copy(LPv[:, h], LGc[:, h])
            v.drain().then_inc(signal("sm_lg"), 1)
            v.wait_ge(signal("scan_ids"), 16 * 24)
            v.tensor_tensor(SAME, IDS[:, 1:SCAN + 2], IDS[:, 0:SCAN + 1], ALU.is_equal)
            v.tensor_tensor(ccol[0:64, 4:5], IDS[:, 1:2], IDS[:, SCAN:SCAN + 1], ALU.is_equal)
            v.drain()
            v.tensor_scalar(NEG, SAME, -1.0, -LOW, ALU.add, ALU.mult)
            v.tensor_copy(ccol[0:64, 2:3], SAME[:, 0:1])
            v.tensor_copy(ccol[0:64, 3:4], SAME[:, SCAN:SCAN + 1])
            v.drain()
            v.wait_ge(signal("sm_in"), 7)
            segment_ends(v, SL, ALU.add, ALU.max, LOW, NEG)
            row_carry(v, 0, True)
            v.tensor_tensor_scan(SP_, NEG[:, 0:SCAN], SL, ccol[0:64, 5:6], ALU.add, ALU.max)
            v.drain()
            v.tensor_tensor_scan(SQn[:, ::-1], NEG[:, 1:SCAN + 1][:, ::-1], SP_[:, ::-1], ccol[0:64, 6:7], ALU.add, ALU.max)
            v.drain()
            v.tensor_tensor(SL, SL, SQn, ALU.subtract).then_inc(signal("sm_sub"), 1)
            v.memset(BT, 0.0)
            v.wait_ge(signal("sm_exp"), 1)
            segment_ends(v, SL, ALU.mult, ALU.add, 0.0, SAME)
            row_carry(v, 1, False)
            v.tensor_tensor_scan(SP_, SAME[:, 0:SCAN], SL, ccol[0:64, 5:6], ALU.mult, ALU.add)
            v.tensor_tensor_scan(SQn[:, ::-1], SAME[:, 1:SCAN + 1][:, ::-1], SL[:, ::-1], ccol[0:64, 6:7], ALU.mult, ALU.add)
            v.drain()
            v.tensor_tensor(SP_, SP_, SQn, ALU.add)
            v.drain()
            v.tensor_tensor(SP_, SP_, SL, ALU.subtract)
            v.drain()
            v.reciprocal(SP_, SP_)
            v.drain()
            v.tensor_tensor(SL, SL, SP_, ALU.mult).then_inc(signal("sm_alpha"), 1)
            BTv = BT.rearrange("p (c k) h -> p k h c", c=HC)
            for q in range(4):
                n_ = min(8, KC - 8 * q)
                v.wait_ge(signal("sm_back"), q + 1)
                B = bank[4 + q % 2][0:TE, 0:n_ * 64].rearrange("p (k r h c) -> p k r h c", r=2, h=HEADS, c=HC)
                for k in range(n_):
                    v.tensor_copy(BTv[0:TE, 8 * q + k], B[:, k, 0])
                v.drain()
                for k in range(n_):
                    ins = v.tensor_tensor(BTv[0:TE, 8 * q + k], BTv[0:TE, 8 * q + k], B[:, k, 1], ALU.add)
                ins.then_inc(signal("alpha_out"), 1)
            v.drain()
            build_S_dve(v, "s0", 0)

            def weigh(c, b, j):
                if not early(c):
                    v.wait_ge(signal("m_tp"), c - 1)
                v.tensor_tensor(Zs[b], big1[:, tiles(c), :].unsqueeze(2).broadcast_to([P, C, HEADS, F]),
                                bc(BT[:, tiles(c), :], F), ALU.mult).then_inc(signal("m_z"), 1)
            pipelined(v, [(0, weigh)])
            v.wait_ge(signal("flags"), 16)
            carry_dve(v, "m")

            def guard(c, b, j):
                v.wait_ge(signal("n_sum"), c + 1)
                x_ = bank[b][:, 0:C * F]
                hi, lo = pairs(VS[:, b]), SQ[:, b].rearrange("p c d f -> p (c d f)")[:, 0:C * F]
                v.tensor_scalar(hi, x_, 0.0, HUGE, ALU.max, ALU.min)
                v.tensor_scalar(lo, x_, 0.0, -HUGE, ALU.min, ALU.max)
                v.drain()
                v.tensor_tensor(hi, hi, lo, ALU.add).then_inc(signal("n_safe"), 1)

            def renew(c, b, j):
                v.wait_ge(signal("n_proj"), c + 1)
                if not early(c):
                    v.wait_ge(signal(f"n_out{b}"), j * (16 * C))
                v.tensor_tensor(G[:, b, :, 0, :], bank[4 + b][:, 0:C * F].rearrange("p (c f) -> p c f", f=F), big2[:, tiles(c), :], ALU.add)
                v.tensor_copy(idx_s[:, b, 0, :], scat_i[0][:, tiles(c)])
                v.drain().then_inc(signal("n_rows"), 1)
            pipelined(v, [(0, guard), (2, renew)])

        def L0_act(s_):
            def step(c, b, j):
                norm_act(s_, "g", c, b, j, LOOP_A, dBuf)
                s_.wait_ge(signal("g_tp"), c + 1)
                s_.activation(pairs(TS[:, b]), bank[b][:, 0:C * F], ACT.Copy).then_inc(signal("g_dt"), 1)
                s_.activation(big1[:, tiles(c), :], VS[:, b], ACT.Copy)
                s_.wait_ge(signal("g_lg"), c + 1)
                s_.sem_inc(signal("turn"), 1)
                s_.activation(LG[:, tiles(c), :], bank[2 + b][:, 0:C * H8].rearrange("p (c h) -> p c h", h=H8), ACT.Copy).then_inc(signal("g_raw"), 1)
            s_.wait_ge(signal("scores_c"), 2)
            pipelined(s_, [(0, step)])
            dense_root(s_, LOOP_A, NCH - 1, 1, P, dBuf)
            SLk = SL.rearrange("q (k e) -> q k e", e=TE)
            for q in range(7):
                n_ = min(4, KC - 4 * q)
                s_.wait_ge(signal("sm_t"), q + 1)
                s_.activation(SLk[:, 4 * q:4 * q + n_, :], bank[q % 2][0:64, 0:n_ * P].rearrange("q (k e) -> q k e", e=P)[:, :, 0:TE], ACT.Copy).then_inc(signal("sm_in"), 1)
            s_.wait_ge(signal("sm_sub"), 1)
            s_.activation(SL, SL, ACT.Exp).then_inc(signal("sm_exp"), 1)

            def out_t(c, b, j):
                s_.wait_ge(signal("m_tp"), c + 1)
                s_.activation(ZTs[b][:, 0:512], bank[2 * b][:, :], ACT.Copy)
                s_.activation(ZTs[b][:, 512:1024], bank[2 * b + 1][:, :], ACT.Copy).then_inc(signal("m_ev"), 1)

            def out_v(c, b, j):
                s_.wait_ge(signal("m_mm"), c + 1)
                s_.activation(pairs(VS[:, b]), bank[4 + b][:, 0:C * F], ACT.Copy, scale=1.0 / HEADS).then_inc(signal("m_v"), 1)
                s_.activation(big1[:, tiles(c), :], bank[4 + b][:, 0:C * F].rearrange("p (c f) -> p c f", f=F), ACT.Copy, scale=1.0 / HEADS)

            pipelined(s_, [(0, out_t), (1, out_v), (2, lambda c, b, j: ends_act(s_, "m", c, b, j))])

            def widen(c, b, j):
                if not early(c):
                    s_.wait_ge(signal("n_sum"), c - 1)
                    s_.sem_inc(signal("turn"), 1)
                s_.activation(STg[b], S[:, tiles(c), :], ACT.Copy).then_inc(signal("n_st"), 1)

            def out_g(c, b, j):
                s_.wait_ge(signal("n_tp"), c + 1)
                s_.activation(pairs(TS[:, b]), bank[2 + b][:, 0:C * F], ACT.Copy).then_inc(signal("n_gt"), 1)
            s_.wait_ge(signal("m_carry_t"), 1)
            pipelined(s_, [(0, widen), (1, out_g)])

        def ends_act(s_, tag, c, b, j, base=0):
            s_.wait_ge(signal(f"{tag}_fl"), c + (base + 1))
            s_.sem_inc(signal("turn"), 1)
            s_.activation(FLS[:, tiles(c), :], bank[6 + b][0:F, 0:2 * C].rearrange("f (c k) -> f c k", k=2), ACT.Copy).then_inc(signal(f"{tag}_fl_c"), 1)

        def ends_pe(pe, tag, ready, c, b, j, base=0, base2=0):
            pe.wait_ge(signal(ready), c + (base + 1))
            if not early(c):
                pe.wait_ge(signal(f"{tag}_fl_c"), c + (base2 - 1))
            pe.sem_inc(signal("turn"), 1)
            for k in range(C):
                ins = pe.matmul(bank[6 + b][0:F, 2 * k:2 * k + 2], VS[:, b, k, :], SE[:, one(c, k), :].rearrange("p o k -> p (o k)"), start=True, stop=True)
            ins.then_inc(signal(f"{tag}_fl"), 1)

        def L0_pe(pe):
            def turn(c, b, j):
                pe.wait_ge(signal("g_dl"), c + 1)
                for q in range(C // 2):
                    ins = pe.transpose(bank[b][:, q * P:(q + 1) * P], pairs(VS[:, b, 2 * q:2 * q + 2, :]), ident[:, :])
                ins.then_inc(signal("g_tp"), 1)
                pe.wait_ge(signal("g_dt"), c + 1)
                for q in range(C // 2):
                    ins = pe.matmul(bank[2 + b][:, q * 2 * H8:(q + 1) * 2 * H8], pairs(TS[:, b, 2 * q:2 * q + 2, :]), A2[:, :], start=True, stop=True)
                ins.then_inc(signal("g_lg"), 1)
            pe.wait_ge(signal("scores_c"), 2)
            pipelined(pe, [(0, turn)])
            pe.wait_ge(signal("sm_lg"), 1)
            for k in range(KC):
                q = k // 4
                if q >= 2 and k % 4 == 0:
                    pe.wait_ge(signal("sm_in"), q - 1)
                ins = pe.transpose(bank[q % 2][0:64, (k % 4) * P:(k % 4 + 1) * P], LGP[:, k * 64:(k + 1) * 64], ident[:, :])
                if k % 4 == 3 or k == KC - 1:
                    ins.then_inc(signal("sm_t"), 1)
            pe.wait_ge(signal("sm_alpha"), 1)
            SLk = SL.rearrange("q (k e) -> q k e", e=TE)
            for k in range(KC):
                q = k // 8
                if q >= 2 and k % 8 == 0:
                    pe.wait_ge(signal("alpha_out"), q - 1)
                ins = pe.transpose(bank[4 + q % 2][0:TE, (k % 8) * 64:(k % 8 + 1) * 64], SLk[:, k, :], ident[0:64, 0:64])
                if k % 8 == 7 or k == KC - 1:
                    ins.then_inc(signal("sm_back"), 1)

            def turn_z(c, b, j):
                pe.wait_ge(signal("m_z"), c + 1)
                for q in range(2):
                    for k in range(C):
                        ins = pe.transpose(bank[2 * b + q][:, k * P:(k + 1) * P], Zs[b][:, k, 2 * q:2 * q + 2, :].rearrange("p h f -> p (h f)"), ident[:, :])
                ins.then_inc(signal("m_tp"), 1)

            def project(c, b, j):
                pe.wait_ge(signal("m_ev"), c + 1)
                for k in range(C):
                    for q in range(2):
                        ins = pe.matmul(bank[4 + b][:, k * F:(k + 1) * F], ZTs[b][:, q * 512 + k * P:q * 512 + (k + 1) * P], wm[:, q, :],
                                        start=(q == 0), stop=(q == 1))
                ins.then_inc(signal("m_mm"), 1)
            pe.wait_ge(signal("s0_S"), 1)
            pipelined(pe, [(0, turn_z), (1, project), (2, lambda c, b, j: ends_pe(pe, "m", "m_v", c, b, j))])
            carry_pe(pe, "m")

            def total(c, b, j):
                pe.wait_ge(signal("n_st"), c + 1)
                for k in range(C):
                    ins = pe.matmul(bank[b][:, k * F:(k + 1) * F], STg[b][:, k, :], big1[:, one(c, k), :].rearrange("p o f -> p (o f)"), start=True, stop=True)
                ins.then_inc(signal("n_sum"), 1)

            def turn_g(c, b, j):
                pe.wait_ge(signal("n_safe"), c + 1)
                for q in range(C // 2):
                    ins = pe.transpose(bank[2 + b][:, q * P:(q + 1) * P], pairs(VS[:, b, 2 * q:2 * q + 2, :]), ident[:, :])
                ins.then_inc(signal("n_tp"), 1)

            def out_proj(c, b, j):
                pe.wait_ge(signal("n_gt"), c + 1)
                if not early(c):
                    pe.wait_ge(signal("n_rows"), c - 1)
                for q in range(C // 2):
                    ins = pe.matmul(bank[4 + b][:, q * P:(q + 1) * P], pairs(TS[:, b, 2 * q:2 * q + 2, :]), wo[:, :], start=True, stop=True)
                ins.then_inc(signal("n_proj"), 1)
            pe.wait_ge(signal("m_carried"), 16 * 4)
            pipelined(pe, [(0, total), (1, turn_g), (2, out_proj)])


        def rows_of(ap, c):
            return ap[0:SLOTS, :].rearrange("(t e) f -> e t f", e=TE)[:, tiles(c), :]

        def L1_pool(g, top, narrow):
            g.iota(steps_i, [[1, DEG]], base=0, channel_multiplier=0)
            g.drain()
            g.tensor_copy(steps, steps_i)
            narrow(3 * T // 2, far_i[1], small_v1, gather_from=pos_d, into=pos_i)
            g.sem_inc(signal("pos_in"), 1)
            gather_pair(g, top, "h", x1_d)
            g.wait_ge(signal("pos_split"), 1)
            for l in range(LAYERS):
                if l:
                    def step(c, b, j, l=l):
                        g.wait_ge(signal(f"h_free{b}"), j + (26 * l + 1))
                        g.sem_inc(signal("turn"), 1)
                        for k in range(C):
                            g.indirect_dma_start(G[:, b, k, 1, :], None, xt_d[l - 1],
                                                 bass.IndirectOffsetOnAxis(ap=idx_s[:, b, 0, k:k + 1], axis=0),
                                                 bounds_check=top, oob_is_err=False).then_inc(signal(f"h_in{b}"), 16)
                    pipelined(g, [(0, step)])
                g.wait_ge(signal("r_stored"), 16 * (l + 1))
                narrow(4 * T // 2 + l * BY_DMA // 2, pos_i, small_v1, gather_from=dt_d[l],
                       into=DCc[:, :].unsqueeze(2), units=BY_DMA // DSMALL, size=DSMALL)
                g.sem_inc(signal("deg_done"), 1)

            def last(c, b, j):
                g.wait_ge(signal("q2_fin"), c + 1)
                g.sem_inc(signal("turn"), 1)
                for k in range(C):
                    g.indirect_dma_start(out, bass.IndirectOffsetOnAxis(ap=idx_s[:, b, 0, k:k + 1], axis=0), G[:, b, k, 0, :], None,
                                         bounds_check=top, oob_is_err=False).then_inc(signal(f"f_out{b}"), 16)
            pipelined(g, [(0, last)])
            for b in range(2):
                g.wait_ge(signal(f"f_out{b}"), 16 * C * (NCH // 2))

        def L1_sp(sp):
            sp.wait_ge(signal("n_rows"), NCH)
            sp.dma_start(FLB[0][:, :, :], at(flag_d, 2 * T, [[0, F], [1, 2 * T]])).then_inc(signal("flags"), 16)

            def near_ids(c, b, j):
                if not early(c):
                    sp.wait_ge(signal("s1_made"), c - 1)
                off = 128 + c * 512
                src = node_d[1:2, off:off + 512] if isinstance(c, int) else node_d[1:2, ds(off, 512)]
                sp.dma_start(NBL[b].rearrange("p t e -> p (t e)"), src.broadcast_to([P, 512])).then_inc(signal(f"s1_ids{b}"), 16)

            def store_base(c, b, j):
                sp.wait_ge(signal("h_base"), c + 1)
                sp.dma_start(rows_of(base_d, c), VS[0:TE, b]).then_inc(signal(f"h_stored{b}"), 16)
            sp.wait_ge(signal("x1_fixed"), 1)
            dense_sp(sp, RUN_B, x1_d, out)
            dense_in_loop_sp(sp, LOOP_B, x1_d, out, bBuf, [(0, near_ids), (1, store_base)])
            for l in range(LAYERS):
                sp.wait_ge(signal("r_ends"), l + 1)
                for h in range(2):
                    sp.dma_start(crow[0:1, h * T:(h + 1) * T], ccol[0:HT, 2 * h:2 * h + 2]).then_inc(signal("r_row"), 16)
                sp.wait_ge(signal("r_carry"), l + 1)
                for h in range(2):
                    sp.dma_start(ccol[0:HT, 4 + 2 * h:6 + 2 * h], carr[0:1, h * T:(h + 1) * T]).then_inc(signal("r_col"), 16)
                sp.wait_ge(signal("r_d"), l + 1)
                sp.dma_start(at(dt_d[l], 0, [[TE, HT], [HT * TE, 2], [1, TE]]), PB_).then_inc(signal("r_stored"), 16)
                sp.wait_ge(signal("r_stored"), 16 * (l + 1))
                if l == 0:
                    sp.wait_ge(signal("pos_split"), 2)
                    sp.dma_start(at(row_d, 0, [[P, HT], [HT * P, 2], [1, P]]), ER).then_inc(signal("flags"), 16)
                    sp.wait_ge(signal("flags"), 48)

                def spread(c, b, j, l=l):
                    if not early(c):
                        sp.wait_ge(signal("o_hot"), c + (l * NLK - 1))
                    off = c * (C * P) + BY_DMA * P
                    src = row_d[:, off:off + C * P] if isinstance(c, int) else row_d[:, ds(off, C * P)]
                    sp.dma_start(RB[b], src.broadcast_to([P, C * P])).then_inc(signal(f"o_ids{b}"), 16)
                pipelined(sp, [(0, spread)], NLK)
                carry_sp(sp, "m", big1, l + 1)
                if l < 2:
                    def store(c, b, j, l=l):
                        sp.wait_ge(signal("q_out"), c + (l * NCH + 1))
                        sp.dma_start(rows_of(xt_d[l], c), TS[0:TE, b]).then_inc(signal(f"q_stored{b}"), 16)
                    pipelined(sp, [(0, store)])
                    for b in range(2):
                        sp.wait_ge(signal(f"q_stored{b}"), 16 * (NCH // 2) * (l + 1))
                    sp.sem_inc(signal("table"), 1)
                else:
                    for b in range(2):
                        sp.wait_ge(signal(f"h_stored{b}"), 16 * (NCH // 2))

                    def load(c, b, j):
                        if not early(c):
                            sp.wait_ge(signal("q2_fin"), c - 1)
                        for n_, t_ in enumerate((base_d, xt_d[0], xt_d[1])):
                            sp.dma_start(LR[b][0:TE, n_], rows_of(t_, c)).then_inc(signal(f"q2_ld{b}"), 16)
                    pipelined(sp, [(0, load)])

        def L1_dve(v):
            v.wait_ge(signal("x1_fixed"), 1)
            idx = (own_i[1], far_i[1])
            for b in range(2):
                stage_indices(v, "h", idx, b, b)
            dense_dve(v, RUN_B)
            for k in range(3):
                v.wait_ge(signal(f"da_out{k}"), 32 * dense_stores(k))
            def step0(c, b, j, l=0):
                if not early(c):
                    v.wait_ge(signal("h_t"), c + (l * NCH - 1))
                    v.wait_ge(signal("h_cc"), c + (l * NCH - 1))
                norm_dve(v, "h", c, b, j, LOOP_B, bBuf)
                if not early(c):
                    v.wait_ge(signal(f"h_stored{b}"), j * 16)
                v.tensor_tensor(VS[:, b], G[:, b, :, 0, :], XC[:, b, :, 0, :], ALU.add).then_inc(signal("h_base"), 1)
                v.drain().then_inc(signal("h_xc"), 1)
                stage_indices(v, "h", idx, c + 2, b)
                dense_second(v, LOOP_B, c, b, P, bBuf)
                v.wait_ge(signal(f"s1_ids{b}"), (j + 1) * 16)
                v.tensor_tensor(S[:, tiles(c), :], NBL[b], bc(node[1][:, tiles(c)], P), ALU.is_equal).then_inc(signal("s1_made"), 1)
            pipelined(v, [(0, step0)])
            dense_third(v, LOOP_B, NCH - 1, 1, P, bBuf)
            v.drain()
            v.tensor_copy(SE[:, :, :], S[:, :, TE:])
            v.drain().then_inc(signal("s1_S"), 1)
            for b in range(2):
                v.wait_ge(signal(f"dl_out{b}"), 16 * NCH)

            for l in range(LAYERS):
                if l:
                    v.wait_ge(signal("table"), l)
                    for b in range(2):
                        stage_indices(v, "h", (pos_i,), b, b)

                    def step(c, b, j, l=l):
                        v.wait_ge(signal(f"h_in{b}"), (j + (25 * (l + 1) + 1)) * (16 * C))
                        v.tensor_copy(G[:, b, :, 0, :], big2[:, tiles(c), :]).then_inc(signal("h_xc"), 1)

                    def refill(c, b, j, l=l):
                        v.wait_ge(signal("h_t"), c + (l * NCH + 1))
                        v.wait_ge(signal("h_cc"), c + (l * NCH + 1))
                        stage_indices(v, "h", (pos_i,), c + 2, b)
                    pipelined(v, [(0, step), (1, refill)])
                rowsum_dve(v, l)
                if l == 0:
                    v.wait_ge(signal("pos_in"), 1)
                    v.tensor_scalar(QI[0], pos_i[:, 0:T], 7, None, ALU.logical_shift_right)
                    v.tensor_scalar(QI[1], pos_i[:, 0:T], P - 1, None, ALU.bitwise_and)
                    v.tensor_copy(RES[0], pos_i[:, 0:T])
                    v.drain()
                    v.tensor_copy(tile_far[:, :], QI[0])
                    v.tensor_copy(RES[1], QI[1])
                    v.drain()
                    v.scalar_tensor_tensor(pos_i[:, 0:T], tile_far[:, :], float(TE - P), RES[0], ALU.mult, ALU.add)
                    v.drain().then_inc(signal("pos_split"), 1)
                    v.wait_ge(signal("tiles_turned"), 2)
                    v.tensor_copy(ER, bank[0][0:HT, 256:512].rearrange("r (q j) -> r q j", q=2))
                    v.drain().then_inc(signal("pos_split"), 1)
                lookup_dve(v, l)
                v.wait_ge(signal("deg_done"), l + 1)
                v.tensor_tensor(VAL0[:, :], VAL0[:, :], DCc[:, :], ALU.mult)
                v.drain()
                v.tensor_scalar(VAL1[:, :], VAL0[:, :], em[:, 0:1], None, ALU.add)
                v.drain()

                def value(tag, V_, done, sig, more=0):
                    def fn(c, b, j, l=l):
                        if not early(c):
                            v.wait_ge(signal(done), c + (l * NCH + more - 1))
                        v.tensor_tensor(VS[:, b], big1[:, tiles(c), :], bc(V_[:, tiles(c)], F), ALU.mult).then_inc(signal(sig), 1)
                    return fn
                pipelined(v, [(0, value("p", VAL0, "m_fl", "p_v", NCH))])
                carry_dve(v, "m", l + 1)
                v.wait_ge(signal("m_carried"), 64 * (l + 2))
                stages = [(0, value("q", VAL1, "q_sum", "q_v"))]
                if l == 2:
                    def final(c, b, j, l=l):
                        v.wait_ge(signal(f"q2_ld{b}"), (j + 1) * 48)
                        v.tensor_tensor(LR[b][0:TE, 1], LR[b][0:TE, 1], LR[b][0:TE, 2], ALU.add)
                        v.wait_ge(signal("q_sum"), c + (l * NCH + 1))
                        if not early(c):
                            v.wait_ge(signal(f"f_out{b}"), j * (16 * C))
                        v.tensor_tensor(G[0:TE, b, :, 0, :], bank[b][0:TE, 0:C * F].rearrange("p (c f) -> p c f", f=F), LR[b][0:TE, 0], ALU.add)
                        v.drain()
                        v.tensor_tensor(G[0:TE, b, :, 0, :], G[0:TE, b, :, 0, :], LR[b][0:TE, 1], ALU.add)
                        v.tensor_copy(idx_s[:, b, 0, :], scat_i[1][:, tiles(c)])
                        v.drain().then_inc(signal("q2_fin"), 1)
                    stages.append((1, final))
                else:
                    def keep(c, b, j, l=l):
                        v.wait_ge(signal("q_out"), c + (l * NCH + 1))
                        v.tensor_copy(big2[:, tiles(c), :], TS[:, b]).then_inc(signal("q_b2"), 1)
                    stages.append((2, keep))
                pipelined(v, stages)
                v.drain()

        def lookup_dve(v, l):
            v.memset(DG[:, :, :], 0.0)
            v.drain()
            v.tensor_copy(DG[0:TE, 0, 0:T], bank[1][0:TE, 0:T])
            v.memset(DG[0:1, 0, T:DEG], 10.0)
            v.drain()
            v.tensor_tensor(RES[0][0:TE], bank[1][0:TE, 0:T], DG[0:TE, 0, 0:T], ALU.subtract)
            v.drain()
            v.tensor_copy(DG[0:TE, 1, 0:T], RES[0][0:TE])
            v.drain()
            v.tensor_tensor(RES[0][0:TE], RES[0][0:TE], DG[0:TE, 1, 0:T], ALU.subtract)
            v.drain()
            v.tensor_copy(DG[0:TE, 2, 0:T], RES[0][0:TE])
            v.drain()

            def hot(c, b, j):
                v.wait_ge(signal(f"o_ids{b}"), (j + (l * (NLK // 2) + 1)) * 16)
                v.tensor_scalar(OH[b], RB[b], pnum[:, 0:1], None, ALU.is_equal).then_inc(signal("o_hot"), 1)

            def select(c, b, j):
                v.wait_ge(signal("o_mm"), c + (l * NLK + 1))
                for k in range(C):
                    col = one(c, k + BY_DMA)
                    v.scalar_tensor_tensor(PICK[k], steps, tile_far[:, col], bank[2 + 2 * b + k // 2][:, (k % 2) * 256:(k % 2) * 256 + DEG],
                                                 ALU.is_equal, ALU.mult, accum_out=DCc[:, col])
                v.drain().then_inc(signal("o_sel"), 1)
            pipelined(v, [(0, hot), (1, select)], NLK)

        def lookup_pe(pe, l):
            def bring(c, b, j):
                pe.wait_ge(signal("o_hot"), c + (l * NLK + 1))
                if not early(c):
                    pe.wait_ge(signal("o_sel"), c + (l * NLK - 1))
                for k in range(C):
                    for part in range(3):
                        ins = pe.matmul(bank[2 + 2 * b + k // 2][:, (k % 2) * 256:(k % 2) * 256 + DEG], OH[b][0:TE, k * P:(k + 1) * P],
                                        DG[0:TE, part, 0:DEG], start=(part == 0), stop=(part == 2))
                ins.then_inc(signal("o_mm"), 1)
            pipelined(pe, [(0, bring)], NLK)

        def rowsum_dve(v, l):
            v.wait_ge(signal("r_sig"), l + 1)
            v.tensor_scalar(MSK[:, :], MSK[:, :], ZETA - GAMMA, GAMMA, ALU.mult, ALU.add)
            v.memset(VAL0[:, :], 0.0)
            v.drain()
            v.tensor_scalar(MSK[:, :], MSK[:, :], 0.0, 1.0, ALU.max, ALU.min).then_inc(signal("r_m"), 1)
            v.wait_ge(signal("r_t"), 2 * l + 1)
            v.tensor_copy(MT, bank[0][0:HT, 0:256].rearrange("r (h e) -> r h e", h=2)[:, :, 0:TE])
            v.drain()

            def both(i0, i1):
                for h in range(2):
                    v.tensor_tensor_scan(PF[:, h, :], smr[:, h, 0:TE], MT[:, h, :], i0[h], ALU.mult, ALU.add)
                    v.tensor_tensor_scan(PB_[:, h, ::-1], smr[:, h, 1:TE + 1][:, ::-1], MT[:, h, ::-1], i1[h], ALU.mult, ALU.add)
                v.drain()
            both((0.0, 0.0), (0.0, 0.0))
            for h in range(2):
                v.tensor_copy(ccol[0:HT, 2 * h:2 * h + 1], PF[:, h, TE - 1:TE])
                v.tensor_copy(ccol[0:HT, 2 * h + 1:2 * h + 2], PB_[:, h, 0:1])
            v.drain().then_inc(signal("r_ends"), 1)
            m = T - 1
            nl, fu = FLB[0][0:1, 0, :], FLB[0][0:1, 1, :]
            A_, B_, A2_, B2_ = [den[0:1, 800 + k * 200:800 + k * 200 + m] for k in range(4)]
            R = crow.rearrange("o (t k) -> o t k", k=2)
            O = carr.rearrange("o (t k) -> o t k", k=2)
            if l == 0:
                v.wait_ge(signal("flags"), 32)
            v.memset(carr, 0.0)
            v.tensor_tensor(A_, nl[:, 0:m], fu[:, 0:m], ALU.mult)
            v.tensor_tensor(A2_, nl[:, 0:m], fu[:, 1:T], ALU.mult)
            v.wait_ge(signal("r_row"), 32 * (l + 1))
            v.tensor_tensor(B_, nl[:, 0:m], R[:, 0:m, 0], ALU.mult)
            v.tensor_tensor(B2_, nl[:, 0:m], R[:, 1:T, 1], ALU.mult)
            v.drain()
            v.tensor_tensor_scan(O[:, 1:T, 0], A_, B_, 0.0, ALU.mult, ALU.add)
            v.tensor_tensor_scan(O[:, 0:m, 1][:, ::-1], A2_[:, ::-1], B2_[:, ::-1], 0.0, ALU.mult, ALU.add)
            v.drain().then_inc(signal("r_carry"), 1)
            v.wait_ge(signal("r_col"), 32 * (l + 1))
            both([ccol[0:HT, 4 + 2 * h:5 + 2 * h] for h in range(2)], [ccol[0:HT, 5 + 2 * h:6 + 2 * h] for h in range(2)])
            v.tensor_tensor(PF, PF, PB_, ALU.add)
            v.drain()
            v.tensor_tensor(PF, PF, MT, ALU.subtract).then_inc(signal("r_total"), 1)
            v.wait_ge(signal("r_root"), l + 1)
            v.reciprocal(PB_, PB_)
            v.drain()
            v.tensor_scalar(PB_, PB_, 10.0, None, ALU.min).then_inc(signal("r_d"), 1)
            v.wait_ge(signal("r_t"), 2 * l + 2)
            v.tensor_tensor(VAL0[0:TE, :], MSK[0:TE, :], bank[1][0:TE, 0:T], ALU.mult)
            v.drain().then_inc(signal("r_val"), 1)

        def L1_act(s_):
            dense_act(s_, RUN_B)
            for l in range(LAYERS):

                def fill(c, b, j, l=l):
                    if l == 0:
                        norm_act(s_, "h", c, b, j, LOOP_B, bBuf)
                    s_.wait_ge(signal("h_xc"), c + (l * NCH + 1))
                    s_.sem_inc(signal("turn"), 1)
                    s_.activation(big1[:, tiles(c), :], (XC if l == 0 else G)[:, b, :, 1, :], ACT.Copy).then_inc(signal("h_cc"), 1)
                    s_.wait_ge(signal("h_t"), c + (l * NCH + 1))
                    s_.activation(TT[b][0], bank[b][:, :], ACT.Copy).then_inc(signal("h_e1"), 1)

                def e2(c, b, j, l=l):
                    s_.wait_ge(signal("h_m1"), c + (l * NCH + 1))
                    s_.activation(TT[b][1], bank[2 + b][:, :], ACT.Relu, bias=bias1[:, l:l + 1]).then_inc(signal("h_e2"), 1)

                def e3(c, b, j, l=l):
                    s_.wait_ge(signal("h_m2"), c + (l * NCH + 1))
                    s_.activation(TT[b][2][0:F], bank[4 + b][0:F, :], ACT.Relu, bias=bias2[:, l:l + 1]).then_inc(signal("h_e3"), 1)

                def e4(c, b, j, l=l):
                    s_.wait_ge(signal("h_m3"), c + (l * NCH + 1))
                    s_.sem_inc(signal("turn"), 1)
                    s_.activation(MSK[:, tiles(c)], bank[6 + b][:, 0:C], ACT.Copy).then_inc(signal("h_e4"), 1)
                pipelined(s_, [(0, fill), (1, e2), (2, e3), (3, e4)])
                if l == 0:
                    dense_root(s_, LOOP_B, NCH - 1, 1, P, bBuf)
                s_.drain()
                s_.activation(MSK[:, :], MSK[:, :], ACT.Sigmoid, bias=bias3[:, l:l + 1]).then_inc(signal("r_sig"), 1)
                s_.wait_ge(signal("r_total"), l + 1)
                s_.activation(PB_, PF, ACT.Sqrt, bias=tiny_c[0:HT, :]).then_inc(signal("r_root"), 1)
                pipelined(s_, [(0, lambda c, b, j, l=l: ends_act(s_, "m", c, b, j, (l + 1) * NCH))])

                def widen(c, b, j, l=l):
                    if not early(c):
                        s_.wait_ge(signal("q_sum"), c + (l * NCH - 1))
                        s_.sem_inc(signal("turn"), 1)
                    s_.activation(STg[b], S[:, tiles(c), :], ACT.Copy).then_inc(signal("q_st"), 1)

                def copy_out(c, b, j, l=l):
                    if not early(c):
                        s_.wait_ge(signal(f"q_stored{b}"), (j + 25 * l) * 16)
                        s_.wait_ge(signal("q_b2"), c + (l * NCH - 1))
                    s_.wait_ge(signal("q_sum"), c + (l * NCH + 1))
                    s_.sem_inc(signal("turn"), 1)
                    s_.activation(pairs(TS[:, b]), bank[b][:, 0:C * F], ACT.Copy).then_inc(signal("q_out"), 1)
                s_.wait_ge(signal("m_carry_t"), l + 2)
                pipelined(s_, [(0, widen)] + ([(1, copy_out)] if l < 2 else []))

        def L1_pe(pe):
            for l in range(LAYERS):

                def turn(c, b, j, l=l):
                    pe.wait_ge(signal("h_xc"), c + (l * NCH + 1))
                    for k in range(C):
                        ins = pe.transpose(bank[b][:, k * P:(k + 1) * P], (XC if l == 0 else G)[:, b, k].rearrange("p d f -> p (d f)"), ident[:, :])
                    ins.then_inc(signal("h_t"), 1)

                def m1(c, b, j, l=l):
                    pe.wait_ge(signal("h_e1"), c + (l * NCH + 1))
                    pe.matmul(bank[2 + b][:, :], wb[:, l, :], TT[b][0], start=True, stop=True).then_inc(signal("h_m1"), 1)

                def m2(c, b, j, l=l):
                    pe.wait_ge(signal("h_e2"), c + (l * NCH + 1))
                    pe.matmul(bank[4 + b][0:F, :], at1[:, l, :], TT[b][1], start=True, stop=True).then_inc(signal("h_m2"), 1)

                def m3(c, b, j, l=l):
                    pe.wait_ge(signal("h_e3"), c + (l * NCH + 1))
                    if not early(c):
                        pe.wait_ge(signal("h_e4"), c + (l * NCH - 1))
                    for k in range(C):
                        ins = pe.matmul(bank[6 + b][:, k:k + 1], TT[b][2][0:F, k * P:(k + 1) * P], at2[:, l:l + 1], start=True, stop=True)
                    ins.then_inc(signal("h_m3"), 1)
                if l:
                    pe.wait_ge(signal("q_out"), l * NCH)
                pipelined(pe, [(0, turn), (1, m1), (2, m2), (3, m3)])
                pe.wait_ge(signal("r_m"), l + 1)
                for h in range(2):
                    ins = pe.transpose(bank[0][0:HT, h * P:(h + 1) * P], MSK[:, h * HT:(h + 1) * HT], ident[:, :])
                ins.then_inc(signal("r_t"), 1)
                pe.wait_ge(signal("r_d"), l + 1)
                for h in range(2):
                    ins = pe.transpose(bank[1][0:TE, h * HT:(h + 1) * HT], PB_[:, h, :], ident[0:HT, 0:HT])
                ins.then_inc(signal("r_t"), 1)
                if l == 0:
                    pe.wait_ge(signal("pos_split"), 1)
                    for h in range(2):
                        ins = pe.transpose(bank[0][0:HT, 256 + h * P:256 + (h + 1) * P], RES[1][:, h * HT:(h + 1) * HT], ident[:, :])
                    ins.then_inc(signal("tiles_turned"), 1)
                lookup_pe(pe, l)
                if l == 0:
                    pe.wait_ge(signal("s1_S"), 1)
                pipelined(pe, [(0, lambda c, b, j, l=l: ends_pe(pe, "m", "p_v", c, b, j, l * NCH, (l + 1) * NCH))])
                carry_pe(pe, "m", l + 1)

                def total(c, b, j, l=l):
                    pe.wait_ge(signal("q_v"), c + (l * NCH + 1))
                    if not early(c):
                        pe.wait_ge(signal("q2_fin" if l == 2 else "q_out"), c + ((l * NCH if l < 2 else 0) - 1))
                    pe.wait_ge(signal("q_st"), c + (l * NCH + 1))
                    for k in range(C):
                        ins = pe.matmul(bank[b][:, k * F:(k + 1) * F], STg[b][:, k, :], VS[:, b, k, :], start=True, stop=True)
                    ins.then_inc(signal("q_sum"), 1)
                pipelined(pe, [(0, total)])

        @block.sync
        def _(sp):
            sp.wait_ge(signal("pads_set"), 1)
            full, part = E // SW, E % SW
            for o, name in enumerate(("dst", "src")):
                sp.dma_start(NI[0:full, o * SW:(o + 1) * SW], a[name][0:full * SW].rearrange("(p j) -> p j", j=SW)).then_inc(signal("ids_in"), 16)
                sp.dma_start(NI[full:full + 1, o * SW:o * SW + part], a[name][full * SW:E].rearrange("(p j) -> p j", p=1)).then_inc(signal("ids_in"), 16)
            sp.dma_start(EW[0:full, :], a["edge_weight"][0:full * SW].rearrange("(p j) -> p j", j=SW)).then_inc(signal("ids_in"), 16)
            sp.dma_start(EW[full:full + 1, 0:part], a["edge_weight"][full * SW:E].rearrange("(p j) -> p j", p=1)).then_inc(signal("ids_in"), 16)
            wi = signal("weights_in")
            wpj, wout = a["L0_gnn_w_proj"], a["L0_gnn_w_out"]
            for r in range(2):
                half = slice(r * F, (r + 1) * F)
                sp.dma_start(wp4[half], wpj.rearrange("h f g -> f h g")).then_inc(wi, 16)
                sp.dma_start(wm[half], wpj.rearrange("(q r) f g -> r f q g", r=2)[r]).then_inc(wi, 16)
                sp.dma_start(wo[half, half], wout).then_inc(wi, 16)
                sp.dma_start(wb[half, :, half], a[("L1_gnn_nb_W", "L1_gnn_self_W")[r]].rearrange("l i o -> i l o")).then_inc(wi, 16)
                sp.dma_start(bias1[half, :], a[("L1_gnn_nb_b", "L1_gnn_self_b")[r]].rearrange("l f -> f l"), allow_slow_non_contiguous=True).then_inc(wi, 16)
                sp.dma_start(rsT[:, r * HEADS:(r + 1) * HEADS], a[("L0_gnn_radial_score", "L0_gnn_tangential_score")[r]].rearrange("h f -> f h"), allow_slow_non_contiguous=True).then_inc(wi, 16)
            sp.dma_start(at1[:, :, :], a["L1_gnn_att1_W"].rearrange("l i o -> i l o")).then_inc(wi, 16)
            sp.dma_start(at2[:, :], a["L1_gnn_att2_W"].rearrange("l f o -> f (l o)"), allow_slow_non_contiguous=True).then_inc(wi, 16)
            sp.dma_start(bias2[:, :], a["L1_gnn_att1_b"].rearrange("l f -> f l"), allow_slow_non_contiguous=True).then_inc(wi, 16)
            sp.dma_start(bias3[:, :], at(a["L1_gnn_att2_b"], 0, [[0, P], [1, LAYERS]])).then_inc(wi, 16)
            sp.dma_start(rscale[:, :], at(a["L0_gnn_radial_distance_scale"], 0, [[0, P], [1, 1]])).then_inc(wi, 16)
            for l in range(2):
                sp.dma_start(xt_d[l][SLOTS:SLOTS + 8, :], zrow).then_inc(signal("tables_out"), 16)
            for l in range(LAYERS):
                sp.dma_start(at(dt_d[l], SLOTS, [[1, 8], [1, 1]]), zrow_ten).then_inc(signal("tables_out"), 16)
            sp.wait_ge(signal("payload_made"), 1)
            sp.dma_start(pay_d[0:full * SW, :].rearrange("(p j) w -> p j w", j=SW), PAYT[0:full]).then_inc(signal("tables_out"), 16)
            sp.dma_start(pay_d[full * SW:E, :].rearrange("(p j) w -> p j w", p=1), PAYT[full:full + 1, 0:part, :]).then_inc(signal("tables_out"), 16)
            sp.dma_start(dstf_d[0:full * SW, :].rearrange("(p j) w -> p (j w)", j=SW), NF[0:full, 0:SW]).then_inc(signal("tables_out"), 16)
            sp.dma_start(dstf_d[full * SW:E, :].rearrange("(p j) w -> p (j w)", p=1), NF[full:full + 1, 0:part]).then_inc(signal("tables_out"), 16)
            sp.dma_start(pos_d.rearrange("(p j) w -> p (j w)", p=100), INIT).then_inc(signal("tables_out"), 16)
            sp.wait_ge(signal("sorted"), 1)
            for o in range(2):
                sp.dma_start(key_d[o].rearrange("(p j) -> p j", p=P), KA[:, o * SW:(o + 1) * SW]).then_inc(signal("keys_out"), 16)
            sp.wait_ge(signal("keys_out"), 32)
            for o in range(2):
                sp.dma_start(TR[:, o * 254:(o + 1) * 254].rearrange("r (h j) -> r h j", h=2).bitcast(F32),
                             at(key_d, o * SORT, [[TE, HT], [HT * TE, 2], [1, 127]])).then_inc(signal("keys_back"), 16)
            sp.wait_ge(signal("decoded"), 1)
            for o in range(2):
                sp.dma_start(at(node_d, o * NTROW + 128, [[128, HT], [HT * 128, 2], [1, 128]]), NTt[:, 2 * o:2 * o + 2, :]).then_inc(signal("nodes_out"), 16)
                for k, t_ in enumerate((NLt, FUt)):
                    sp.dma_start(at(flag_d, (2 * o + k) * T, [[1, HT], [HT, 2]]), t_[:, 2 * o:2 * o + 2], allow_slow_non_contiguous=True).then_inc(signal("nodes_out"), 16)
            for off in (0, 128 + T * 128):
                sp.dma_start(at(node_d, off, [[NTROW, 2], [1, 128]]), PADT).then_inc(signal("nodes_out"), 16)
            dense_sp(sp, RUN_A, a["x"], x1_d)
            dense_in_loop_sp(sp, LOOP_A, a["x"], x1_d, dBuf)
            L0_sp(sp)
            L1_sp(sp)
            sp.wait_ge(signal("nodes_out"), 16 * 8)
            sp.wait_ge(signal("tables_out"), 16 * 10)

        @block.vector
        def _(v):
            v.memset(NI, N)
            v.memset(EW, 0.0)
            v.memset(eps_c[:, :], LN_EPS)
            v.memset(PADT, -1.0)
            v.memset(zrow, 0.0)
            v.memset(zrow_ten, 10.0)
            v.memset(tiny_c[:, :], 1e-6)
            v.memset(A2[:, :], 0.0)
            v.memset(wo[:, :], 0.0)
            v.memset(wb[:, :, :], 0.0)
            v.memset(INIT, float(T * P))
            v.memset(SIt, NOWHERE)
            v.memset(Et, 0.0).then_inc(signal("pads_set"), 1)
            v.wait_ge(signal("ids_in"), 16 * 6)
            v.tensor_copy(NF, NI)
            v.drain()
            v.tensor_copy(PAYT[:, :, 0], NF[:, SW:2 * SW])
            v.tensor_copy(PAYT[:, :, 1], EW).then_inc(signal("payload_made"), 1)
            v.tensor_scalar(T1t, NF, float(HALF), None, ALU.is_ge)
            v.tensor_scalar(KA, NF, float(-HALF), None, ALU.add)
            v.tensor_scalar(KB, NF, -1.0, float(HALF - 1), ALU.mult, ALU.add)
            v.drain()
            v.tensor_tensor(KA, KA, KB, ALU.max)
            v.tensor_scalar(T2t.bitcast(I32), T1t, -1.0, None, ALU.add)
            v.drain()
            v.tensor_scalar(NI, KA, float(OFFSET >> 15), None, ALU.add)
            v.tensor_scalar(T2t.bitcast(I32), T2t.bitcast(I32), FLIP, None, ALU.bitwise_and)
            v.drain()
            v.tensor_scalar(NI, NI, 15, None, ALU.logical_shift_left)
            v.wait_ge(signal("iotas"), 1)
            v.drain()
            v.tensor_tensor(NI, NI, EI, ALU.bitwise_or)
            v.drain()
            v.tensor_tensor(KA.bitcast(I32), NI, T2t.bitcast(I32), ALU.bitwise_xor)
            v.tensor_scalar(em[:, :], PI, float(TE), None, ALU.is_ge)
            for b in range(7):
                v.tensor_scalar(PB[:, b:b + 1], PI, b, 1, ALU.logical_shift_right, ALU.bitwise_and)
            v.drain()
            v.tensor_scalar(SG[:, 0:7], PB, -2.0, 1.0, ALU.mult, ALU.add)
            v.drain()
            v.tensor_tensor(SG[:, 8:14], SG[:, 0:6], SG[:, 1:7], ALU.mult)
            v.tensor_scalar(SG[:, 7:8], SG[:, 0:1], -1.0, None, ALU.mult)
            cur, oth = KA, KB
            v4 = cur.rearrange("p (g q) -> p g q", q=4)[:, :, 2:4]
            v.drain()
            v.tensor_scalar(v4, v4, -1.0, None, ALU.mult)

            def exchange(cur, oth, d):
                x = cur.rearrange("p (g t d) -> p g t d", t=2, d=d)
                y = oth.rearrange("p (g t d) -> p g t d", t=2, d=d)
                v.drain()
                v.tensor_tensor(y[:, :, 0, :], x[:, :, 0, :], x[:, :, 1, :], ALU.min)
                v.tensor_tensor(y[:, :, 1, :], x[:, :, 0, :], x[:, :, 1, :], ALU.max)
                return oth, cur

            turns = 0
            for k in range(1, 16):
                if k >= 9:
                    v.drain().then_inc(signal("turn_in"), 1)
                    turns += 1
                    v.wait_ge(signal("turned"), 2 * turns - 1)
                    v.tensor_copy(cur, bank[0][:, :])
                    for st in range(k - 9, -1, -1):
                        cur, oth = exchange(cur, oth, 1 << st)
                    mid_side.append(0 if cur is KA else 1)
                    v.drain().then_inc(signal("turn_in"), 1)
                    v.wait_ge(signal("turned"), 2 * turns)
                    v.tensor_copy(cur, bank[1][:, :])
                for st in range(min(k, 8) - 1, -1, -1):
                    cur, oth = exchange(cur, oth, 1 << st)
                end_side.append(0 if cur is KA else 1)
                v.drain()
                if k <= 6:
                    w = 1 << k
                    m = cur.rearrange("p (g q) -> p g q", q=4 * w)[:, :, w:3 * w]
                    v.tensor_scalar(m, m, -1.0, None, ALU.mult)
                elif k == 7:
                    m = cur.rearrange("p (g q) -> p g q", q=256)
                    v.tensor_scalar(m[:, :, 0:128], m[:, :, 0:128], SG[:, 0:1], None, ALU.mult)
                    v.tensor_scalar(m[:, :, 128:256], m[:, :, 128:256], SG[:, 7:8], None, ALU.mult)
                elif k <= 13:
                    v.tensor_scalar(cur, cur, SG[:, k:k + 1], None, ALU.mult)
                elif k == 14:
                    v.tensor_scalar(cur, cur, SG[:, 6:7], None, ALU.mult)
            if cur is not KA:
                v.tensor_copy(KA, cur)
            v.drain().then_inc(signal("sorted"), 1)

            v.wait_ge(signal("keys_back"), 32)
            v.tensor_scalar(D1, TR, 31, None, ALU.arith_shift_right)
            v.drain()
            v.tensor_scalar(D2, D1, FLIP, None, ALU.bitwise_and)
            v.tensor_copy(D3, D1)
            v.drain()
            v.tensor_tensor(D1, TR, D2, ALU.bitwise_xor)
            v.drain()
            v.tensor_scalar(D2, D1, 32767, None, ALU.bitwise_and)
            v.tensor_scalar(D1, D1, 15, None, ALU.logical_shift_right)
            v.drain()
            v.tensor_scalar(D4, D3, 2.0, 1.0, ALU.mult, ALU.add)
            v.drain()
            v.scalar_tensor_tensor(D4, D1, float(-(OFFSET >> 15)), D4, ALU.add, ALU.mult)
            v.drain()
            ndf = ND.rearrange("r q j -> r (q j)")
            v.scalar_tensor_tensor(ndf, D3, float(HALF), D4, ALU.add, ALU.add)
            v.tensor_scalar(Et[:, :, 0:TE], D2.rearrange("r (q j) -> r q j", j=127)[:, :, 0:TE], float(E - 1), None, ALU.min)
            v.drain()
            v.tensor_copy(NTt[:, :, 0:TE], ND[:, :, 0:TE])
            v.tensor_copy(NTt[:, :, TE:TE + 1], ND[:, :, 0:1])
            v.tensor_copy(NTt[:, :, TE + 1:TE + 2], ND[:, :, TE - 1:TE])
            v.tensor_tensor(NE, ND[:, :, 0:TE], ND[:, :, 1:TE + 1], ALU.not_equal)
            v.tensor_tensor(FUt, ND[:, :, 0], ND[:, :, TE - 1], ALU.is_equal)
            v.drain()
            v.tensor_scalar(NLt, NE[:, :, TE - 1], -1.0, 1.0, ALU.mult, ALU.add)
            v.tensor_scalar(SIt[:, :, 0:TE], NE, -FAR, FAR, ALU.mult, ALU.add)
            v.drain()
            v.tensor_tensor(SIt[:, :, 0:TE], SIt[:, :, 0:TE], ND[:, :, 0:TE], ALU.add)
            v.memset(smr[:, :, 0:1], 1.0)
            v.tensor_scalar(smr[:, :, 1:TE + 1], NE[:, 2:4, :], -1.0, 1.0, ALU.mult, ALU.add)
            v.drain().then_inc(signal("decoded"), 1)
            for ix in (*scat_i, *own_i, *far_i, pos_i):
                v.memset(ix[:, T:], 0)
            v.wait_ge(signal("tiles_turned"), 1)
            for o in range(2):
                v.tensor_copy(node[o][:, :], bank[3 * o][:, 0:T])
                v.tensor_scalar(own_i[o][:, 0:T], bank[3 * o][:, 0:T], float(N - 1), None, ALU.min)
                v.tensor_copy(scat_i[o][:, 0:T], bank[3 * o + 1][:, 0:T])
                v.tensor_copy(perm_i[o][:, 0:T], bank[3 * o + 2][:, 0:T])
            v.drain().then_inc(signal("indices_ready"), 1)
            dense_dve(v, RUN_A)
            L0_dve(v)
            L1_dve(v)

        @block.scalar
        def _(s_):
            s_.wait_ge(signal("scores_t"), 1)
            s_.activation(wT, bank[6][0:F, :], ACT.Copy).then_inc(signal("scores_c"), 1)
            s_.wait_ge(signal("scores_t"), 2)
            s_.activation(A2[0:F, 0:H8], bank[7][0:F, 0:H8], ACT.Copy)
            s_.activation(A2[F:P, H8:], bank[7][F:P, 0:H8], ACT.Copy).then_inc(signal("scores_c"), 1)
            dense_act(s_, RUN_A)
            L0_act(s_)
            L1_act(s_)

        @block.tensor
        def _(pe):
            pe.wait_ge(signal("iotas"), 1)
            pe.wait_ge(signal("weights_in"), 16 * 17)
            for h in range(HEADS):
                ins = pe.transpose(bank[6][0:F, h * P:(h + 1) * P], wp4[:, h, :], ident[:, :])
            ins.then_inc(signal("scores_t"), 1)
            pe.wait_ge(signal("scores_c"), 1)
            for h in range(H8):
                ins = pe.matmul(bank[7][:, h:h + 1], wT[:, (h % HEADS) * P:(h % HEADS + 1) * P], rsT[:, h:h + 1], start=True, stop=True)
            ins.then_inc(signal("scores_t"), 1)
            for turn in range(1, 8):
                src = (KA, KB)[end_side[7 + turn - 1]]
                pe.wait_ge(signal("turn_in"), 2 * turn - 1)
                for q in range(4):
                    ins = pe.transpose(bank[0][:, q * P:(q + 1) * P], src[:, q * P:(q + 1) * P], ident[:, :])
                ins.then_inc(signal("turned"), 1)
                src = (KA, KB)[mid_side[turn - 1]]
                pe.wait_ge(signal("turn_in"), 2 * turn)
                for q in range(4):
                    ins = pe.transpose(bank[1][:, q * P:(q + 1) * P], src[:, q * P:(q + 1) * P], ident[:, :])
                ins.then_inc(signal("turned"), 1)
            pe.wait_ge(signal("decoded"), 1)
            for o in range(2):
                for n_, t_ in enumerate((NTt, SIt, Et)):
                    for h in range(2):
                        ins = pe.transpose(bank[3 * o + n_][:, h * HT:(h + 1) * HT], t_[:, 2 * o + h, :], ident[0:HT, 0:HT])
            ins.then_inc(signal("tiles_turned"), 1)
            L0_pe(pe)
            L1_pe(pe)

        @block.gpsimd
        def _(g):
            top = g.to_reg(N - 1)
            for o in range(2):
                g.iota(EI[:, o * SW:(o + 1) * SW], [[1, SW]], base=0, channel_multiplier=SW)
            g.iota(PI, [[0, 1]], base=0, channel_multiplier=1)
            g.iota(posn, [[P, T]], base=0, channel_multiplier=1)
            g.memset(ident[:, :], 0.0)
            g.drain()
            g.tensor_copy(posv[:, :, 0], posn)
            g.tensor_copy(pnum[:, :], posn[:, 0:1])
            g.affine_select(ident[:, :], ident[:, :], [[-1, P]], ALU.not_equal, 1.0, base=0, channel_multiplier=1)
            g.drain().then_inc(signal("iotas"), 1)

            def narrow(before, idx, slot_v, gather_from=None, into=None, scatter_to=None, source=None, w=1, units=NSM, size=SMALL):
                slot_v, slot_i = slot_v[:, :, 0:size], small_i[:, :, 0:size]
                def take(b, c):
                    if into is not None:
                        sl = slice(c * size, (c + 1) * size) if isinstance(c, int) else ds(c * size, size)
                        g.tensor_copy(into[:, sl], slot_v[:, b] if len(into.shape) == 3 else slot_v[:, b, :, 0])

                def issue(b, c):
                    sl = slice(c * size, (c + 1) * size) if isinstance(c, int) else ds(c * size, size)
                    g.tensor_copy(slot_i[:, b], idx[:, sl])
                    if source is not None:
                        g.tensor_copy(slot_v[:, b], source[:, sl])
                    g.drain()
                    for k in range(size):
                        off = bass.IndirectOffsetOnAxis(ap=slot_i[:, b, k:k + 1], axis=0)
                        if gather_from is not None:
                            g.indirect_dma_start(slot_v[:, b, k], None, gather_from, off, bounds_check=top, oob_is_err=False).then_inc(signal(f"narrow{b}"), 16)
                        else:
                            g.indirect_dma_start(scatter_to, off, slot_v[:, b, k], None, bounds_check=top, oob_is_err=False).then_inc(signal(f"narrow{b}"), 16)

                for b in range(2):
                    issue(b, b)
                with g.Fori(1, units // 2) as j:
                    for b in range(2):
                        g.wait_ge(signal(f"narrow{b}"), j * (16 * size) + 16 * before)
                        g.sem_inc(signal("turn"), 1)
                        take(b, j * 2 + (b - 2))
                        g.drain()
                        issue(b, j * 2 + b)
                for b in range(2):
                    g.wait_ge(signal(f"narrow{b}"), 16 * (size * (units // 2) + before))
                    take(b, units - 2 + b)
                g.drain()

            g.wait_ge(signal("indices_ready"), 1)
            g.wait_ge(signal("tables_out"), 16 * 10)
            narrow(0, perm_i[0], small_v, gather_from=pay_d, into=payg, w=2)
            g.tensor_copy(far_i[0][:, 0:T], payg[:, :, 0]).then_inc(signal("payload_in"), 1)
            gather_pair(g, top, "g", a["x"])
            narrow(T // 2, perm_i[1], small_v1, gather_from=dstf_d, into=far_i[1])
            narrow(2 * T // 2, scat_i[1], small_v1, scatter_to=pos_d, source=posv)
            L0_pool(g, top)
            L1_pool(g, top, narrow)


mid_side, end_side = [], []

_INS = ["x", "src", "dst", "edge_weight", "L0_gnn_w_proj", "L0_gnn_radial_score", "L0_gnn_tangential_score",
        "L0_gnn_radial_distance_scale", "L0_gnn_w_out", "L1_gnn_nb_W", "L1_gnn_nb_b", "L1_gnn_self_W",
        "L1_gnn_self_b", "L1_gnn_att1_W", "L1_gnn_att1_b", "L1_gnn_att2_W", "L1_gnn_att2_b"]


def kernel(**inputs):
    import concourse.bacc as bacc
    from concourse.bass_utils import run_bass_kernel_spmd
    nc = bacc.Bacc("TRN2", target_bir_lowering=False, num_devices=1)
    arrays, a = {}, {}
    for name in _INS:
        value = np.ascontiguousarray(inputs[name])
        if value.ndim == 0:
            value = value.reshape(1)
        arrays["in_" + name] = value
        a[name] = nc.dram_tensor("in_" + name, value.shape, mybir.dt.from_np(value.dtype), kind="ExternalInput").ap()
    out = nc.dram_tensor("out_0", (N, F), F32, kind="ExternalOutput").ap()
    del mid_side[:], end_side[:]
    build(nc, a, out)
    r = run_bass_kernel_spmd(nc, [arrays], core_ids=[0])
    return r.results[0]["out_0"]
```
